# Optimizing a Trainium2 kernel written in Bass

```python
import numpy as np
import jax
import jax.numpy as jnp

def _softmax(x, axis=-1):
    return jax.nn.softmax(x, axis=axis)

def _gelu(x):
    return jax.nn.gelu(x, approximate=True)

def _silu(x):
    return jax.nn.silu(x)

def _sigmoid(x):
    return jax.nn.sigmoid(x)

def _layernorm(x, axis=-1, eps=1e-05):
    m = jnp.mean(x, axis=axis, keepdims=True)
    v = jnp.var(x, axis=axis, keepdims=True)
    return (x - m) / jnp.sqrt(v + eps)

def _scatter_add(tgt, idx, src, axis=0):
    return tgt.at[idx].add(src)

def _segment_sum(src, seg, n):
    return jax.ops.segment_sum(src, seg, n)
kernel_name = 'mk_gnn_resnorm_d4_gnn_r8_685bbf'

def setup_inputs(seed: int=0):
    np.random.seed(seed)
    _w = jnp.asarray

    def _rec_inputs():
        import jax
        import jax.numpy as jnp
        _gk = jax.random.key(seed)
        x = -0.0002117 + 1 * jax.random.normal(jax.random.fold_in(_gk, 1), (1250, 512), jnp.float32)
        src = jax.random.randint(jax.random.fold_in(_gk, 2), (20000,), 0, 1250, jnp.int32)
        dst = jax.random.randint(jax.random.fold_in(_gk, 3), (20000,), 0, 1250, jnp.int32)
        _o = jnp.argsort(dst, stable=True)
        src = src[_o]
        dst = dst[_o]
        edge_attr_128 = -5.16925e-05 + 1.00005 * jax.random.normal(jax.random.fold_in(_gk, 13), (20000, 128), jnp.float32)
        return (x, src, dst, edge_attr_128)
    x, src, dst, edge_attr_128 = _rec_inputs()

    def _L0_gnn_setup():
        import jax, jax.numpy as jnp
        import numpy as np
        NUM_NODES = 6250
        NUM_EDGES = 200000
        IN_C = 512
        OUT_C = 512
        key = jax.random.key(seed)
        k1, k2, k3, k4 = jax.random.split(key, 4)
        x = jax.random.normal(k1, (NUM_NODES, IN_C), dtype=jnp.float32)
        edge_index = jax.random.randint(k2, (2, NUM_EDGES), 0, NUM_NODES, dtype=jnp.int64)
        lim = 1.0 / np.sqrt(IN_C)
        W = jax.random.uniform(k3, (OUT_C, IN_C), dtype=jnp.float32, minval=-lim, maxval=lim)
        b = jax.random.uniform(k4, (OUT_C,), dtype=jnp.float32, minval=-lim, maxval=lim)
        return {'x': x, 'edge_index': edge_index, 'W': W, 'b': b}
    _L0_gnn_all = _L0_gnn_setup()
    _L0_gnn_in = {k: v for k, v in _L0_gnn_all.items() if k in ('W', 'b')}
    del _L0_gnn_all

    def _L1_gnn_setup():
        import jax, jax.numpy as jnp
        import numpy as np
        N_NODES = 4096
        N_EDGES = 32768
        D = 512
        NUM_EXPERTS = 4
        TOP_K = 2
        LAYERS = 2
        key = jax.random.key(seed)
        ks = jax.random.split(key, 8)
        x = jax.random.normal(ks[0], (N_NODES, D), dtype=jnp.float32)
        edge_index = jax.random.randint(ks[1], (2, N_EDGES), 0, N_NODES, dtype=jnp.int64)
        s = 1.0 / np.sqrt(D)
        gate_W = jax.random.uniform(ks[2], (D, NUM_EXPERTS), jnp.float32, -s, s)
        gate_b = jax.random.uniform(ks[3], (NUM_EXPERTS,), jnp.float32, -s, s)
        Wl = jax.random.uniform(ks[4], (NUM_EXPERTS, LAYERS, D, D), jnp.float32, -s, s)
        bl = jax.random.uniform(ks[5], (NUM_EXPERTS, LAYERS, D), jnp.float32, -s, s)
        Wr = jax.random.uniform(ks[6], (NUM_EXPERTS, LAYERS, D, D), jnp.float32, -s, s)
        return {'x': x, 'gate_W': gate_W, 'gate_b': gate_b, 'Wl': Wl, 'bl': bl, 'Wr': Wr, 'edge_index': edge_index}
    _L1_gnn_all = _L1_gnn_setup()
    _L1_gnn_in = {k: v for k, v in _L1_gnn_all.items() if k in ('gate_W', 'gate_b', 'Wl', 'bl', 'Wr')}
    del _L1_gnn_all

    def _L2_gnn_setup():
        import jax, jax.numpy as jnp
        import numpy as np
        N_NODES = 1250
        N_EDGES = 20000
        IN_DIM = 512
        OUT_DIM = 512
        LN_EPS = 1e-05
        key = jax.random.key(seed)
        k_x, k_src, k_ws, k_wn = jax.random.split(key, 4)
        x = jax.random.normal(k_x, (N_NODES, IN_DIM), dtype=jnp.float32)
        edge_src = jax.random.randint(k_src, (N_EDGES,), 0, N_NODES, dtype=jnp.int32)
        edge_dst = jnp.repeat(jnp.arange(N_NODES, dtype=jnp.int32), N_EDGES // N_NODES)
        deg = jnp.full((N_NODES,), float(N_EDGES // N_NODES), dtype=jnp.float32)
        scale = 1.0 / np.sqrt(IN_DIM)
        W_self = jax.random.normal(k_ws, (OUT_DIM, IN_DIM), dtype=jnp.float32) * scale
        W_neigh = jax.random.normal(k_wn, (OUT_DIM, IN_DIM), dtype=jnp.float32) * scale
        bias = jnp.zeros((OUT_DIM,), dtype=jnp.float32)
        gamma = jnp.ones((OUT_DIM,), dtype=jnp.float32)
        beta = jnp.zeros((OUT_DIM,), dtype=jnp.float32)
        return {'x': x, 'edge_src': edge_src, 'edge_dst': edge_dst, 'deg': deg, 'W_self': W_self, 'W_neigh': W_neigh, 'bias': bias, 'gamma': gamma, 'beta': beta}
    _L2_gnn_all = _L2_gnn_setup()
    _L2_gnn_in = {k: v for k, v in _L2_gnn_all.items() if k in ('W_self', 'W_neigh', 'bias', 'gamma', 'beta')}
    del _L2_gnn_all

    def _L3_gnn_setup():
        import jax, jax.numpy as jnp
        import numpy as np
        LN_EPS = 1e-05

        def layer_norm(x, g, b):
            m = jnp.mean(x, axis=-1, keepdims=True)
            v = jnp.mean(jnp.square(x - m), axis=-1, keepdims=True)
            return (x - m) * jax.lax.rsqrt(v + LN_EPS) * g + b
        key = jax.random.key(seed)
        ks = jax.random.split(key, 16)
        N, E, D, ED = (6250, 100000, 512, 128)
        s = lambda k, shape, fan: (jax.random.normal(k, shape, jnp.float32) * (1.0 / np.sqrt(fan))).astype(jnp.float32)
        return {'node_feats': jax.random.normal(ks[0], (N, D), jnp.float32), 'edge_index': jax.random.randint(ks[1], (2, E), 0, N, jnp.int64), 'edge_attr': jax.random.normal(ks[2], (E, ED), jnp.float32), 'W_edge': s(ks[3], (ED, D), ED), 'b_edge': jnp.zeros((D,), jnp.float32), 'eps': jnp.zeros((), jnp.float32), 'W1': s(ks[4], (D, 2 * D), D), 'b1': jnp.zeros((2 * D,), jnp.float32), 'g1': jnp.ones((2 * D,), jnp.float32), 'be1': jnp.zeros((2 * D,), jnp.float32), 'W2': s(ks[5], (2 * D, D), 2 * D), 'b2': jnp.zeros((D,), jnp.float32), 'g2': jnp.ones((D,), jnp.float32), 'be2': jnp.zeros((D,), jnp.float32), 'gA': jnp.ones((D,), jnp.float32), 'bA': jnp.zeros((D,), jnp.float32), 'M1': s(ks[6], (D, 2 * D), D), 'M2': s(ks[7], (2 * D, D), 2 * D), 'gB': jnp.ones((D,), jnp.float32), 'bB': jnp.zeros((D,), jnp.float32)}
    _L3_gnn_all = _L3_gnn_setup()
    _L3_gnn_in = {k: v for k, v in _L3_gnn_all.items() if k in ('W_edge', 'b_edge', 'eps', 'W1', 'b1', 'g1', 'be1', 'W2', 'b2', 'g2', 'be2', 'gA', 'bA', 'M1', 'M2', 'gB', 'bB')}
    del _L3_gnn_all
    return {'x': x, 'src': src, 'dst': dst, 'edge_attr_128': edge_attr_128, 'L0_gnn_W': _L0_gnn_in['W'], 'L0_gnn_b': _L0_gnn_in['b'], 'L1_gnn_gate_W': _L1_gnn_in['gate_W'], 'L1_gnn_gate_b': _L1_gnn_in['gate_b'], 'L1_gnn_Wl': _L1_gnn_in['Wl'], 'L1_gnn_bl': _L1_gnn_in['bl'], 'L1_gnn_Wr': _L1_gnn_in['Wr'], 'L2_gnn_W_self': _L2_gnn_in['W_self'], 'L2_gnn_W_neigh': _L2_gnn_in['W_neigh'], 'L2_gnn_bias': _L2_gnn_in['bias'], 'L2_gnn_gamma': _L2_gnn_in['gamma'], 'L2_gnn_beta': _L2_gnn_in['beta'], 'L3_gnn_W_edge': _L3_gnn_in['W_edge'], 'L3_gnn_b_edge': _L3_gnn_in['b_edge'], 'L3_gnn_eps': _L3_gnn_in['eps'], 'L3_gnn_W1': _L3_gnn_in['W1'], 'L3_gnn_b1': _L3_gnn_in['b1'], 'L3_gnn_g1': _L3_gnn_in['g1'], 'L3_gnn_be1': _L3_gnn_in['be1'], 'L3_gnn_W2': _L3_gnn_in['W2'], 'L3_gnn_b2': _L3_gnn_in['b2'], 'L3_gnn_g2': _L3_gnn_in['g2'], 'L3_gnn_be2': _L3_gnn_in['be2'], 'L3_gnn_gA': _L3_gnn_in['gA'], 'L3_gnn_bA': _L3_gnn_in['bA'], 'L3_gnn_M1': _L3_gnn_in['M1'], 'L3_gnn_M2': _L3_gnn_in['M2'], 'L3_gnn_gB': _L3_gnn_in['gB'], 'L3_gnn_bB': _L3_gnn_in['bB']}

def reference(x, src, dst, edge_attr_128, L0_gnn_W, L0_gnn_b, L1_gnn_gate_W, L1_gnn_gate_b, L1_gnn_Wl, L1_gnn_bl, L1_gnn_Wr, L2_gnn_W_self, L2_gnn_W_neigh, L2_gnn_bias, L2_gnn_gamma, L2_gnn_beta, L3_gnn_W_edge, L3_gnn_b_edge, L3_gnn_eps, L3_gnn_W1, L3_gnn_b1, L3_gnn_g1, L3_gnn_be1, L3_gnn_W2, L3_gnn_b2, L3_gnn_g2, L3_gnn_be2, L3_gnn_gA, L3_gnn_bA, L3_gnn_M1, L3_gnn_M2, L3_gnn_gB, L3_gnn_bB):
    import jax
    import jax.numpy as jnp

    def _L0_gnn_ref(x, edge_index, W, b):
        import jax, jax.numpy as jnp
        import numpy as np
        NUM_NODES = 6250
        NUM_EDGES = 200000
        IN_C = 512
        OUT_C = 512
        num_nodes = x.shape[0]
        src = edge_index[0]
        tar = edge_index[1]
        feat = jnp.einsum('ni,oi->no', x, W) + b
        ones_e = jnp.ones((src.shape[0],), dtype=feat.dtype)
        deg = jax.ops.segment_sum(ones_e, src, num_segments=num_nodes) + 1.0
        deg_inv_sqrt = jnp.where(deg > 0, deg ** (-0.5), 0.0)
        w = deg_inv_sqrt[src] * deg_inv_sqrt[tar]
        msgs = w[:, None] * feat[tar]
        out = jax.ops.segment_sum(msgs, src, num_segments=num_nodes)
        out = out + feat * (1.0 / deg)[:, None]
        return out

    def _L1_gnn_ref(x, gate_W, gate_b, Wl, bl, Wr, edge_index):
        import jax, jax.numpy as jnp
        import numpy as np
        N_NODES = 4096
        N_EDGES = 32768
        D = 512
        NUM_EXPERTS = 4
        TOP_K = 2
        LAYERS = 2
        n = x.shape[0]
        src, dst = (edge_index[0], edge_index[1])
        gates = jax.nn.softmax(x @ gate_W + gate_b, axis=-1)
        top_v, top_i = jax.lax.top_k(gates, TOP_K)
        deg = jax.ops.segment_sum(jnp.ones((src.shape[0],), x.dtype), dst, num_segments=n)
        inv_deg = jnp.where(deg > 0, 1.0 / jnp.maximum(deg, 1.0), 0.0)[:, None]

        def sage_conv(h, W_l, b_l, W_r):
            aggr = jax.ops.segment_sum(h[src], dst, num_segments=n) * inv_deg
            return aggr @ W_l + b_l + h @ W_r
        expert_outs = []
        for e in range(NUM_EXPERTS):
            h = x
            for l in range(LAYERS):
                h = sage_conv(h, Wl[e, l], bl[e, l], Wr[e, l])
                h = jax.nn.relu(h)
            expert_outs.append(h)
        expert_outputs = jnp.stack(expert_outs, axis=1)
        sel = jnp.take_along_axis(expert_outputs, top_i[:, :, None], axis=1)
        out = jnp.sum(sel * top_v[:, :, None], axis=1)
        return out

    def _L2_gnn_ref(x, edge_src, edge_dst, deg, W_self, W_neigh, bias, gamma, beta):
        import jax, jax.numpy as jnp
        import numpy as np
        N_NODES = 1250
        N_EDGES = 20000
        IN_DIM = 512
        OUT_DIM = 512
        LN_EPS = 1e-05
        n = x.shape[0]
        h_self = jnp.einsum('nd,od->no', x, W_self)
        neigh_sum = jax.ops.segment_sum(x[edge_src], edge_dst, num_segments=n)
        neigh_mean = neigh_sum / jnp.maximum(deg, 1.0)[:, None]
        h_neigh = jnp.einsum('nd,od->no', neigh_mean, W_neigh)
        h = h_self + h_neigh + bias
        mu = jnp.mean(h, axis=-1, keepdims=True)
        var = jnp.mean(jnp.square(h - mu), axis=-1, keepdims=True)
        h = (h - mu) * jax.lax.rsqrt(var + LN_EPS)
        return h * gamma + beta

    def _L3_gnn_ref(node_feats, edge_index, edge_attr, W_edge, b_edge, eps, W1, b1, g1, be1, W2, b2, g2, be2, gA, bA, M1, M2, gB, bB):
        import jax, jax.numpy as jnp
        import numpy as np
        LN_EPS = 1e-05

        def layer_norm(x, g, b):
            m = jnp.mean(x, axis=-1, keepdims=True)
            v = jnp.mean(jnp.square(x - m), axis=-1, keepdims=True)
            return (x - m) * jax.lax.rsqrt(v + LN_EPS) * g + b
        N = node_feats.shape[0]
        src, dst = (edge_index[0], edge_index[1])
        edge_emb = edge_attr @ W_edge + b_edge
        msg = jax.nn.relu(node_feats[src] + edge_emb)
        aggr = jax.ops.segment_sum(msg, dst, num_segments=N)
        h = (1.0 + eps) * node_feats + aggr
        h = jax.nn.gelu(layer_norm(h @ W1 + b1, g1, be1), approximate=False)
        h = jax.nn.gelu(layer_norm(h @ W2 + b2, g2, be2), approximate=False)
        h = layer_norm(node_feats + h, gA, bA)
        m = jax.nn.gelu(h @ M1, approximate=False) @ M2
        return layer_norm(h + m, gB, bB)
    edge_index = jnp.stack([src, dst])
    deg = jnp.maximum(jax.ops.segment_sum(jnp.ones(dst.shape, jnp.float32), dst, num_segments=1250), 1.0)
    x = _layernorm(x + _L0_gnn_ref(x, edge_index, L0_gnn_W, L0_gnn_b), axis=-1)
    x = _layernorm(x + _L1_gnn_ref(x, L1_gnn_gate_W, L1_gnn_gate_b, L1_gnn_Wl, L1_gnn_bl, L1_gnn_Wr, edge_index), axis=-1)
    x = _layernorm(x + _L2_gnn_ref(x, src, dst, deg, L2_gnn_W_self, L2_gnn_W_neigh, L2_gnn_bias, L2_gnn_gamma, L2_gnn_beta), axis=-1)
    x = _layernorm(x + _L3_gnn_ref(x, edge_index, edge_attr_128, L3_gnn_W_edge, L3_gnn_b_edge, L3_gnn_eps, L3_gnn_W1, L3_gnn_b1, L3_gnn_g1, L3_gnn_be1, L3_gnn_W2, L3_gnn_b2, L3_gnn_g2, L3_gnn_be2, L3_gnn_gA, L3_gnn_bA, L3_gnn_M1, L3_gnn_M2, L3_gnn_gB, L3_gnn_bB), axis=-1)
    return x

_drawn_inputs = setup_inputs


def setup_inputs(seed=0):
    import zlib

    import numpy as np

    out = dict(_drawn_inputs(seed))
    spreads = {'L2_gnn_bias': (0.0, 0.1),
     'L2_gnn_gamma': (1.0, 0.2),
     'L2_gnn_beta': (0.0, 0.1),
     'L3_gnn_b_edge': (0.0, 0.277),
     'L3_gnn_b1': (0.0, 0.8),
     'L3_gnn_g1': (1.0, 0.2),
     'L3_gnn_be1': (0.0, 0.1),
     'L3_gnn_b2': (0.0, 0.1),
     'L3_gnn_g2': (1.0, 0.2),
     'L3_gnn_be2': (0.0, 0.1),
     'L3_gnn_gA': (1.0, 0.2),
     'L3_gnn_bA': (0.0, 0.1),
     'L3_gnn_gB': (1.0, 0.2),
     'L3_gnn_bB': (0.0, 0.1)}
    factors = {'L1_gnn_gate_b': 4.406, 'L1_gnn_bl': 5.446}
    for name, (base, spread) in spreads.items():
        noise = np.random.default_rng([zlib.crc32(name.encode()), seed]).standard_normal(out[name].shape)
        drawn = base * np.exp(spread * noise) if base else spread * noise
        out[name] = jnp.asarray(drawn.astype(out[name].dtype))
    for name, factor in factors.items():
        out[name] = (out[name] * factor).astype(out[name].dtype)
    return out
```

```python
import numpy as np
import concourse.bass as bass
from concourse import mybir
from contextlib import ExitStack

F32 = mybir.dt.float32
F32R = mybir.dt.float32r
F16 = mybir.dt.float16
BF16 = mybir.dt.bfloat16
I32 = mybir.dt.int32
ALU = mybir.AluOpType
ACT = mybir.ActivationFunctionType
AX = mybir.AxisListType

P = 128
N_NODES = 1250
NT = 10
NP = NT * P
N_EDGES = 20000
ET = 160
EPW = ET // NT
MARGIN = 3
NO_NODE = 4096
D = 512
KT = D // P
NE = 4
EPS = 1e-5


def shifts(j, r):
    own, at = divmod(r, EPW)
    ws = [own]
    if at < MARGIN and not (isinstance(j, int) and 2 * j + own == 0):
        ws.insert(0, own - 1)
    if at >= EPW - MARGIN and not (isinstance(j, int) and 2 * j + own == NT - 1):
        ws.append(own + 1)
    return ws


def opens(j, r, s):
    if isinstance(j, int) and 2 * j + s == 0:
        return r == 0
    return r == EPW * s - MARGIN


def closes(j, r, s):
    if isinstance(j, int) and 2 * j + s == NT - 1:
        return r == 2 * EPW - 1
    return r == EPW * (s + 1) + MARGIN - 1


def need(eng, sem, value, since=0):
    if isinstance(value, int) and value <= 0:
        return
    eng.wait_ge(sem, since + value)


def tile_loop(eng, step):
    for n in (0, 1):
        step(n, n)
    with eng.Fori(1, NT // 2 - 1) as i:
        step(2 * i, 0)
        step(2 * i + 1, 1)
    for n in (NT - 2, NT - 1):
        step(n, n % 2)


def node_loop(eng, step):
    for n in (0, 1):
        step(n, True, False)
    with eng.Fori(2, NT - 1) as n:
        step(n, True, True)
    step(NT - 1, True, True)
    for n in (NT, NT + 1):
        step(n, False, True)


def window_loop(eng, step):
    step(0)
    with eng.Fori(1, NT // 2 - 1) as j:
        step(j)
    step(NT // 2 - 1)


def build(nc, x, src, dst, w0, b0, gate_w, gate_b, w1, b1, w2, l2_bias, l2_gamma, l2_beta,
          edge_attr, w_edge, b_edge, eps, w3, v1, v2, out):
    ctx = ExitStack()
    with ctx:
        base = (nc.sbuf_base + 63) // 64 * 64
        assert nc.sbuf_usable_end - base >= 212800

        def at(offset, name, shape, dt=F32):
            return nc.alloc_sbuf_tensor_at(name, shape, dt, offset=base + offset)

        def sem(name):
            return ctx.enter_context(nc.semaphore(name))

        MAT = KT * D * 4
        NODE = NT * D * 4
        ADJ = NT * NP * 4
        R0, R1 = 0, ADJ
        R2 = R1 + ADJ
        R3 = R2 + 2 * NODE
        R4 = R3 + NODE
        R5 = R4 + 4 * MAT
        ASD = at(R0, "adj_src_dst", [P, NT, NP], F32R)
        ADS = at(R1, "adj_dst_src", [P, NT, NP], F32R)
        G1H = at(R2, "g1_hi", [P, NT, D], F32R)
        G1L = at(R2 + NODE, "g1_lo", [P, NT, D], F32R)
        OHS = at(R2, "onehot_src", [P, 4, NP], BF16)
        OHD = at(R2 + 4 * NP * 2, "onehot_dst", [P, 4, 2, P], BF16)
        X = at(R3, "x_nodes", [P, NT, D])
        W0H = at(R4, "w0_hi", [P, KT, D], F32R)
        W0L = at(R4 + MAT, "w0_lo", [P, KT, D], F32R)
        STG = at(R4 + 2 * MAT, "w_stage", [P, KT, D])
        FB = at(R4 + 3 * MAT, "feat", [P, 2, D])
        TB = at(R4 + 3 * MAT + 4096, "resid", [P, 2, D])
        small = [R5]

        def keep(name, shape, dt=F32):
            nbytes = int(np.prod(shape[1:])) * (2 if dt in (F16, BF16) else 4)
            t = at(small[0], name, shape, dt)
            small[0] += (nbytes + 31) // 32 * 32
            assert small[0] <= 212800, small[0]
            return t


        SRC = keep("src_index", [P, ET], I32)
        DST = keep("dst_f32", [P, ET])
        SRCF = at(R2 + 36864 + 640, "src_f32", [P, ET])
        IOTA = keep("iota_nodes", [P, NP], F16)
        BC0 = at(small[0] - NP * 2, "bias0", [P, D])
        ident = keep("ident", [P, P])
        identr = keep("ident_r", [P, P], F32R)
        ZB = keep("zeros_bf16", [P, P], BF16)
        ones = keep("ones", [P, 2])
        cst = keep("consts", [P, 4])
        dis = keep("deg_inv_sqrt", [P, NT])
        inv = keep("deg_inv", [P, NT])
        degs = keep("deg_src", [P, NT])
        degd = keep("deg_dst", [P, NT])
        bst = keep("bn_stats", [P, 2, 2, 6])
        bmv = keep("bn_mean_var", [P, 2, 2])
        rst = keep("rstd", [P, 2, 2])
        bmv2 = keep("outer_mean_var", [P, 2, 2])
        rst2 = keep("outer_rstd", [P, 2, 2])
        flag = keep("flag", [1, 2], I32)
        GW = keep("gate_w", [P, KT, NE])
        GBI = keep("gate_bias", [P, NE])
        lg = keep("gate_logits", [P, NT, NE])
        ex = keep("gate_exp", [P, NT, NE])
        gv = keep("gate_values", [P, NT, NE])
        gm = keep("gate_max", [P, 2, NT])
        gate = keep("gate_weights", [P, NT, NE])
        IDXB = keep("gather_index", [P, 4], I32)
        ope = keep("one_plus_eps", [P, 2])
        bst1 = keep("bn_stats1", [P, 2, 6])
        bmv1 = keep("bn_mean_var1", [P, 2])
        rst1 = keep("rstd1", [P, 2])
        XSP_AT = small[0]
        XSP = keep("x_split", [P, 2, 2, D], F32R)
        IOTI = at(R2 + 16384, "iota_int", [P, NP], I32)
        BND = at(R2 + 16384, "bounds", [P, 2, NT, EPW], I32)
        BNF = at(R2 + 24576, "bounds_f32", [P, 2, NT * EPW])
        VIO = at(R2 + 28672, "violations", [P, 2, ET])
        VSM = at(R2 + 32768, "violation_sums", [P, 2])
        DSTI = at(R2 + 36864, "dst_int", [P, ET], I32)

        XT = at(R1, "x1_transposed", [P, NT, D])
        AT = at(R1 + NODE, "agg1_transposed", [P, NT, D])
        SPARE = R1 + 2 * NODE
        XA = at(SPARE, "x_agg_split", [P, 2, 2, D], F32R)
        HB = at(SPARE + 8192, "h_nodes", [P, D])
        AGB = at(XSP_AT, "agg_nodes", [P, 2, D])
        WA = at(R4, "w_first", [P, 2, 2, KT, D], F32R)
        WB = at(R2, "w_second", [P, 2, 2, KT, D], F32R)
        ST2 = at(R3, "w_stage2", [P, 2, KT, D])
        RB = at(R3 + 2 * MAT, "r_out", [P, D])
        HT = at(R2 + 4 * MAT, "h_transposed", [P, 2, D], F32R)
        B1A = at(R2 + 4 * MAT + 4096, "bias1_first", [P, D])
        B1B = at(R2 + 4 * MAT + 6144, "bias1_second", [P, D])
        GB = at(XSP_AT, "g_out", [P, 2, D], F32R)
        G2 = at(R1, "g2", [P, 2, NT, D], F32R)
        G1 = at(R2, "g1_again", [P, 2, NT, D], F32R)
        RR = at(SPARE, "r_ring", [P, 5, D])
        ACC = X
        TU = at(XSP_AT, "gated", [P, 2, 2, D])
        WLR = at(R4, "w2_raw", [P, 2, 2, KT, D])
        AG2 = at(XSP_AT, "agg2_nodes", [P, 2, D])
        XA2 = at(SPARE, "x_agg_split2", [P, 2, 2, D], F32R)
        BC2 = at(R2, "bias_gamma_beta2", [P, 3, D])
        Y2 = at(R2 + 6144, "y2", [P, 2, D])
        Z2 = at(R2 + 6144 + 4096, "z2", [P, 2, D])
        X1D = nc.dram_tensor("x1_spill", [P, NT, D], F32)
        GD = nc.dram_tensor("g_spill", [2, P, NE * NT, D], F32)
        RD = nc.dram_tensor("r_spill", [NE * NT, P, D], F32)

        W3H = at(R0, "w3_hi", [P, 8, KT, D], F32R)
        W3L = at(R0 + 8 * MAT, "w3_lo", [P, 8, KT, D], F32R)
        W3R = at(R0 + 8 * MAT, "w3_raw", [P, 8, KT, D])
        FREE = 16 * MAT
        GA = at(FREE, "gathered", [P, 4, D])
        AGGR = at(R4, "edge_sums", [P, NT, D])
        EA = at(R4 + NODE, "edge_attr_raw", [P, 2, D])
        EH = at(R4 + NODE + 4096, "edge_attr_split", [P, 2, 2, D], F32R)
        ZB3 = at(R3, "edge_z", [P, 2, D])
        MSG = at(R3 + 4096, "messages", [P, 2, 2, D], F32R)
        OH3 = at(R3 + 12288, "onehot_dst_r", [P, 4, 2, P], F32R)
        WE = at(R3 + 16384, "w_edge_split", [P, 2, D], F32R)
        WER = at(R3 + 16384, "w_edge_raw", [P, 2, D])
        BE = at(R2 + 14336, "b_edge", [P, D])
        TAB = at(XSP_AT + 4096, "table_rows", [P, 2, D])
        TABD = nc.dram_tensor("x3_table", [NP, D], F32)
        X3D = nc.dram_tensor("x3_spill", [NT, P, D], F32)
        IOT3 = at(R2 + 16384, "iota_int3", [P, NP], I32)
        V1A = at(XSP_AT, "bias1_gamma1", [P, 2, 2 * D])
        V1B = at(FREE, "beta1", [P, 2 * D])
        V2A = at(FREE + 4096, "vectors2_first", [P, 4, D])
        V2B = at(R3 + 8192, "vectors2_last", [P, 3, D])
        Y1 = at(R3, "y1_or_m", [P, 2 * D])
        Y2B = at(R3 + 4096, "y2_or_y", [P, D])
        X3A = at(R3 + 6144, "x3_for_h0", [P, D])
        X3B = at(R3 + 14336, "x3_for_residual", [P, D])
        OUTB = at(R3 + 16384, "out_tile", [P, D])
        S4 = at(R4 + NODE, "split4", [P, 2, D], F32R)
        S8 = at(R4 + NODE + 4096, "split8", [P, 2, 2 * D], F32R)

        big = ctx.enter_context(nc.psum_tensor("banks", [P, 8, 512], F32))
        pb = [big[:, i, :] for i in range(8)]

        T_L1 = NT
        T_L2 = 2 * NT
        T_MLP1 = 3 * NT
        T_MLP2 = 4 * NT
        HT_MLP1 = NE * NT
        HT_MLP2 = (NE + 1) * NT
        F_L1 = NT
        F_EX = 2 * NT
        F_L2 = (2 + NE) * NT
        R_EX = NT
        R_L2 = (1 + NE) * NT
        R_MLP1 = (2 + NE) * NT
        R_MLP2 = (3 + NE) * NT
        A_L1 = NT
        A_EX = 2 * NT
        A_L2 = (2 + NE) * NT
        SC_L2 = NT
        W_L2 = 1
        W_EDGE = 2
        W_MLP = 3
        N_L1 = NT
        N_L2 = 2 * NT
        N_MLP1 = 3 * NT
        N_MLP2 = 4 * NT
        O_MLP1 = NT
        O_MLP2 = 2 * NT
        B_MLP1 = NT
        B_MLP2 = 2 * NT
        GEN_T = ET
        GEN_U = ET - 1
        GEN_W = NT
        GEN_G = ET // 4
        GEN_EA = 16 * (ET // 8)
        GEN_GA = 16 * (ET // 4)

        s_x = sem("x_loaded")
        s_ed = sem("edges_loaded")
        s_w = sem("w_loaded")
        s_b0 = sem("bias0_loaded")
        s_cst = sem("constants")
        s_iota = sem("iota_int_ready")
        s_bnd = sem("bounds_ready")
        s_bndf = sem("bounds_f32_ready")
        s_dve = sem("dve_setup")
        s_viol = sem("violations_ready")
        s_vsum = sem("violations_summed")
        s_flag = sem("flag_ready")
        s_fence = sem("fence")
        s_oh = sem("onehots_ready")
        s_ohu = sem("onehots_used")
        s_win = sem("window_done")
        s_wev = sem("window_copied")
        s_tr = sem("adj_transposed")
        s_tra = sem("adj_copied_act")
        s_trv = sem("adj_copied_dve")
        s_deg = sem("degrees_ready")
        s_degp = sem("deg_src_plus1")
        s_dis = sem("deg_inv_sqrt_ready")
        w_hi = sem("weights_hi")
        w_lo = sem("weights_split")
        s_idr = sem("identity_r_ready")
        rows_t = sem("node_rows_transposed")
        rows_hi = sem("rows_hi")
        rows_lo = sem("rows_split")
        lin1 = sem("first_linear_done")
        s_l0f = sem("l0_feat_ready")
        feat_hi = sem("features_hi")
        feat_lo = sem("features_ready")
        agg = sem("aggregated")
        s_l0r = sem("l0_resid_ready")
        n_stats = sem("norm_stats")
        n_var = sem("norm_var")
        n_eps = sem("norm_var_eps")
        n_rstd = sem("norm_rstd")
        x_ready = sem("layer_output_ready")
        s_be = sem("b_edge_loaded")
        s_we = sem("w_edge_loaded")
        s_io3 = sem("iota3_int")
        s_io3c = sem("iota3_ready")
        s_tab = sem("table_rows_ready")
        s_tst = [sem(f"table_stored_{i}") for i in range(2)]
        s_x3s = sem("x3_stored")
        s_w3a = sem("w3_first_loaded")
        s_w3b = sem("w3_rest_loaded")
        s_ea = [sem(f"edge_attr_loaded_{i}") for i in range(2)]
        s_eh = sem("edge_attr_hi")
        s_el = sem("edge_attr_ready")
        s_ix = sem("gather_index_ready")
        s_ga = [sem(f"gathered_{i}") for i in range(4)]
        s_em = sem("edge_embedded")
        s_z = sem("edge_z_ready")
        s_mh = sem("message_hi")
        s_ml = sem("message_ready")
        s_sc = sem("message_summed")
        s_w3d = sem("edge_window_done")
        s_w3e = sem("edge_window_copied")
        s_eps = sem("eps_loaded")
        s_ope = sem("one_plus_eps_ready")
        s_v1a = sem("vectors1_loaded")
        s_v1b = sem("beta1_loaded")
        s_v2a = sem("vectors2_first_loaded")
        s_v2b = sem("vectors2_last_loaded")
        s_xa = sem("x3_for_h0_loaded")
        s_xb = sem("x3_for_residual_loaded")
        n_h0 = sem("h0_ready")
        n_y1b = sem("y1_biased")
        n_y1s = sem("y1_stats")
        n_y1v = sem("y1_var")
        n_y1e = sem("y1_var_eps")
        n_y1p = sem("y1_rstd")
        n_y1g = sem("y1_gamma")
        n_y1n = sem("y1_normed")
        n_y1 = sem("y1_gelu")
        gamma = sem("times_gamma")
        normed = sem("normed")
        n_y2 = sem("y2_gelu")
        res_add = sem("residual_added")
        n_rg = sem("residual_gamma")
        m_g = sem("m_gelu")
        m_st = sem("out_tile_stored")
        s_spill = sem("x1_spilled")
        s_gw = sem("gate_loaded")
        s_gc = sem("gate_chain")
        s_gex = sem("gate_exp_ready")
        s_1x = sem("l1_xt_ready")
        s_1g = sem("l1_logits_done")
        agg_s = sem("aggregate_scaled")
        s_1b = sem("l1_agg_transposed")
        s_1c = sem("l1_at_ready")
        s_st = sem("expert_weights_loaded")
        s_ba = sem("expert_bias_first_loaded")
        s_bb = sem("expert_bias_second_loaded")
        s_w0h = sem("expert_w_first_hi")
        s_w0 = sem("expert_w_first_ready")
        s_w1h = sem("expert_w_second_hi")
        s_w1 = sem("expert_w_second_ready")
        hid_t = sem("hidden_rows_transposed")
        lin2 = sem("second_linear_done")
        s_h = sem("ex_h_ready")
        hid_hi = sem("hidden_hi")
        hid_lo = sem("hidden_split")
        s_r = sem("ex_r_ready")
        s_sth = sem("g_hi_stored")
        s_stl = sem("g_lo_stored")
        s_str = sem("r_stored")
        s_x1 = sem("x1_reloaded")
        s_gin = [sem(f"g_loaded_{i}") for i in range(2)]
        s_rin = [sem(f"r_loaded_{i}") for i in range(5)]
        s_2t = sem("gather_scaled")
        s_2u = sem("gather_gated")
        s_2c = sem("gather_added")
        s_w2 = sem("w2_loaded")
        s_bc2 = sem("l2_vectors_loaded")
        biased = sem("linear_biased")
        s_3w = sem("l2_dve_steps")
        s_gate = sem("gate_weights_ready")
        o_stats = sem("outer_stats")
        o_var = sem("outer_var")
        o_eps = sem("outer_var_eps")
        o_rstd = sem("outer_rstd")

        block = ctx.enter_context(nc.Block())

        @block.sync
        def _(sp):
            sp.dma_start(DSTI[:], dst).then_inc(s_ed, 16)
            sp.dma_start(SRC[:], src).then_inc(s_ed, 16)
            sp.dma_start(X[:], x).then_inc(s_x, 16)
            sp.dma_start(STG[:], w0).then_inc(s_w, 16)
            sp.wait_ge(s_tr, 1)
            sp.dma_start(BC0[:], b0.partition_broadcast(P)).then_inc(s_b0, 16)
            sp.dma_start(GW[:], gate_w).then_inc(s_gw, 16)
            sp.dma_start(GBI[:], gate_b.partition_broadcast(P)).then_inc(s_gw, 16)
            sp.wait_ge(x_ready, NT)
            sp.dma_start(X1D[:, :, :], X[:]).then_inc(s_spill, 16)
            for e in range(NE):
                if e == 0:
                    sp.wait_ge(s_spill, 16)
                    sp.wait_ge(feat_lo, F_L1 + NT)
                    sp.wait_ge(rows_t, T_L1 + NT)
                else:
                    sp.wait_ge(s_w1, e)
                sp.dma_start(ST2[:], w1[e, 0]).then_inc(s_st, 16)
                if e == 0:
                    sp.wait_ge(agg, A_L1 + NT)
                need(sp, s_h, NT * e)
                sp.dma_start(B1A[:], b1[e, 0].partition_broadcast(P)).then_inc(s_ba, 16)
                sp.wait_ge(s_w0, e + 1)
                sp.dma_start(ST2[:], w1[e, 1]).then_inc(s_st, 16)
                need(sp, s_r, NT * e)
                sp.dma_start(B1B[:], b1[e, 1].partition_broadcast(P)).then_inc(s_bb, 16)
            sp.wait_ge(s_w1, NE)
            sp.wait_ge(s_str, 16 * NE * NT)
            sp.dma_start(ACC[:], X1D[:, :, :]).then_inc(s_x1, 16)
            sp.wait_ge(rows_lo, R_EX + NE * NT)

            def load_g(e):
                sp.wait_ge(s_sth, 16 * NT * (e + 1))
                sp.wait_ge(s_stl, 16 * NT * (e + 1))
                for half in (0, 1):
                    sp.dma_start((G2, G1)[e % 2][:, half].bitcast(F32), GD[half, :, e * NT:(e + 1) * NT, :]).then_inc(s_gin[e % 2], 16)

            def load_r(m, slot):
                need(sp, s_2t, m - 4)
                sp.dma_start(RR[:, slot], RD[bass.ds(m, 1)].rearrange("a p f -> (a p) f")).then_inc(s_rin[slot], 16)

            load_g(0)
            sp.wait_ge(lin1, R_EX + NE * NT)
            for m in range(5):
                load_r(m, m)
            sp.dma_start(WLR[:, :, 1], w2).then_inc(s_w2, 16)
            sp.wait_ge(lin2, NE * NT)
            sp.wait_ge(hid_lo, NE * NT)
            sp.wait_ge(s_r, NE * NT)
            load_g(1)
            for e in range(NE):
                for n in range(5 if e == 0 else 0, NT):
                    load_r(e * NT + n, n % 5)
                    if n == 5 and e in (1, 2):
                        sp.wait_ge(agg, A_EX + NT * e)
                        load_g(e + 1)
            sp.wait_ge(agg, A_EX + NE * NT)
            for i, row in enumerate((l2_bias, l2_gamma, l2_beta)):
                sp.dma_start(BC2[:, i], row.partition_broadcast(P)).then_inc(s_bc2, 16)

            sp.dma_start(BE[:], b_edge.partition_broadcast(P)).then_inc(s_be, 16)
            sp.dma_start(ope[:, 0:1], eps.partition_broadcast(P)).then_inc(s_eps, 16)
            sp.wait_ge(agg, A_L2 + NT)
            sp.dma_start(W3R[:, 0:3], w3[:, 0:3]).then_inc(s_w3a, 16)
            for n in range(NT):
                sp.wait_ge(x_ready, N_L2 + n + 1)
                sp.dma_start(X3D[n], X[:, n, :]).then_inc(s_x3s, 16)
                sp.wait_ge(s_tab, n + 1)
                sp.dma_start(TABD[n * P:(n + 1) * P, :], TAB[:, n % 2]).then_inc(s_tst[n % 2], 16)
            sp.wait_ge(s_x3s, 16 * NT)
            sp.dma_start(WER[:, 1], w_edge).then_inc(s_we, 16)
            for g in range(2):
                sp.dma_start(EA[:, g], edge_attr[g]).then_inc(s_ea[g], 16)
            sp.wait_ge(s_io3c, 1)
            sp.dma_start(W3R[:, 3:8], w3[:, 3:8]).then_inc(s_w3b, 16)
            sp.wait_ge(s_tst[0], 16 * (NT // 2))
            sp.wait_ge(s_tst[1], 16 * (NT // 2))
            for i in (0, 1):
                sp.dma_start(V1A[:, i], v1[i].partition_broadcast(P)).then_inc(s_v1a, 16)
            with sp.Fori(1, ET // 8) as i:
                for b in (0, 1):
                    sp.wait_ge(s_el, 2 * i + b - 1)
                    sp.dma_start(EA[:, b], edge_attr[bass.ds(2 * i + b, 1)].rearrange("a p f -> (a p) f")).then_inc(s_ea[b], 16)
            sp.wait_ge(s_w3e, NT)
            general = sp.value_load(flag[0:1, 0:1], min_val=0, max_val=ET * P)
            with sp.If(general > ET * P - N_EDGES):
                with sp.Fori(0, NT) as d:
                    with sp.Fori(0, ET // 4) as g:
                        for i in range(4):
                            sp.wait_ge(s_sc, GEN_U + (d * (ET // 4) + g) * 4 + i + 1)
                            sp.dma_start(EA[:, 0, 0:P], edge_attr[bass.ds(g, 1), :, i * P:(i + 1) * P].rearrange(
                                "a p f -> (a p) f")).then_inc(s_ea[0], 16)
                sp.wait_ge(s_w3e, GEN_W + NT + 1)
                sp.nop()
            with sp.Else():
                sp.nop()
            sp.nop()
            sp.dma_start(V1B[:], v1[2].partition_broadcast(P)).then_inc(s_v1b, 16)
            for i in range(4):
                sp.dma_start(V2A[:, i], v2[i].partition_broadcast(P)).then_inc(s_v2a, 16)
            for i in range(3):
                sp.dma_start(V2B[:, i], v2[4 + i].partition_broadcast(P)).then_inc(s_v2b, 16)
            for n in range(NT):
                need(sp, n_h0, n)
                sp.dma_start(X3A[:], X3D[n]).then_inc(s_xa, 16)
                if n >= 4:
                    sp.wait_ge(res_add, n - 4)
                    sp.dma_start(X3B[:], X3D[n - 4]).then_inc(s_xb, 16)
            for n in range(NT - 4, NT):
                sp.wait_ge(res_add, n)
                sp.dma_start(X3B[:], X3D[n]).then_inc(s_xb, 16)
            for n in range(NT):
                sp.wait_ge(res_add, NT)
                need(sp, res_add, n, B_MLP1)
                sp.dma_start(X3B[:], X3D[n]).then_inc(s_xb, 16)
                if n >= 1:
                    sp.wait_ge(x_ready, N_MLP2 + n)
                    sp.dma_start(out[:, n - 1, :], OUTB[:]).then_inc(m_st, 16)
            sp.wait_ge(x_ready, N_MLP2 + NT)
            sp.dma_start(out[:, NT - 1, :], OUTB[:]).then_inc(m_st, 16)
            sp.wait_ge(m_st, 16 * NT)

        @block.gpsimd
        def _(g):
            g.iota(IOTI[:], pattern=[[1, NP]], base=0, channel_multiplier=0).then_inc(s_iota, 1)
            g.memset(ident[:], 0.0).then_inc(s_cst, 1)
            g.memset(ones[:], 1.0).then_inc(s_cst, 1)
            g.memset(ZB[:], 0.0).then_inc(s_cst, 1)
            g.memset(cst[:, 0:1], EPS).then_inc(s_cst, 1)
            g.memset(cst[:, 1:2], -0.5).then_inc(s_cst, 1)
            g.memset(cst[:, 2:4], 1.0).then_inc(s_cst, 1)
            g.wait_ge(s_cst, 6)
            g.affine_select(out=ident[:], in_=ident[:], compare_op=ALU.not_equal, fill=1.0, base=0,
                            pattern=[[-1, P]], channel_multiplier=1).then_inc(s_cst, 1)
            g.wait_ge(s_dve, 1)
            L, H = BND[:, 0], BND[:, 1]
            g.iota(L[:, :, 0:MARGIN], pattern=[[P, NT], [0, MARGIN]], base=-P, channel_multiplier=0).then_inc(s_bnd, 1)
            g.iota(L[:, :, MARGIN:], pattern=[[P, NT], [0, EPW - MARGIN]], base=0, channel_multiplier=0).then_inc(s_bnd, 1)
            g.iota(H[:, :, 0:EPW - MARGIN], pattern=[[P, NT], [0, EPW - MARGIN]], base=P, channel_multiplier=0).then_inc(s_bnd, 1)
            g.iota(H[:, :, EPW - MARGIN:], pattern=[[P, NT], [0, MARGIN]], base=2 * P, channel_multiplier=0).then_inc(s_bnd, 1)
            g.wait_ge(s_degp, 1)
            g.tensor_tensor(dis[:], degs[:], cst[:, 1:2].to_broadcast([P, NT]), ALU.pow).then_inc(s_dis, 1)

            def rstd(n, b, since=0):
                need(g, n_var, n + 1, since)
                g.tensor_tensor(rst[:, b, 0:1], bmv[:, b, 1:2], cst[:, 0:1], ALU.add).then_inc(n_eps, 1)
                need(g, n_eps, n + 1, since)
                g.tensor_tensor(rst[:, b, 1:2], rst[:, b, 0:1], cst[:, 1:2], ALU.pow).then_inc(n_rstd, 1)

            def rstd_outer(n, b, since=0):
                need(g, o_var, n + 1, since)
                g.tensor_tensor(rst2[:, b, 0:1], bmv2[:, b, 1:2], cst[:, 0:1], ALU.add).then_inc(o_eps, 1)
                need(g, o_eps, n + 1, since)
                g.tensor_tensor(rst2[:, b, 1:2], rst2[:, b, 0:1], cst[:, 1:2], ALU.pow).then_inc(o_rstd, 1)
            tile_loop(g, rstd)

            with g.Fori(0, NE * NT) as m:
                g.wait_ge(feat_hi, F_EX + m + 1)
                g.dma_start(GD[0, :, bass.ds(m, 1), :].rearrange("p a f -> p (a f)"), GB[:, 0].bitcast(F32)).then_inc(s_sth, 16)
                g.wait_ge(feat_lo, F_EX + m + 1)
                g.dma_start(GD[1, :, bass.ds(m, 1), :].rearrange("p a f -> p (a f)"), GB[:, 1].bitcast(F32)).then_inc(s_stl, 16)
                g.wait_ge(s_r, m + 1)
                g.dma_start(RD[bass.ds(m, 1)].rearrange("a p f -> (a p) f"), RB[:]).then_inc(s_str, 16)

            tile_loop(g, lambda n, b: rstd(n, b, N_L1))

            def both(n, b):
                rstd(n, b, N_L2)
                if not (isinstance(n, int) and n == 0):
                    rstd_outer(n - 1, 1 - b)
            tile_loop(g, both)
            rstd_outer(NT - 1, 1)

            g.wait_ge(s_be, 16)
            for n in range(NT):
                g.wait_ge(x_ready, N_L2 + n + 1)
                if n >= 2:
                    g.wait_ge(s_tst[n % 2], 16 * (n // 2))
                g.tensor_tensor(TAB[:, n % 2], X[:, n, :], BE[:], ALU.add).then_inc(s_tab, 1)
            g.iota(IOT3[:], pattern=[[1, NP]], base=0, channel_multiplier=0).then_inc(s_io3, 1)
            g.wait_ge(s_tst[0], 16 * (NT // 2))
            g.wait_ge(s_tst[1], 16 * (NT // 2))

            def gathers(j):
                for r in range(2 * EPW):
                    t = 2 * EPW * j + r
                    need(g, s_z, t - 3)
                    g.sem_inc(s_fence, 1)
                    g.tensor_copy(IDXB[:, r % 4:r % 4 + 1], SRC[:, bass.ds(t, 1)]).then_inc(s_ix, 1)
                    need(g, s_ix, t + 1)
                    g.sem_inc(s_fence, 1)
                    g.indirect_dma_start(GA[:, r % 4], None, TABD[:, :],
                                         bass.IndirectOffsetOnAxis(ap=IDXB[:, r % 4:r % 4 + 1], axis=0)).then_inc(
                                             s_ga[r % 4], 16)
            window_loop(g, gathers)
            g.wait_ge(s_w3e, NT)
            general = g.value_load(flag[0:1, 0:1], min_val=0, max_val=ET * P)
            with g.If(general > ET * P - N_EDGES):
                with g.Fori(0, NT) as d:
                    with g.Fori(0, ET) as t:
                        g.wait_ge(s_sc, GEN_U + d * ET + t + 1)
                        g.sem_inc(s_fence, 1)
                        g.tensor_copy(IDXB[:, 0:1], SRC[:, bass.ds(t, 1)]).then_inc(s_ix, 1)
                        g.wait_ge(s_ix, GEN_T + d * ET + t + 1)
                        g.sem_inc(s_fence, 1)
                        g.indirect_dma_start(GA[:, 0], None, TABD[:, :],
                                             bass.IndirectOffsetOnAxis(ap=IDXB[:, 0:1], axis=0)).then_inc(s_ga[0], 16)
                g.nop()
            with g.Else():
                g.nop()
            g.nop()

            def rstd1(n):
                need(g, n_y1v, n + 1)
                g.tensor_tensor(rst1[:, 0:1], bmv1[:, 1:2], cst[:, 0:1], ALU.add).then_inc(n_y1e, 1)
                need(g, n_y1e, n + 1)
                g.tensor_tensor(rst1[:, 1:2], rst1[:, 0:1], cst[:, 1:2], ALU.pow).then_inc(n_y1p, 1)

            def first_half(n, up, down):
                if down:
                    rstd(n - 2, 0, N_MLP1)
                if up:
                    rstd1(n)
                if down:
                    rstd_outer(n - 2, 0, O_MLP1)
            node_loop(g, first_half)
            with g.Fori(0, NT) as n:
                rstd(n, 0, N_MLP2)
                rstd_outer(n, 0, O_MLP2)

        @block.scalar
        def _(a):
            a.wait_ge(s_w, 16)
            nc.scalar.copy(W0H[:], STG[:]).then_inc(w_hi, 1)

            def windows(j):
                for b in (0, 1):
                    d = 2 * j + b
                    need(a, s_win, d + 1)
                    for c, w in ((0, 512), (1, 512), (2, 256)):
                        last = nc.scalar.copy(ADS[:, bass.ds(d, 1), 512 * c:512 * c + w].rearrange("p a f -> p (a f)"),
                                              pb[3 * b + c][:, 0:w])
                    last.then_inc(s_wev, 1)
            window_loop(a, windows)
            a.wait_ge(s_flag, 1)
            general = a.value_load(flag[0:1, 0:1], min_val=0, max_val=ET * P)
            with a.If(general > ET * P - N_EDGES):
                a.sem_inc(s_wev, 1)
                with a.Fori(0, NT) as d:
                    a.wait_ge(s_win, GEN_W + d + 1)
                    for c, w in ((0, 512), (1, 512), (2, 256)):
                        last = nc.scalar.copy(ADS[:, bass.ds(d, 1), 512 * c:512 * c + w].rearrange("p a f -> p (a f)"),
                                              pb[c][:, 0:w])
                    last.then_inc(s_wev, 1)
                a.nop()
            with a.Else():
                a.nop()
            a.nop()

            def transposed(n, b):
                need(a, s_tr, 3 * n + 1)
                nc.scalar.copy(ASD[:, 0:4, bass.ds(n * P, P)],
                               pb[3 * b].rearrange("p (k c) -> p k c", k=4)).then_inc(s_tra, 1)
            tile_loop(a, transposed)

            def l0(n, b):
                need(a, rows_t, n + 1)
                need(a, lin1, n - 1)
                nc.scalar.copy(XSP[:, b, 0, :], pb[b]).then_inc(rows_hi, 1)
                if not (isinstance(n, int) and n == 0):
                    hi_of_feat(n - 1, 1 - b)

            def hi_of_feat(n, b):
                need(a, s_l0f, n + 1)
                nc.scalar.copy(G1H[:, bass.ds(n, 1), :].rearrange("p a f -> p (a f)"), FB[:, b, :]).then_inc(feat_hi, 1)
            tile_loop(a, l0)
            hi_of_feat(NT - 1, 1)

            a.wait_ge(agg, NT)
            def l1_x(n, b):
                need(a, x_ready, n + 1)
                nc.scalar.copy(G1H[:, bass.ds(n, 1), :].rearrange("p a f -> p (a f)"),
                               X[:, bass.ds(n, 1), :].rearrange("p a f -> p (a f)")).then_inc(feat_hi, 1)
                need(a, rows_t, n + 1, T_L1)
                nc.scalar.copy(XT[:, bass.ds(n, 1), :].rearrange("p a f -> p (a f)"), pb[b]).then_inc(s_1x, 1)
            tile_loop(a, l1_x)
            a.wait_ge(s_gc, 3)
            nc.scalar.activation(ex[:], lg[:], ACT.Exp).then_inc(s_gex, 1)

            def l1_scaled(n, b):
                need(a, agg, n + 1, A_L1)
                need(a, s_1b, n - 1)
                nc.scalar.activation(AGB[:, b], pb[2 + b], ACT.Copy, scale=inv[:, bass.ds(n, 1)]).then_inc(agg_s, 1)
            tile_loop(a, l1_scaled)

            def first_weights_hi(e):
                a.wait_ge(s_st, 32 * e + 16)
                a.wait_ge(lin1, R_EX + NT * e) if not isinstance(e, int) else need(a, lin1, NT * e, R_EX)
                nc.scalar.copy(WA[:, :, 0], ST2[:]).then_inc(s_w0h, 1)

            def second_weights_hi(e):
                a.wait_ge(s_st, 32 * e + 32)
                need(a, lin2, NT * e)
                nc.scalar.copy(WB[:, :, 0], ST2[:]).then_inc(s_w1h, 1)

            def xa_hi(m, n):
                need(a, lin1, m, R_EX)
                nc.scalar.copy(XA[:, 0, 0], XT[:, bass.ds(n, 1), :].rearrange("p a f -> p (a f)"))
                nc.scalar.copy(XA[:, 1, 0], AT[:, bass.ds(n, 1), :].rearrange("p a f -> p (a f)")).then_inc(rows_hi, 1)

            def hT_hi(m):
                need(a, hid_t, m + 1)
                nc.scalar.activation(HT[:, 0], pb[2], ACT.Relu).then_inc(hid_hi, 1)

            def g_hi(m):
                need(a, lin2, m + 1)
                need(a, s_sth, 16 * m)
                nc.scalar.copy(GB[:, 0], pb[4]).then_inc(feat_hi, 1)

            def expert(e, final):
                with a.Fori(1, NT - 1) as n:
                    m = e * NT + n
                    hT_hi(m - 1)
                    xa_hi(m + 1, n + 1)
                    g_hi(m - 1)
                m = e * NT + NT - 1
                hT_hi(m - 1)
                if not final:
                    xa_hi(m + 1, 0)
                    first_weights_hi(e + 1)
                g_hi(m - 1)
                if not final:
                    hT_hi(m)
                    xa_hi(m + 2, 1)
                    g_hi(m)
                    second_weights_hi(e + 1)

            first_weights_hi(0)
            a.wait_ge(s_1c, NT)
            xa_hi(0, 0)
            a.wait_ge(agg, A_L1 + NT)
            second_weights_hi(0)
            xa_hi(1, 1)
            with a.Fori(0, NE - 1) as e:
                expert(e, False)
            expert(NE - 1, True)
            hT_hi(NE * NT - 1)
            g_hi(NE * NT - 1)

            def gated(m, e, n, b):
                need(a, s_2t, m + 1)
                need(a, s_2c, m - 1)
                nc.scalar.activation(TU[:, 1, b], TU[:, 0, b], ACT.Relu, scale=gate[:, bass.ds(n, 1), e:e + 1].rearrange(
                    "p a f -> p (a f)")).then_inc(s_2u, 1)

            for e in range(NE):
                if e == 1:
                    a.wait_ge(s_w2, 16)
                    nc.scalar.copy(WA[:, :, 0], WLR[:, :, 1]).then_inc(w_hi, 1)

                def step(n, b):
                    gated(e * NT + n, e, n, b)
                    if e == NE - 1 and not (isinstance(n, int) and n < 2):
                        x2_hi(n - 2)

                def x2_hi(n):
                    if isinstance(n, int) and n == 0:
                        a.wait_ge(agg, A_EX + (NE - 1) * NT)
                    need(a, x_ready, n + 1, N_L1)
                    nc.scalar.copy(G2[:, 0, bass.ds(n, 1)].rearrange("p a f -> p (a f)"),
                                   X[:, bass.ds(n, 1), :].rearrange("p a f -> p (a f)")).then_inc(feat_hi, 1)
                tile_loop(a, step)
            x2_hi(NT - 2)
            x2_hi(NT - 1)

            def l2(n, b):
                need(a, agg, n + 1, A_L2)
                need(a, rows_t, n - 1, T_L2)
                nc.scalar.activation(AG2[:, b], pb[2 + b], ACT.Copy, scale=inv[:, bass.ds(n, 1)]).then_inc(agg_s, 1)
                need(a, rows_t, n + 1, T_L2)
                nc.scalar.copy(XA2[:, 0, 0], pb[0])
                nc.scalar.copy(XA2[:, 1, 0], pb[1]).then_inc(rows_hi, 1)
            tile_loop(a, l2)

            a.wait_ge(s_we, 16)
            nc.scalar.copy(WE[:, 0], WER[:, 1]).then_inc(w_hi, 1)

            def attr_hi(i, b):
                a.wait_ge(s_ea[b], 16 * i + 16)
                need(a, s_em, 4 * (2 * i + b - 1))
                nc.scalar.copy(EH[:, b, 0], EA[:, b]).then_inc(s_eh, 1)

            def w3_hi(q):
                if isinstance(q, int):
                    a.wait_ge(s_w3a, 16)
                else:
                    a.wait_ge(s_w3b, 16)
                nc.scalar.copy(W3H[:, bass.ds(q, 1)].rearrange("p a k f -> p (a k f)"),
                               W3R[:, bass.ds(q, 1)].rearrange("p a k f -> p (a k f)")).then_inc(w_hi, 1)

            def edges_hi(j):
                for r in range(2 * EPW):
                    t = 2 * EPW * j + r
                    if r % 4 == 1 and not (isinstance(j, int) and j == 4 and r > 28):
                        attr_hi(4 * j + (r // 4 + 1) // 2, (r // 4 + 1) % 2)
                    need(a, s_z, t + 1)
                    need(a, s_sc, t - 1)
                    nc.scalar.activation(MSG[:, r % 2, 0], ZB3[:, r % 2], ACT.Relu).then_inc(s_mh, 1)
                    if r % EPW == 8 and not (isinstance(j, int) and j == 4):
                        w3_hi(2 * j + r // EPW)
                    if r % EPW == MARGIN + 1 and not (isinstance(j, int) and j == 0 and r < EPW):
                        window_copy(2 * j + r // EPW - 1, (r // EPW + 1) % 2)

            def window_copy(d, b):
                need(a, s_w3d, d + 1)
                nc.scalar.copy(AGGR[:, bass.ds(d, 1)].rearrange("p a f -> p (a f)"), pb[4 + b]).then_inc(s_w3e, 1)
            a.wait_ge(s_tab, NT)
            a.wait_ge(lin1, R_L2 + NT)
            attr_hi(0, 0)
            window_loop(a, edges_hi)
            window_copy(NT - 1, 1)
            general = a.value_load(flag[0:1, 0:1], min_val=0, max_val=ET * P)
            with a.If(general > ET * P - N_EDGES):
                a.sem_inc(s_w3e, 1)
                with a.Fori(0, NT) as d:
                    with a.Fori(0, ET) as t:
                        a.wait_ge(s_ea[0], GEN_EA + (d * ET + t) * 16 + 16)
                        nc.scalar.copy(EH[:, 0, 0, 0:P], EA[:, 0, 0:P]).then_inc(s_eh, 1)
                        a.wait_ge(s_z, GEN_T + d * ET + t + 1)
                        nc.scalar.activation(MSG[:, 0, 0], ZB3[:, 0], ACT.Relu).then_inc(s_mh, 1)
                    a.wait_ge(s_w3d, GEN_W + d + 1)
                    nc.scalar.copy(AGGR[:, bass.ds(d, 1)].rearrange("p a f -> p (a f)"), pb[4]).then_inc(s_w3e, 1)
                a.nop()
            with a.Else():
                a.nop()
            a.nop()

            def s4_hi(n):
                need(a, rows_t, n + 1, T_MLP1)
                nc.scalar.copy(S4[:, 0], pb[0]).then_inc(rows_hi, 1)

            def first_half(n, up, down):
                if not (isinstance(n, int) and n in (0, NT + 1)):
                    need(a, hid_t, n, HT_MLP1)
                    nc.scalar.copy(S8[:, 0], big[:, 1:3].rearrange("p a f -> p (a f)")).then_inc(hid_hi, 1)
                if down:
                    need(a, normed, n - 1)
                    nc.scalar.activation(Y2B[:], Y2B[:], ACT.Gelu).then_inc(n_y2, 1)
                if up:
                    need(a, n_y1n, n + 1)
                    nc.scalar.activation(Y1[:], Y1[:], ACT.Gelu).then_inc(n_y1, 1)
                if up and not (isinstance(n, int) and n == NT - 1):
                    s4_hi(n + 1)
            s4_hi(0)
            node_loop(a, first_half)

            def m4_hi(n):
                need(a, rows_t, n + 1, T_MLP2)
                nc.scalar.copy(S4[:, 0], pb[0]).then_inc(rows_hi, 1)

            def second_half(n, more):
                need(a, lin1, n + 1, R_MLP2)
                nc.scalar.activation(Y1[:], big[:, 3:5].rearrange("p a f -> p (a f)"), ACT.Gelu).then_inc(m_g, 1)
                if more:
                    m4_hi(n + 1)
                need(a, hid_t, n + 1, HT_MLP2)
                nc.scalar.copy(S8[:, 0], big[:, 1:3].rearrange("p a f -> p (a f)")).then_inc(hid_hi, 1)
            m4_hi(0)
            with a.Fori(0, NT - 1) as n:
                second_half(n, True)
            second_half(NT - 1, False)

        @block.vector
        def _(v):
            v.wait_ge(s_iota, 1)
            nc.vector.tensor_copy(IOTA[:], IOTI[:]).then_inc(s_dve, 1)
            v.wait_ge(s_ed, 32)
            nc.vector.tensor_copy(DST[:], DSTI[:]).then_inc(s_dve, 1)
            nc.vector.tensor_copy(SRCF[:], SRC[:]).then_inc(s_dve, 1)
            v.wait_ge(s_bnd, 4)
            nc.vector.tensor_copy(BNF[:], BND[:].rearrange("p a d t -> p a (d t)")).then_inc(s_bndf, 1)
            v.wait_ge(s_bndf, 1)
            v.wait_ge(s_dve, 3)
            nc.vector.tensor_tensor(VIO[:, 0, :], DST[:], BNF[:, 0, :], ALU.is_lt)
            nc.vector.tensor_tensor(VIO[:, 1, :], DST[:], BNF[:, 1, :], ALU.is_ge).then_inc(s_dve, 1)
            v.wait_ge(s_dve, 4)
            nc.vector.tensor_reduce(VSM[:, 0:1], VIO[:], axis=AX.XY, op=ALU.add).then_inc(s_viol, 1)

            def onehots(j):
                for r in range(2 * EPW):
                    t = 2 * EPW * j + r
                    need(v, s_ohu, t - 3)
                    nc.vector.tensor_scalar(OHS[:, r % 4, :], IOTA[:], SRCF[:, bass.ds(t, 1)], None, ALU.is_equal)
                    ws = shifts(j, r)
                    for i, s in enumerate(ws):
                        col = bass.ds((2 * j + s) * P, P)
                        last = nc.vector.tensor_scalar(OHD[:, r % 4, i, :], IOTA[:, col], DST[:, bass.ds(t, 1)], None,
                                                       ALU.is_equal)
                    last.then_inc(s_oh, 1)
            window_loop(v, onehots)

            v.wait_ge(s_vsum, 1)
            nc.vector.tensor_copy(flag[0:1, 0:1], pb[7][0:1, 0:1]).then_inc(s_flag, 1)
            v.wait_ge(s_flag, 1)
            general = v.value_load(flag[0:1, 0:1], min_val=0, max_val=ET * P)
            with v.If(general > ET * P - N_EDGES):
                with v.Fori(0, NT) as d:
                    with v.Fori(0, ET) as t:
                        v.wait_ge(s_ohu, GEN_U + d * ET + t + 1)
                        nc.vector.tensor_scalar(OHS[:, 0, :], IOTA[:], SRCF[:, bass.ds(t, 1)], None, ALU.is_equal)
                        nc.vector.tensor_scalar(OHD[:, 0, 0, :], IOTA[:, bass.ds(d * P, P)], DST[:, bass.ds(t, 1)],
                                                None, ALU.is_equal).then_inc(s_oh, 1)
                v.nop()
            with v.Else():
                v.nop()
            v.nop()

            def transposed(n, b):
                need(v, s_tr, 3 * n + 3)
                nc.vector.tensor_copy(ASD[:, 4:8, bass.ds(n * P, P)],
                                      pb[3 * b + 1].rearrange("p (k c) -> p k c", k=4))
                nc.vector.tensor_copy(ASD[:, 8:10, bass.ds(n * P, P)],
                                      pb[3 * b + 2][:, 0:256].rearrange("p (k c) -> p k c", k=2)).then_inc(s_trv, 1)
            tile_loop(v, transposed)
            v.wait_ge(s_tra, NT)
            v.wait_ge(s_trv, NT)
            nc.vector.tensor_reduce(degs[:], ASD[:].bitcast(F32), axis=AX.X, op=ALU.add).then_inc(s_deg, 1)
            v.wait_ge(s_deg, 1)
            nc.vector.tensor_scalar(degs[:], degs[:], 1.0, None, ALU.add).then_inc(s_degp, 1)
            v.wait_ge(s_w, 16)
            v.wait_ge(w_hi, 1)
            nc.vector.tensor_tensor(W0L[:], STG[:], W0H[:].bitcast(F32), ALU.subtract).then_inc(w_lo, 1)
            nc.vector.tensor_reduce(degd[:], ADS[:].bitcast(F32), axis=AX.X, op=ALU.add).then_inc(s_deg, 1)
            v.wait_ge(s_deg, 2)
            nc.vector.tensor_scalar(degd[:], degd[:], 1.0, None, ALU.max).then_inc(s_deg, 1)
            v.wait_ge(s_deg, 3)
            nc.vector.reciprocal(inv[:], degd[:]).then_inc(s_deg, 1)
            v.wait_ge(s_dis, 1)
            v.wait_ge(s_b0, 16)
            v.wait_ge(s_cst, 7)
            nc.vector.tensor_copy(identr[:], ident[:]).then_inc(s_idr, 1)

            def l0(n, b):
                need(v, rows_hi, n + 1)
                nc.vector.tensor_tensor(XSP[:, b, 1, :], pb[b], XSP[:, b, 0, :].bitcast(F32),
                                        ALU.subtract).then_inc(rows_lo, 1)
                if not (isinstance(n, int) and n == 0):
                    feat(n - 1, 1 - b)

            def feat(n, b):
                need(v, lin1, n + 1)
                need(v, feat_lo, n - 1)
                nc.vector.tensor_tensor(TB[:, b, :], pb[2 + b], BC0[:], ALU.add).then_inc(s_l0r, 1)
                need(v, s_l0r, n + 1)
                nc.vector.tensor_scalar(FB[:, b, :], TB[:, b, :], dis[:, bass.ds(n, 1)], None,
                                        ALU.mult).then_inc(s_l0f, 1)
                need(v, feat_hi, n + 1)
                nc.vector.tensor_tensor(G1L[:, bass.ds(n, 1), :].rearrange("p a f -> p (a f)"), FB[:, b, :],
                                        G1H[:, bass.ds(n, 1), :].rearrange("p a f -> p (a f)").bitcast(F32),
                                        ALU.subtract).then_inc(feat_lo, 1)
            tile_loop(v, l0)
            feat(NT - 1, 1)

            def resid(n, b):
                need(v, agg, n + 1)
                xn = X[:, bass.ds(n, 1), :].rearrange("p a f -> p (a f)")
                need(v, x_ready, n - 1)
                nc.vector.scalar_tensor_tensor(TB[:, b, :], pb[4 + b], dis[:, bass.ds(n, 1)], xn,
                                               ALU.mult, ALU.add).then_inc(s_l0r, 1)
                need(v, s_l0r, NT + n + 1)
                nc.vector.bn_stats(bst[:, b, 0, :], TB[:, b, :]).then_inc(n_stats, 1)
                need(v, n_stats, n + 1)
                v.sem_inc(s_fence, 1)
                nc.vector.bn_aggr(bmv[:, b, :], bst[:, b, 0, :]).then_inc(n_var, 1)
                if not (isinstance(n, int) and n == 0):
                    norm(n - 1, 1 - b)

            def norm(n, b):
                xn = X[:, bass.ds(n, 1), :].rearrange("p a f -> p (a f)")
                need(v, n_rstd, n + 1)
                nc.vector.tensor_scalar(xn, TB[:, b, :], bmv[:, b, 0:1], rst[:, b, 1:2], ALU.subtract,
                                        ALU.mult).then_inc(x_ready, 1)
            tile_loop(v, resid)
            norm(NT - 1, 1)

            v.wait_ge(agg, NT)
            v.wait_ge(x_ready, NT)
            def x1_lo(n, b):
                need(v, feat_hi, n + 1, F_L1)
                nc.vector.tensor_tensor(G1L[:, bass.ds(n, 1), :].rearrange("p a f -> p (a f)"),
                                        X[:, bass.ds(n, 1), :].rearrange("p a f -> p (a f)"),
                                        G1H[:, bass.ds(n, 1), :].rearrange("p a f -> p (a f)").bitcast(F32),
                                        ALU.subtract).then_inc(feat_lo, 1)
            tile_loop(v, x1_lo)

            v.wait_ge(s_gw, 32)
            v.wait_ge(s_1g, NT)
            v.wait_ge(s_1x, NT)
            wide = [P, NT, NE]
            nc.vector.tensor_tensor(lg[:], pb[7][:, 0:NT * NE].rearrange("p (n e) -> p n e", e=NE),
                                    GBI[:].unsqueeze(1).to_broadcast(wide), ALU.add).then_inc(s_gc, 1)
            v.wait_ge(s_gc, 1)
            nc.vector.tensor_reduce(gm[:, 0], lg[:], axis=AX.X, op=ALU.max).then_inc(s_gc, 1)
            v.wait_ge(s_gc, 2)
            nc.vector.tensor_tensor(lg[:], lg[:], gm[:, 0].unsqueeze(2).to_broadcast(wide), ALU.subtract).then_inc(s_gc, 1)
            v.wait_ge(s_gex, 1)
            nc.vector.tensor_reduce(gm[:, 0], ex[:], axis=AX.X, op=ALU.add).then_inc(s_gc, 1)
            v.wait_ge(s_gc, 4)
            nc.vector.reciprocal(gm[:, 1], gm[:, 0]).then_inc(s_gc, 1)
            v.wait_ge(s_gc, 5)
            nc.vector.tensor_tensor(gv[:], ex[:], gm[:, 1].unsqueeze(2).to_broadcast(wide), ALU.mult).then_inc(s_gc, 1)
            v.wait_ge(s_gc, 6)
            steps = 6
            nc.vector.memset(lg[:], 0.0).then_inc(s_gc, 1)
            steps += 1
            for e in range(NE):
                for j in range(NE):
                    if j == e:
                        continue
                    v.wait_ge(s_gc, steps)
                    nc.vector.tensor_tensor(ex[:, :, 0:1], gv[:, :, j:j + 1], gv[:, :, e:e + 1],
                                            ALU.is_ge if j < e else ALU.is_gt).then_inc(s_gc, 1)
                    v.wait_ge(s_gc, steps + 1)
                    nc.vector.tensor_tensor(lg[:, :, e:e + 1], lg[:, :, e:e + 1], ex[:, :, 0:1], ALU.add).then_inc(s_gc, 1)
                    steps += 2
            v.wait_ge(s_gc, steps)
            nc.vector.scalar_tensor_tensor(gate[:], lg[:], 1.5, gv[:], ALU.is_lt, ALU.mult).then_inc(s_gate, 1)

            def l1_at(n, b):
                need(v, s_1b, n + 1)
                nc.vector.tensor_copy(AT[:, bass.ds(n, 1), :].rearrange("p a f -> p (a f)"), pb[4 + b]).then_inc(s_1c, 1)
            tile_loop(v, l1_at)

            def first_weights_lo(e):
                v.wait_ge(s_w0h, e + 1)
                nc.vector.tensor_tensor(WA[:, :, 1], ST2[:], WA[:, :, 0].bitcast(F32), ALU.subtract).then_inc(s_w0, 1)

            def second_weights_lo(e):
                v.wait_ge(s_w1h, e + 1)
                nc.vector.tensor_tensor(WB[:, :, 1], ST2[:], WB[:, :, 0].bitcast(F32), ALU.subtract).then_inc(s_w1, 1)

            def xa_lo(m, n):
                need(v, rows_hi, m + 1, R_EX)
                nc.vector.tensor_tensor(XA[:, 0, 1], XT[:, bass.ds(n, 1), :].rearrange("p a f -> p (a f)"),
                                        XA[:, 0, 0].bitcast(F32), ALU.subtract)
                nc.vector.tensor_tensor(XA[:, 1, 1], AT[:, bass.ds(n, 1), :].rearrange("p a f -> p (a f)"),
                                        XA[:, 1, 0].bitcast(F32), ALU.subtract).then_inc(rows_lo, 1)

            def hT_lo(m):
                need(v, hid_hi, m + 1)
                nc.vector.scalar_tensor_tensor(HT[:, 1], pb[2], 0.0, HT[:, 0].bitcast(F32), ALU.max,
                                               ALU.subtract).then_inc(hid_lo, 1)

            def h_biased(m):
                need(v, lin1, m + 1, R_EX)
                need(v, hid_t, m)
                nc.vector.tensor_tensor(HB[:], pb[0], B1A[:], ALU.add).then_inc(s_h, 1)

            def g_lo_and_r(m):
                need(v, feat_hi, m + 1, F_EX)
                need(v, s_stl, 16 * m)
                nc.vector.tensor_tensor(GB[:, 1], pb[4], GB[:, 0].bitcast(F32), ALU.subtract).then_inc(feat_lo, 1)
                need(v, s_str, 16 * m)
                nc.vector.tensor_tensor(RB[:], pb[5], B1B[:], ALU.add).then_inc(s_r, 1)

            def expert(e, final):
                with v.Fori(1, NT - 1) as n:
                    m = e * NT + n
                    hT_lo(m - 1)
                    h_biased(m)
                    xa_lo(m + 1, n + 1)
                    g_lo_and_r(m - 1)
                m = e * NT + NT - 1
                hT_lo(m - 1)
                h_biased(m)
                if not final:
                    xa_lo(m + 1, 0)
                    first_weights_lo(e + 1)
                g_lo_and_r(m - 1)
                if not final:
                    hT_lo(m)
                    v.wait_ge(s_ba, 16 * (e + 2))
                    h_biased(m + 1)
                    xa_lo(m + 2, 1)
                    g_lo_and_r(m)
                    second_weights_lo(e + 1)
                    v.wait_ge(s_bb, 16 * (e + 2))

            first_weights_lo(0)
            xa_lo(0, 0)
            second_weights_lo(0)
            v.wait_ge(s_ba, 16)
            v.wait_ge(s_bb, 16)
            h_biased(0)
            xa_lo(1, 1)
            with v.Fori(0, NE - 1) as e:
                expert(e, False)
            expert(NE - 1, True)
            hT_lo(NE * NT - 1)
            g_lo_and_r(NE * NT - 1)

            v.wait_ge(s_x1, 16)

            def scaled(m, e, n, b):
                need(v, agg, m + 1, A_EX)
                need(v, s_2u, m - 1)
                k = (0 if isinstance(n, int) and n < 5 else 1)
                nc.vector.scalar_tensor_tensor(TU[:, 0, b], pb[b], inv[:, n:n + 1], RR[:, n % 5], ALU.mult,
                                               ALU.add).then_inc(s_2t, 1)

            def added(m, n, b):
                need(v, s_2u, m + 1)
                need(v, s_2c, m)
                nc.vector.tensor_tensor(ACC[:, n, :], ACC[:, n, :], TU[:, 1, b], ALU.add).then_inc(s_2c, 1)

            def x1_stats(n):
                b = n % 2
                v.wait_ge(s_2c, (NE - 1) * NT + n + 1)
                nc.vector.bn_stats(bst[:, b, 0, :], ACC[:, n, :]).then_inc(n_stats, 1)
                v.wait_ge(n_stats, N_L1 + n + 1)
                nc.vector.bn_aggr(bmv[:, b, :], bst[:, b, 0, :]).then_inc(n_var, 1)

            def x2_norm(n):
                b = n % 2
                v.wait_ge(n_rstd, N_L1 + n + 1)
                nc.vector.tensor_scalar(X[:, n, :], ACC[:, n, :], bmv[:, b, 0:1], rst[:, b, 1:2], ALU.subtract,
                                        ALU.mult).then_inc(x_ready, 1)

            def x2_lo(n):
                v.wait_ge(feat_hi, F_L2 + n + 1)
                nc.vector.tensor_tensor(G2[:, 1, n], X[:, n, :], G2[:, 0, n].bitcast(F32), ALU.subtract).then_inc(feat_lo, 1)
            for e in range(NE):
                if e == 1:
                    v.wait_ge(w_hi, W_L2 + 1)
                    nc.vector.tensor_tensor(WA[:, :, 1], WLR[:, :, 1], WA[:, :, 0].bitcast(F32),
                                            ALU.subtract).then_inc(w_lo, 1)
                for n in range(NT):
                    m = e * NT + n
                    v.wait_ge(s_rin[n % 5], 16 * (2 * e + n // 5 + 1))
                    scaled(m, e, n, n % 2)
                    if m > 0:
                        added(m - 1, (n - 1) % NT, (n - 1) % 2)
                    if e == NE - 1 and n >= 1:
                        x1_stats(n - 1)
                    if e == NE - 1 and n >= 2:
                        x2_norm(n - 2)
                    if e == NE - 1 and n >= 3:
                        x2_lo(n - 3)

            added(NE * NT - 1, NT - 1, 1)
            x1_stats(NT - 1)
            x2_norm(NT - 2)
            x2_lo(NT - 3)
            x2_norm(NT - 1)
            x2_lo(NT - 2)
            x2_lo(NT - 1)

            v.wait_ge(s_bc2, 48)

            def l2_split(n, b):
                need(v, rows_hi, n + 1, R_L2)
                nc.vector.tensor_tensor(XA2[:, 0, 1], pb[0], XA2[:, 0, 0].bitcast(F32), ALU.subtract)
                nc.vector.tensor_tensor(XA2[:, 1, 1], pb[1], XA2[:, 1, 0].bitcast(F32), ALU.subtract).then_inc(rows_lo, 1)
                if not (isinstance(n, int) and n == 0):
                    l2_bias_stats(n - 1, 1 - b)
                if not (isinstance(n, int) and n < 2):
                    l2_norm(n - 2, b)
                if not (isinstance(n, int) and n == 0):
                    l2_affine(n - 1, 1 - b)

            def l2_bias_stats(n, b):
                need(v, lin1, n + 1, R_L2)
                nc.vector.tensor_tensor(Y2[:, b], pb[4 + b], BC2[:, 0], ALU.add).then_inc(biased, 1)
                need(v, biased, n + 1)
                nc.vector.bn_stats(bst[:, b, 0, :], Y2[:, b]).then_inc(n_stats, 1)
                need(v, n_stats, n + 1, N_L2)
                v.sem_inc(s_fence, 1)
                nc.vector.bn_aggr(bmv[:, b, :], bst[:, b, 0, :]).then_inc(n_var, 1)

            def l2_affine(n, b):
                xn = X[:, bass.ds(n, 1), :].rearrange("p a f -> p (a f)")
                need(v, n_rstd, n + 1, N_L2)
                nc.vector.tensor_scalar(Z2[:, b], Y2[:, b], bmv[:, b, 0:1], rst[:, b, 1:2], ALU.subtract,
                                        ALU.mult).then_inc(s_3w, 1)
                need(v, s_3w, 4 * n + 1)
                nc.vector.tensor_tensor(Z2[:, b], Z2[:, b], BC2[:, 1], ALU.mult).then_inc(s_3w, 1)
                need(v, s_3w, 4 * n + 2)
                nc.vector.tensor_tensor(Z2[:, b], Z2[:, b], BC2[:, 2], ALU.add).then_inc(s_3w, 1)
                need(v, s_3w, 4 * n + 3)
                nc.vector.tensor_tensor(Z2[:, b], Z2[:, b], xn, ALU.add).then_inc(s_3w, 1)
                need(v, s_3w, 4 * n + 4)
                nc.vector.bn_stats(bst[:, b, 1, :], Z2[:, b]).then_inc(o_stats, 1)
                need(v, o_stats, n + 1)
                v.sem_inc(s_fence, 1)
                nc.vector.bn_aggr(bmv2[:, b, :], bst[:, b, 1, :]).then_inc(o_var, 1)

            def l2_norm(n, b):
                xn = X[:, bass.ds(n, 1), :].rearrange("p a f -> p (a f)")
                need(v, o_rstd, n + 1)
                nc.vector.tensor_scalar(xn, Z2[:, b], bmv2[:, b, 0:1], rst2[:, b, 1:2], ALU.subtract,
                                        ALU.mult).then_inc(x_ready, 1)
            tile_loop(v, l2_split)
            l2_bias_stats(NT - 1, 1)
            l2_norm(NT - 2, 0)
            l2_affine(NT - 1, 1)
            l2_norm(NT - 1, 1)

            v.wait_ge(s_eps, 16)
            nc.vector.tensor_scalar(ope[:, 1:2], ope[:, 0:1], 1.0, None, ALU.add).then_inc(s_ope, 1)
            v.wait_ge(s_io3, 1)
            nc.vector.tensor_copy(IOTA[:], IOT3[:]).then_inc(s_io3c, 1)
            v.wait_ge(s_io3c, 1)
            v.wait_ge(w_hi, W_EDGE + 1)
            nc.vector.tensor_tensor(WE[:, 1], WER[:, 1], WE[:, 0].bitcast(F32), ALU.subtract).then_inc(w_lo, 1)

            def attr_lo(i, b):
                need(v, s_eh, 2 * i + b + 1)
                nc.vector.tensor_tensor(EH[:, b, 1], EA[:, b], EH[:, b, 0].bitcast(F32), ALU.subtract).then_inc(s_el, 1)

            def w3_lo(q):
                need(v, w_hi, q + 1, W_MLP)
                flat = lambda ap: ap.rearrange("p a k f -> p (a k f)")
                nc.vector.tensor_tensor(flat(W3L[:, bass.ds(q, 1)]), flat(W3R[:, bass.ds(q, 1)]),
                                        flat(W3H[:, bass.ds(q, 1)]).bitcast(F32), ALU.subtract).then_inc(w_lo, 1)

            def message_lo(t, b):
                need(v, s_mh, t + 1)
                nc.vector.scalar_tensor_tensor(MSG[:, b, 1], ZB3[:, b], 0.0, MSG[:, b, 0].bitcast(F32), ALU.max,
                                               ALU.subtract).then_inc(s_ml, 1)

            def edges_lo(j):
                for r in range(2 * EPW):
                    t = 2 * EPW * j + r
                    if r % 4 == 1 and not (isinstance(j, int) and j == 4 and r > 28):
                        attr_lo(4 * j + (r // 4 + 1) // 2, (r // 4 + 1) % 2)
                    need(v, s_sc, t - 3)
                    for i, w in enumerate(shifts(j, r)):
                        nc.vector.tensor_scalar(OH3[:, r % 4, i], IOTA[:, bass.ds((2 * j + w) * P, P)],
                                                DST[:, bass.ds(t, 1)], None, ALU.is_equal)
                    v.wait_ge(s_ga[r % 4], 16 * (8 * j + r // 4 + 1))
                    need(v, s_em, t + 1)
                    need(v, s_ml, t - 1)
                    nc.vector.tensor_tensor(ZB3[:, r % 2], pb[r % 4], GA[:, r % 4], ALU.add).then_inc(s_z, 1)
                    if not (isinstance(j, int) and t == 0):
                        message_lo(t - 1, (r + 1) % 2)
                    if r % EPW == 8 and not (isinstance(j, int) and j == 4):
                        w3_lo(2 * j + r // EPW)
            attr_lo(0, 0)
            window_loop(v, edges_lo)
            message_lo(ET - 1, 1)

            v.wait_ge(s_w3e, NT)
            general = v.value_load(flag[0:1, 0:1], min_val=0, max_val=ET * P)
            with v.If(general > ET * P - N_EDGES):
                with v.Fori(0, NT) as d:
                    with v.Fori(0, ET) as t:
                        v.wait_ge(s_eh, GEN_G + d * ET + t + 1)
                        nc.vector.tensor_tensor(EH[:, 0, 1, 0:P], EA[:, 0, 0:P], EH[:, 0, 0, 0:P].bitcast(F32),
                                                ALU.subtract)
                        nc.vector.tensor_scalar(OH3[:, 0, 0], IOTA[:, bass.ds(d * P, P)], DST[:, bass.ds(t, 1)], None,
                                                ALU.is_equal).then_inc(s_el, 1)
                        v.wait_ge(s_ga[0], GEN_GA + (d * ET + t) * 16 + 16)
                        v.wait_ge(s_em, GEN_T + d * ET + t + 1)
                        nc.vector.tensor_tensor(ZB3[:, 0], pb[0], GA[:, 0], ALU.add).then_inc(s_z, 1)
                        v.wait_ge(s_mh, GEN_T + d * ET + t + 1)
                        nc.vector.scalar_tensor_tensor(MSG[:, 0, 1], ZB3[:, 0], 0.0, MSG[:, 0, 0].bitcast(F32), ALU.max,
                                                       ALU.subtract).then_inc(s_ml, 1)
                v.wait_ge(s_w3e, GEN_W + NT + 1)
                v.nop()
            with v.Else():
                v.nop()
            v.nop()

            def tile_of(t, n):
                return t[:, bass.ds(n, 1)].rearrange("p a f -> p (a f)")

            def h0(n):
                need(v, s_xa, 16 * (n + 1))
                nc.vector.scalar_tensor_tensor(tile_of(AGGR, n), X3A[:], ope[:, 1:2], tile_of(AGGR, n), ALU.mult,
                                               ALU.add).then_inc(n_h0, 1)

            def s4_lo(n):
                need(v, rows_hi, n + 1, R_MLP1)
                nc.vector.tensor_tensor(S4[:, 1], pb[0], S4[:, 0].bitcast(F32), ALU.subtract).then_inc(rows_lo, 1)

            def first_half(n, up, down):
                if not (isinstance(n, int) and n in (0, NT + 1)):
                    need(v, hid_hi, n, HT_MLP1)
                    nc.vector.tensor_tensor(S8[:, 1], big[:, 1:3].rearrange("p a f -> p (a f)"), S8[:, 0].bitcast(F32),
                                            ALU.subtract).then_inc(hid_lo, 1)
                if down:
                    need(v, lin2, n - 1, HT_MLP1)
                    need(v, x_ready, n - 2, N_MLP1)
                    nc.vector.tensor_tensor(Y2B[:], pb[5], V2A[:, 0], ALU.add).then_inc(biased, 1)
                    need(v, biased, n - 1, B_MLP1)
                    nc.vector.bn_stats(bst[:, 0, 0, :], Y2B[:]).then_inc(n_stats, 1)
                    need(v, n_stats, n - 1, N_MLP1)
                    v.sem_inc(s_fence, 1)
                    nc.vector.bn_aggr(bmv[:, 0, :], bst[:, 0, 0, :]).then_inc(n_var, 1)
                if up:
                    need(v, lin1, n + 1, R_MLP1)
                    need(v, hid_t, n, HT_MLP1)
                    nc.vector.tensor_tensor(Y1[:], big[:, 3:5].rearrange("p a f -> p (a f)"), V1A[:, 0], ALU.add).then_inc(n_y1b, 1)
                    need(v, n_y1b, n + 1)
                    nc.vector.bn_stats(bst1[:, 0, :], Y1[:, 0:D])
                    nc.vector.bn_stats(bst1[:, 1, :], Y1[:, D:]).then_inc(n_y1s, 1)
                    need(v, n_y1s, n + 1)
                    v.sem_inc(s_fence, 1)
                    nc.vector.bn_aggr(bmv1[:], bst1[:].rearrange("p a f -> p (a f)")).then_inc(n_y1v, 1)
                if down:
                    need(v, n_rstd, n - 1, N_MLP1)
                    nc.vector.scalar_tensor_tensor(Y2B[:], Y2B[:], bmv[:, 0, 0:1], V2A[:, 1], ALU.subtract,
                                                   ALU.mult).then_inc(gamma, 1)
                    need(v, gamma, n - 1)
                    nc.vector.scalar_tensor_tensor(Y2B[:], Y2B[:], rst[:, 0, 1:2], V2A[:, 2], ALU.mult,
                                                   ALU.add).then_inc(normed, 1)
                if up:
                    need(v, n_y1p, n + 1)
                    nc.vector.scalar_tensor_tensor(Y1[:], Y1[:], bmv1[:, 0:1], V1A[:, 1], ALU.subtract,
                                                   ALU.mult).then_inc(n_y1g, 1)
                    need(v, n_y1g, n + 1)
                    nc.vector.scalar_tensor_tensor(Y1[:], Y1[:], rst1[:, 1:2], V1B[:], ALU.mult,
                                                   ALU.add).then_inc(n_y1n, 1)
                if down:
                    need(v, n_y2, n - 1)
                    need(v, s_xb, 16 * (n - 1))
                    nc.vector.tensor_tensor(Y2B[:], Y2B[:], X3B[:], ALU.add).then_inc(res_add, 1)
                    need(v, res_add, n - 1)
                    nc.vector.bn_stats(bst[:, 0, 1, :], Y2B[:]).then_inc(o_stats, 1)
                    need(v, o_stats, n - 1, O_MLP1)
                    v.sem_inc(s_fence, 1)
                    nc.vector.bn_aggr(bmv2[:, 0, :], bst[:, 0, 1, :]).then_inc(o_var, 1)
                if up and not (isinstance(n, int) and n == NT - 1):
                    s4_lo(n + 1)
                if down:
                    need(v, o_rstd, n - 1, O_MLP1)
                    nc.vector.scalar_tensor_tensor(Y2B[:], Y2B[:], bmv2[:, 0, 0:1], V2A[:, 3], ALU.subtract,
                                                   ALU.mult).then_inc(n_rg, 1)
                    need(v, n_rg, n - 1)
                    nc.vector.scalar_tensor_tensor(tile_of(AGGR, n - 2), Y2B[:], rst2[:, 0, 1:2], V2B[:, 0], ALU.mult,
                                                   ALU.add).then_inc(x_ready, 1)
                if up and not (isinstance(n, int) and n >= NT - 2):
                    h0(n + 2)
            v.wait_ge(s_ope, 1)
            h0(0)
            h0(1)
            s4_lo(0)
            v.wait_ge(s_v1a, 32)
            v.wait_ge(s_v1b, 16)
            v.wait_ge(s_v2a, 64)
            v.wait_ge(s_v2b, 48)
            for n in (0, 1):
                first_half(n, True, False)
            with v.Fori(2, NT - 2) as n:
                first_half(n, True, True)
            for n in (NT - 2, NT - 1):
                first_half(n, True, True)
            for n in (NT, NT + 1):
                first_half(n, False, True)

            def m4_lo(n):
                need(v, rows_hi, n + 1, R_MLP2)
                nc.vector.tensor_tensor(S4[:, 1], pb[0], S4[:, 0].bitcast(F32), ALU.subtract).then_inc(rows_lo, 1)

            def m8_lo(n):
                need(v, hid_hi, n + 1, HT_MLP2)
                nc.vector.tensor_tensor(S8[:, 1], big[:, 1:3].rearrange("p a f -> p (a f)"), S8[:, 0].bitcast(F32),
                                        ALU.subtract).then_inc(hid_lo, 1)

            def y_stats(n):
                need(v, lin2, n + 1, HT_MLP2)
                need(v, x_ready, n, N_MLP2)
                nc.vector.tensor_tensor(Y2B[:], pb[5], tile_of(AGGR, n), ALU.add).then_inc(biased, 1)
                need(v, biased, n + 1, B_MLP2)
                nc.vector.bn_stats(bst[:, 0, 0, :], Y2B[:]).then_inc(n_stats, 1)
                need(v, n_stats, n + 1, N_MLP2)
                v.sem_inc(s_fence, 1)
                nc.vector.bn_aggr(bmv[:, 0, :], bst[:, 0, 0, :]).then_inc(n_var, 1)

            def y_out(n):
                need(v, n_rstd, n + 1, N_MLP2)
                nc.vector.scalar_tensor_tensor(Y2B[:], Y2B[:], bmv[:, 0, 0:1], V2B[:, 1], ALU.subtract,
                                               ALU.mult).then_inc(gamma, 1)
                need(v, gamma, n + 1, B_MLP1)
                nc.vector.scalar_tensor_tensor(Y2B[:], Y2B[:], rst[:, 0, 1:2], V2B[:, 2], ALU.mult,
                                               ALU.add).then_inc(normed, 1)
                need(v, normed, n + 1, B_MLP1)
                need(v, s_xb, 16 * (NT + n + 1))
                nc.vector.tensor_tensor(Y2B[:], Y2B[:], X3B[:], ALU.add).then_inc(res_add, 1)
                need(v, res_add, n + 1, B_MLP1)
                nc.vector.bn_stats(bst[:, 0, 1, :], Y2B[:]).then_inc(o_stats, 1)
                need(v, o_stats, n + 1, O_MLP2)
                v.sem_inc(s_fence, 1)
                nc.vector.bn_aggr(bmv2[:, 0, :], bst[:, 0, 1, :]).then_inc(o_var, 1)
                need(v, o_rstd, n + 1, O_MLP2)
                need(v, m_st, 16 * n)
                nc.vector.tensor_scalar(OUTB[:], Y2B[:], bmv2[:, 0, 0:1], rst2[:, 0, 1:2], ALU.subtract,
                                        ALU.mult).then_inc(x_ready, 1)

            m4_lo(0)
            m4_lo(1)
            m8_lo(0)
            with v.Fori(1, NT - 1) as n:
                m4_lo(n + 1)
                y_stats(n - 1)
                m8_lo(n)
                y_out(n - 1)
            y_stats(NT - 2)
            m8_lo(NT - 1)
            y_out(NT - 2)
            y_stats(NT - 1)
            y_out(NT - 1)

        @block.tensor
        def _(pe):
            pe.wait_ge(s_cst, 7)
            pe.wait_ge(s_viol, 1)
            nc.tensor.matmul(pb[7][0:1, 0:1], ones[:, 0:1], VSM[:, 0:1], start=True, stop=True).then_inc(s_vsum, 1)

            def windows(j):
                for r in range(2 * EPW):
                    t = 2 * EPW * j + r
                    need(pe, s_oh, t + 1)
                    for i, s in enumerate(shifts(j, r)):
                        first, final = opens(j, r, s), closes(j, r, s)
                        if first:
                            need(pe, s_wev, 2 * j + s - 1)
                        for c, w in ((0, 512), (1, 512), (2, 256)):
                            last = nc.tensor.matmul(pb[3 * (s % 2) + c][:, 0:w], OHD[:, r % 4, i, :],
                                                    OHS[:, r % 4, 512 * c:512 * c + w], start=first, stop=final)
                        if final:
                            last.then_inc(s_win, 1)
                    if not final:
                        last.then_inc(s_ohu, 1)
            window_loop(pe, windows)

            pe.wait_ge(s_flag, 1)
            pe.wait_ge(s_wev, NT)
            general = pe.value_load(flag[0:1, 0:1], min_val=0, max_val=ET * P)
            with pe.If(general > ET * P - N_EDGES):
                pe.sem_inc(s_ohu, 1)
                with pe.Fori(0, NT) as d:
                    pe.wait_ge(s_wev, GEN_W + d + 1)
                    for c, w in ((0, 512), (1, 512), (2, 256)):
                        nc.tensor.matmul(pb[c][:, 0:w], ZB[:], OHS[:, 0, 512 * c:512 * c + w], start=True, stop=False)
                    with pe.Fori(0, ET) as t:
                        pe.wait_ge(s_oh, GEN_T + d * ET + t + 1)
                        for c, w in ((0, 512), (1, 512), (2, 256)):
                            last = nc.tensor.matmul(pb[c][:, 0:w], OHD[:, 0, 0, :], OHS[:, 0, 512 * c:512 * c + w],
                                                    start=False, stop=False)
                        last.then_inc(s_ohu, 1)
                    for c, w in ((0, 512), (1, 512), (2, 256)):
                        last = nc.tensor.matmul(pb[c][:, 0:w], ZB[:], OHS[:, 0, 512 * c:512 * c + w], start=False, stop=True)
                    last.then_inc(s_win, 1)
                pe.nop()
            with pe.Else():
                pe.nop()
            pe.nop()

            for d in range(NT):
                if d >= 2:
                    pe.wait_ge(s_tra, d - 1)
                    pe.wait_ge(s_trv, d - 1)
                for k in range(NT):
                    last = nc.tensor.transpose(pb[3 * (d % 2) + k // 4][:, P * (k % 4):P * (k % 4 + 1)],
                                               ADS[:, d, k * P:(k + 1) * P].bitcast(F32), ident[:])
                    if k in (3, 7, 9):
                        last.then_inc(s_tr, 1)

            def l0_transpose(n):
                if n == 0:
                    pe.wait_ge(s_x, 16)
                if n >= 2:
                    pe.wait_ge(rows_lo, n - 1)
                for k in range(KT):
                    last = nc.tensor.transpose(pb[n % 2][:, P * k:P * (k + 1)], X[:, n, k * P:(k + 1) * P], ident[:])
                last.then_inc(rows_t, 1)

            pe.wait_ge(s_tra, NT)
            pe.wait_ge(s_trv, NT)
            l0_transpose(0)
            for n in range(NT):
                if n + 1 < NT:
                    l0_transpose(n + 1)
                b = n % 2
                if n == 0:
                    pe.wait_ge(w_lo, 1)
                pe.wait_ge(rows_lo, n + 1)
                if n >= 2:
                    pe.wait_ge(s_l0f, n - 1)
                for k in range(KT):
                    xh, xl = XSP[:, b, 0, k * P:(k + 1) * P], XSP[:, b, 1, k * P:(k + 1) * P]
                    nc.tensor.matmul(pb[2 + b], xh, W0H[:, k, :], start=k == 0, stop=False)
                    nc.tensor.matmul(pb[2 + b], xh, W0L[:, k, :], start=False, stop=False)
                    last = nc.tensor.matmul(pb[2 + b], xl, W0H[:, k, :], start=False, stop=k == KT - 1)
                last.then_inc(lin1, 1)

            pe.wait_ge(s_idr, 1)
            for n in range(NT):
                b = 4 + n % 2
                if n >= 2:
                    pe.wait_ge(s_l0r, NT + n - 1)
                for k in range(NT):
                    if n == 0:
                        pe.wait_ge(feat_lo, k + 1)
                    for g in (G1H, G1L):
                        nc.tensor.matmul(pb[b], ADS[:, k, n * P:(n + 1) * P], g[:, k, :], start=k == 0 and g is G1H,
                                         stop=False)
                nc.tensor.matmul(pb[b], identr[:], G1H[:, n, :], start=False, stop=False)
                nc.tensor.matmul(pb[b], identr[:], G1L[:, n, :], start=False, stop=True).then_inc(agg, 1)

            pe.wait_ge(s_gw, 32)
            for n in range(NT):
                pe.wait_ge(x_ready, n + 1)
                if n >= 2:
                    pe.wait_ge(s_1x, n - 1)
                for k in range(KT):
                    last = nc.tensor.transpose(pb[n % 2][:, P * k:P * (k + 1)], X[:, n, k * P:(k + 1) * P], ident[:])
                last.then_inc(rows_t, 1)
            for n in range(NT):
                pe.wait_ge(s_1x, n + 1)
                for k in range(KT):
                    last = nc.tensor.matmul(pb[7][:, n * NE:(n + 1) * NE], XT[:, n, k * P:(k + 1) * P], GW[:, k, :],
                                            start=k == 0, stop=k == KT - 1)
                last.then_inc(s_1g, 1)

            def l1_agg_transpose(n):
                pe.wait_ge(agg_s, n + 1)
                if n >= 2:
                    pe.wait_ge(s_1c, n - 1)
                for k in range(KT):
                    last = nc.tensor.transpose(pb[4 + n % 2][:, P * k:P * (k + 1)], AGB[:, n % 2, k * P:(k + 1) * P], ident[:])
                last.then_inc(s_1b, 1)

            for n in range(NT):
                if n >= 2:
                    pe.wait_ge(agg_s, n - 1)
                for k in range(NT):
                    if n == 0:
                        pe.wait_ge(feat_lo, F_L1 + k + 1)
                    for g in (G1H, G1L):
                        last = nc.tensor.matmul(pb[2 + n % 2], ASD[:, k, n * P:(n + 1) * P], g[:, k, :],
                                                start=k == 0 and g is G1H, stop=k == NT - 1 and g is G1L)
                last.then_inc(agg, 1)
                if n >= 1:
                    l1_agg_transpose(n - 1)
            l1_agg_transpose(NT - 1)

            def split_product(out, xh, xl, w, start, stop):
                wh, wl = w
                for k in range(KT):
                    c = slice(k * P, (k + 1) * P)
                    nc.tensor.matmul(out, xh[:, c], wh[:, k, :], start=start and k == 0, stop=False)
                    nc.tensor.matmul(out, xh[:, c], wl[:, k, :], start=False, stop=False)
                    last = nc.tensor.matmul(out, xl[:, c], wh[:, k, :], start=False, stop=stop and k == KT - 1)
                return last

            def first_layer(m):
                need(pe, rows_lo, m + 1, R_EX)
                split_product(pb[0], XA[:, 0, 0], XA[:, 0, 1], (WA[:, 0, 0], WA[:, 0, 1]), True, False)
                split_product(pb[0], XA[:, 1, 0], XA[:, 1, 1], (WA[:, 1, 0], WA[:, 1, 1]), False, True).then_inc(lin1, 1)

            def transpose_h(m):
                need(pe, s_h, m + 1)
                for k in range(KT):
                    last = nc.tensor.transpose(pb[2][:, P * k:P * (k + 1)], HB[:, k * P:(k + 1) * P], ident[:])
                last.then_inc(hid_t, 1)

            def second_layer(m):
                need(pe, hid_lo, m + 1)
                need(pe, s_r, m)
                split_product(pb[4], HT[:, 0], HT[:, 1], (WB[:, 0, 0], WB[:, 0, 1]), True, True)
                split_product(pb[5], HT[:, 0], HT[:, 1], (WB[:, 1, 0], WB[:, 1, 1]), True, True).then_inc(lin2, 1)

            def expert(e, final):
                m = e * NT + 1
                transpose_h(m - 1)
                first_layer(m)
                pe.wait_ge(s_w1, e + 1)
                second_layer(m - 1)
                with pe.Fori(2, NT) as n:
                    transpose_h(e * NT + n - 1)
                    first_layer(e * NT + n)
                    second_layer(e * NT + n - 1)
                if not final:
                    m = e * NT + NT
                    transpose_h(m - 1)
                    pe.wait_ge(s_w0, e + 2)
                    first_layer(m)
                    second_layer(m - 1)

            pe.wait_ge(s_w0, 1)
            first_layer(0)
            with pe.Fori(0, NE - 1) as e:
                expert(e, False)
            expert(NE - 1, True)
            transpose_h(NE * NT - 1)
            second_layer(NE * NT - 1)

            for e in range(NE):
                pe.wait_ge(s_gin[e % 2], 32 * (e // 2 + 1))
                G = (G2, G1)[e % 2]
                for n in range(NT):
                    m = e * NT + n
                    need(pe, s_2t, m - 1)
                    for k in range(NT):
                        for half in (0, 1):
                            last = nc.tensor.matmul(pb[m % 2], ASD[:, k, n * P:(n + 1) * P], G[:, half, k],
                                                    start=k == 0 and half == 0, stop=k == NT - 1 and half == 1)
                    last.then_inc(agg, 1)

            def l2_transpose(n):
                pe.wait_ge(agg_s, SC_L2 + n + 1)
                if n >= 1:
                    pe.wait_ge(rows_lo, R_L2 + n)
                for k in range(KT):
                    nc.tensor.transpose(pb[0][:, P * k:P * (k + 1)], X[:, n, k * P:(k + 1) * P], ident[:])
                for k in range(KT):
                    last = nc.tensor.transpose(pb[1][:, P * k:P * (k + 1)], AG2[:, n % 2, k * P:(k + 1) * P], ident[:])
                last.then_inc(rows_t, 1)

            def l2_linear(n):
                pe.wait_ge(rows_lo, R_L2 + n + 1)
                if n >= 2:
                    pe.wait_ge(biased, n - 1)
                split_product(pb[4 + n % 2], XA2[:, 0, 0], XA2[:, 0, 1], (WA[:, 0, 0], WA[:, 0, 1]), True, False)
                split_product(pb[4 + n % 2], XA2[:, 1, 0], XA2[:, 1, 1], (WA[:, 1, 0], WA[:, 1, 1]), False, True).then_inc(lin1, 1)

            pe.wait_ge(s_2t, NE * NT)
            pe.wait_ge(w_lo, W_L2 + 1)
            for n in range(NT):
                if n >= 1:
                    l2_transpose(n - 1)
                if n >= 2:
                    pe.wait_ge(agg_s, SC_L2 + n - 1)
                for k in range(NT):
                    if n == 0:
                        pe.wait_ge(feat_lo, F_L2 + k + 1)
                    for half in (0, 1):
                        last = nc.tensor.matmul(pb[2 + n % 2], ASD[:, k, n * P:(n + 1) * P], G2[:, half, k],
                                                start=k == 0 and half == 0, stop=k == NT - 1 and half == 1)
                last.then_inc(agg, 1)
                if n >= 1:
                    l2_linear(n - 1)
            l2_transpose(NT - 1)
            l2_linear(NT - 1)

            def scatter(j):
                for r in range(2 * EPW):
                    t = 2 * EPW * j + r
                    if not (isinstance(j, int) and t + 2 >= ET):
                        embed_at(j, r + 2)
                    need(pe, s_ml, t + 1)
                    for i, w in enumerate(shifts(j, r)):
                        first, final = opens(j, r, w), closes(j, r, w)
                        if first:
                            need(pe, s_w3e, 2 * j + w - 1)
                        nc.tensor.matmul(pb[4 + w % 2], OH3[:, r % 4, i], MSG[:, r % 2, 0], start=first, stop=False)
                        last = nc.tensor.matmul(pb[4 + w % 2], OH3[:, r % 4, i], MSG[:, r % 2, 1], start=False, stop=final)
                        if final:
                            last.then_inc(s_w3d, 1)
                    if not final:
                        last.then_inc(s_sc, 1)

            def embed_at(j, r):
                t = 2 * EPW * j + r
                if r % 4 == 0:
                    need(pe, s_el, 8 * j + r // 4 + 1)
                need(pe, s_z, t - 3)
                b, c = (r // 4) % 2, slice((r % 4) * P, (r % 4 + 1) * P)
                nc.tensor.matmul(pb[r % 4], EH[:, b, 0, c], WE[:, 0], start=True, stop=False)
                nc.tensor.matmul(pb[r % 4], EH[:, b, 0, c], WE[:, 1], start=False, stop=False)
                nc.tensor.matmul(pb[r % 4], EH[:, b, 1, c], WE[:, 0], start=False, stop=True).then_inc(s_em, 1)

            pe.wait_ge(w_lo, W_EDGE + 1)
            pe.wait_ge(biased, NT)
            embed_at(0, 0)
            embed_at(0, 1)
            window_loop(pe, scatter)

            pe.wait_ge(s_w3e, NT)
            general = pe.value_load(flag[0:1, 0:1], min_val=0, max_val=ET * P)
            with pe.If(general > ET * P - N_EDGES):
                pe.sem_inc(s_sc, 1)
                with pe.Fori(0, NT) as d:
                    pe.wait_ge(s_w3e, GEN_W + d + 1)
                    nc.tensor.matmul(pb[4], ZB[:], IOTA[:, 0:512], start=True, stop=False)
                    with pe.Fori(0, ET) as t:
                        pe.wait_ge(s_el, GEN_G + d * ET + t + 1)
                        nc.tensor.matmul(pb[0], EH[:, 0, 0, 0:P], WE[:, 0], start=True, stop=False)
                        nc.tensor.matmul(pb[0], EH[:, 0, 0, 0:P], WE[:, 1], start=False, stop=False)
                        nc.tensor.matmul(pb[0], EH[:, 0, 1, 0:P], WE[:, 0], start=False, stop=True).then_inc(s_em, 1)
                        pe.wait_ge(s_ml, GEN_T + d * ET + t + 1)
                        nc.tensor.matmul(pb[4], OH3[:, 0, 0], MSG[:, 0, 0], start=False, stop=False)
                        nc.tensor.matmul(pb[4], OH3[:, 0, 0], MSG[:, 0, 1], start=False, stop=False).then_inc(s_sc, 1)
                    nc.tensor.matmul(pb[4], ZB[:], IOTA[:, 0:512], start=False, stop=True).then_inc(s_w3d, 1)
                pe.nop()
            with pe.Else():
                pe.nop()
            pe.nop()

            def up_product(first_matrix):
                split_product(pb[3], S4[:, 0], S4[:, 1], (W3H[:, first_matrix], W3L[:, first_matrix]), True, True)
                return split_product(pb[4], S4[:, 0], S4[:, 1], (W3H[:, first_matrix + 1], W3L[:, first_matrix + 1]), True, True)

            def down_product(first_matrix):
                split_product(pb[5], S8[:, 0, 0:D], S8[:, 1, 0:D], (W3H[:, first_matrix], W3L[:, first_matrix]), True, False)
                return split_product(pb[5], S8[:, 0, D:], S8[:, 1, D:], (W3H[:, first_matrix + 1], W3L[:, first_matrix + 1]), False, True)

            def transpose_row(n, done):
                for k in range(KT):
                    last = nc.tensor.transpose(pb[0][:, P * k:P * (k + 1)], AGGR[:, n, k * P:(k + 1) * P], ident[:])
                last.then_inc(done, 1)

            def transpose_wide(done):
                for k in range(2 * KT):
                    last = nc.tensor.transpose(pb[1 + k // KT][:, P * (k % KT):P * (k % KT + 1)],
                                               Y1[:, k * P:(k + 1) * P], ident[:])
                last.then_inc(done, 1)

            pe.wait_ge(w_lo, W_MLP + 8)
            pe.wait_ge(n_h0, 1)
            transpose_row(0, rows_t)
            for n in range(NT + 2):
                if n >= 2:
                    pe.wait_ge(hid_lo, HT_MLP1 + n - 1)
                    if n >= 3:
                        pe.wait_ge(biased, B_MLP1 + n - 2)
                    down_product(2).then_inc(lin2, 1)
                if 1 <= n <= NT:
                    pe.wait_ge(n_y1, n)
                    transpose_wide(hid_t)
                if n < NT:
                    pe.wait_ge(rows_lo, R_MLP1 + n + 1)
                    need(pe, n_y1b, n)
                    up_product(0).then_inc(lin1, 1)
                if n + 1 < NT:
                    pe.wait_ge(n_h0, n + 2)
                    transpose_row(n + 1, rows_t)

            pe.wait_ge(x_ready, N_MLP1 + 1)
            transpose_row(0, rows_t)
            for n in range(NT + 1):
                if n < NT:
                    pe.wait_ge(rows_lo, R_MLP2 + n + 1)
                    need(pe, m_g, n)
                    if n == 0:
                        pe.wait_ge(n_y1b, NT)
                    up_product(4).then_inc(lin1, 1)
                if n + 1 < NT:
                    pe.wait_ge(x_ready, N_MLP1 + n + 2)
                    transpose_row(n + 1, rows_t)
                if n >= 1:
                    pe.wait_ge(hid_lo, HT_MLP2 + n)
                    if n >= 2:
                        pe.wait_ge(biased, B_MLP2 + n - 1)
                    down_product(6).then_inc(lin2, 1)
                if n < NT:
                    pe.wait_ge(m_g, n + 1)
                    transpose_wide(hid_t)


_INS = ["x", "src", "dst", "w0", "b0", "gate_w", "gate_b", "w1", "b1", "w2", "l2_bias", "l2_gamma", "l2_beta",
        "edge_attr", "w_edge", "b_edge", "eps", "w3", "v1", "v2"]


def kernel(**inputs):
    import numpy as _np
    import concourse.bacc as _bacc
    from concourse import mybir as _mybir
    from concourse.bass_utils import run_bass_kernel_spmd as _run

    def edges(a, fill):
        padded = _np.full(ET * P, fill, _np.int32)
        padded[:N_EDGES] = a
        return _np.ascontiguousarray(padded.reshape(ET, P).T)

    def matrix(w):
        return _np.ascontiguousarray(w.reshape(KT, P, D).transpose(1, 0, 2))

    wl, wr = _np.asarray(inputs["L1_gnn_Wl"]), _np.asarray(inputs["L1_gnn_Wr"])
    w1 = _np.stack([_np.stack([_np.stack([matrix(wr[e, 0]), matrix(wl[e, 0])], axis=1),
                               _np.stack([matrix(wl[e, 1]), matrix(wr[e, 1])], axis=1)]) for e in range(NE)])
    w3 = []
    for up, down in (("L3_gnn_W1", "L3_gnn_W2"), ("L3_gnn_M1", "L3_gnn_M2")):
        u, d = _np.asarray(inputs[up]), _np.asarray(inputs[down])
        w3 += [matrix(u[:, :D]), matrix(u[:, D:]), matrix(d[:D]), matrix(d[D:])]
    w3 = _np.stack(w3, axis=1)
    attr = _np.zeros((ET * P, P), _np.float32)
    attr[:N_EDGES] = inputs["edge_attr_128"]
    xp = _np.zeros((NP, D), _np.float32)
    xp[:N_NODES] = inputs["x"]
    data = {
        "x": _np.ascontiguousarray(xp.reshape(NT, P, D).transpose(1, 0, 2)),
        "src": edges(_np.asarray(inputs["src"]), 0), "dst": edges(_np.asarray(inputs["dst"]), NO_NODE),
        "w0": matrix(_np.asarray(inputs["L0_gnn_W"]).T), "b0": _np.asarray(inputs["L0_gnn_b"]),
        "gate_w": _np.asarray(inputs["L1_gnn_gate_W"]).reshape(KT, P, NE).transpose(1, 0, 2),
        "gate_b": _np.asarray(inputs["L1_gnn_gate_b"]),
        "w1": w1, "b1": _np.asarray(inputs["L1_gnn_bl"]),
        "w2": _np.stack([matrix(_np.asarray(inputs["L2_gnn_W_self"]).T),
                         matrix(_np.asarray(inputs["L2_gnn_W_neigh"]).T)], axis=1),
        "l2_bias": _np.asarray(inputs["L2_gnn_bias"]), "l2_gamma": _np.asarray(inputs["L2_gnn_gamma"]),
        "l2_beta": _np.asarray(inputs["L2_gnn_beta"]),
        "edge_attr": _np.ascontiguousarray(attr.reshape(ET // 4, 4 * P, P).transpose(0, 2, 1)),
        "w_edge": _np.asarray(inputs["L3_gnn_W_edge"]), "b_edge": _np.asarray(inputs["L3_gnn_b_edge"]),
        "eps": _np.asarray(inputs["L3_gnn_eps"]).reshape(1), "w3": w3,
        "v1": _np.stack([_np.asarray(inputs["L3_gnn_" + n]) for n in ("b1", "g1", "be1")]),
        "v2": _np.stack([_np.asarray(inputs["L3_gnn_" + n]) for n in ("b2", "g2", "be2", "gA", "bA", "gB", "bB")]),
    }
    nc = _bacc.Bacc("TRN2", target_bir_lowering=False, num_devices=1)
    arrays, args = {}, []
    for name in _INS:
        a = _np.ascontiguousarray(data[name])
        arrays[f"in_{name}_dram"] = a
        args.append(nc.dram_tensor(f"in_{name}_dram", a.shape, _mybir.dt.from_np(a.dtype), kind="ExternalInput").ap())
    out = nc.dram_tensor("out_dram", (P, NT, D), _mybir.dt.float32, kind="ExternalOutput").ap()
    build(nc, *args, out)
    r = _run(nc, [arrays], core_ids=[0])
    y = r.results[0]["out_dram"]
    return _np.ascontiguousarray(y.transpose(1, 0, 2).reshape(NP, D)[:N_NODES])
```

```python
import numpy as np
import concourse.bass as bass
from concourse import mybir
from contextlib import ExitStack

F32 = mybir.dt.float32
F32R = mybir.dt.float32r
F16 = mybir.dt.float16
BF16 = mybir.dt.bfloat16
I32 = mybir.dt.int32
ALU = mybir.AluOpType
ACT = mybir.ActivationFunctionType
AX = mybir.AxisListType

P = 128
N_NODES = 1250
NT = 10
NP = NT * P
N_EDGES = 20000
ET = 160
EPW = ET // NT
MARGIN = 2
NO_NODE = 4096
D = 512
KT = D // P
NE = 4
AHEAD = 3
EPS = 1e-5


def shifts(j, r):
    own, at = divmod(r, EPW)
    ws = [own]
    if at < MARGIN and not (isinstance(j, int) and 2 * j + own == 0):
        ws.insert(0, own - 1)
    if at >= EPW - MARGIN and not (isinstance(j, int) and 2 * j + own == NT - 1):
        ws.append(own + 1)
    return ws


def opens(j, r, s):
    if isinstance(j, int) and 2 * j + s == 0:
        return r == 0
    return r == EPW * s - MARGIN


def closes(j, r, s):
    if isinstance(j, int) and 2 * j + s == NT - 1:
        return r == 2 * EPW - 1
    return r == EPW * (s + 1) + MARGIN - 1


def whole(r):
    return r % 4 == 1


def splits(j, r):
    return 2 * EPW * 3 // 4 * j + (sum(not whole(i) for i in range(r + 1)) if r >= -1 else -1)


def need(eng, sem, value, since=0):
    if isinstance(value, int) and value <= 0:
        return
    eng.wait_ge(sem, since + value)


def tile_loop(eng, step):
    for n in (0, 1):
        step(n, n)
    with eng.Fori(1, NT // 2 - 1) as i:
        step(2 * i, 0)
        step(2 * i + 1, 1)
    for n in (NT - 2, NT - 1):
        step(n, n % 2)


def node_loop(eng, step):
    for q in range(3):
        step(q, q)
    with eng.Fori(3, NT - 2) as q:
        step(q, 3)
    for q in range(NT - 2, NT + 3):
        step(q, q)
    with eng.Fori(NT + 3, 2 * NT - 1) as q:
        step(q, NT + 3)
    for q in range(2 * NT - 1, 2 * NT + 2):
        step(q, q)


def window_loop(eng, step):
    step(0)
    with eng.Fori(1, NT // 2 - 1) as j:
        step(j)
    step(NT // 2 - 1)


def build(nc, x, src, dst, w0, b0, gate_w, gate_b, w1, b1, w2, l2_bias, l2_gamma, l2_beta,
          edge_attr, w_edge, b_edge, eps, w3, v1, v2, out):
    ctx = ExitStack()
    with ctx:
        base = (nc.sbuf_base + 63) // 64 * 64
        assert nc.sbuf_usable_end - base >= 212800

        def at(offset, name, shape, dt=F32):
            return nc.alloc_sbuf_tensor_at(name, shape, dt, offset=base + offset)

        def sem(name):
            return ctx.enter_context(nc.semaphore(name))

        MAT = KT * D * 4
        NODE = NT * D * 4
        ADJ = NT * NP * 4
        R0, R1 = 0, ADJ
        R2 = R1 + ADJ
        R3 = R2 + 2 * NODE
        R4 = R3 + NODE
        R5 = R4 + 4 * MAT
        ASD = at(R0, "adj_src_dst", [P, NT, NP], F32R)
        ADS = at(R1, "adj_dst_src", [P, NT, NP], F32R)
        G1H = at(R2, "g1_hi", [P, NT, D], F32R)
        G1L = at(R2 + NODE, "g1_lo", [P, NT, D], F32R)
        OHS = at(R2, "onehot_src", [P, 4, NP], BF16)
        OHD = at(R2 + 4 * NP * 2, "onehot_dst", [P, 4, 2, P], BF16)
        X = at(R3, "x_nodes", [P, NT, D])
        W0H = at(R4, "w0_hi", [P, KT, D], F32R)
        W0L = at(R4 + MAT, "w0_lo", [P, KT, D], F32R)
        STG = at(R4 + 2 * MAT, "w_stage", [P, KT, D])
        FB = at(R4 + 3 * MAT, "feat", [P, 2, D])
        TB = at(R4 + 3 * MAT + 4096, "resid", [P, 2, D])
        small = [R5]

        def keep(name, shape, dt=F32):
            nbytes = int(np.prod(shape[1:])) * (2 if dt in (F16, BF16) else 4)
            t = at(small[0], name, shape, dt)
            small[0] += (nbytes + 31) // 32 * 32
            assert small[0] <= 212800, small[0]
            return t


        SRC = keep("src_index", [P, ET], I32)
        DST = keep("dst_f32", [P, ET])
        SRCF = at(R2 + 36864 + 640, "src_f32", [P, ET])
        IOTA = keep("iota_nodes", [P, NP], F16)
        BC0 = at(small[0] - NP * 2, "bias0", [P, D])
        ident = keep("ident", [P, P])
        identr = keep("ident_r", [P, P], F32R)
        ZB = keep("zeros_bf16", [P, P], BF16)
        ones = keep("ones", [P, 2])
        onesr = keep("ones_r", [P, 2], F32R)
        cst = keep("consts", [P, 4])
        dis = keep("deg_inv_sqrt", [P, NT])
        inv = keep("deg_inv", [P, NT])
        degs = keep("deg_src", [P, NT])
        degd = keep("deg_dst", [P, NT])
        bst = keep("bn_stats", [P, 2, 2, 6])
        bmv = keep("bn_mean_var", [P, 2, 2])
        rst = keep("rstd", [P, 2, 2])
        bmv2 = keep("outer_mean_var", [P, 2, 2])
        rst2 = keep("outer_rstd", [P, 2, 2])
        flag = keep("flag", [1, 2], I32)
        GW = keep("gate_w", [P, KT, NE])
        GBI = keep("gate_bias", [P, NE])
        lg = keep("gate_logits", [P, NT, NE])
        ex = keep("gate_exp", [P, NT, NE])
        gv = keep("gate_values", [P, NT, NE])
        gm = keep("gate_max", [P, 2, NT])
        gate = keep("gate_weights", [P, NT, NE])
        IDXB = keep("gather_index", [P, 16], I32)
        ope = keep("one_plus_eps", [P, 2])
        bst1 = keep("bn_stats1", [P, 2, 6])
        bmv1 = keep("bn_mean_var1", [P, 2])
        rst1 = keep("rstd1", [P, 2])
        XSP_AT = small[0]
        DROW = at(XSP_AT + 8192 - NP * 4, "deg_src_row", [1, NP])
        XSP = keep("x_split", [P, 2, 2, D], F32R)
        IOTI = at(R2 + 16384, "iota_int", [P, NP], I32)
        BND = at(R2 + 16384, "bounds", [P, 2, NT, EPW], I32)
        BNF = at(R2 + 24576, "bounds_f32", [P, 2, NT * EPW])
        VIO = at(R2 + 28672, "violations", [P, 2, ET])
        VSM = at(R2 + 32768, "violation_sums", [P, 2])
        DSTI = at(R2 + 36864, "dst_int", [P, ET], I32)

        XT = at(R1, "x1_transposed", [P, NT, D])
        AT = at(R1 + NODE, "agg1_transposed", [P, NT, D])
        SPARE = R1 + 2 * NODE
        XA = at(SPARE, "x_agg_split", [P, 2, 2, D], F32R)
        HB = at(SPARE + 8192, "h_nodes", [P, D])
        AGB = at(XSP_AT, "agg_nodes", [P, 2, D])
        WA = at(R4, "w_first", [P, 2, 2, KT, D], F32R)
        WB = at(R2, "w_second", [P, 2, 2, KT, D], F32R)
        ST2 = at(R3, "w_stage2", [P, 2, KT, D])
        RB = at(R3 + 2 * MAT, "r_out", [P, D])
        HT = at(R2 + 4 * MAT, "h_transposed", [P, 2, D], F32R)
        B1A = at(R2 + 4 * MAT + 4096, "bias1_first", [P, D])
        B1B = at(R2 + 4 * MAT + 6144, "bias1_second", [P, D])
        GB = at(XSP_AT + 6144, "g_out", [P, D])
        G2 = at(R1, "g2", [P, 2, NT, D], F32R)
        G1 = at(R2, "g1_again", [P, 2, NT, D], F32R)
        RR = at(SPARE, "r_ring", [P, 5, D])
        G2R = at(R1, "g2_raw", [P, 2, NT, D])
        G1R = at(R2, "g1_raw", [P, 2, NT, D])
        X1R = at(R4, "x1_again", [P, NT, D])
        ACC = X
        TU = at(XSP_AT, "gated", [P, 2, 2, D])
        WLR = at(R4, "w2_raw", [P, 2, 2, KT, D])
        AG2 = at(XSP_AT, "agg2_nodes", [P, 2, D])
        XA2 = at(SPARE, "x_agg_split2", [P, 2, 2, D], F32R)
        BC2 = at(R2, "bias_gamma_beta2", [P, 3, D])
        Y2 = at(R2 + 6144, "y2", [P, 2, D])
        Z2 = at(R2 + 6144 + 4096, "z2", [P, 2, D])
        X1D = nc.dram_tensor("x1_spill", [P, NT, D], F32)
        GD = nc.dram_tensor("g_spill", [P, NE * NT, D], F32)
        RD = nc.dram_tensor("r_spill", [NE * NT, P, D], F32)

        W3H = at(R0, "w3_hi", [P, 8 * KT, D], F32R)
        W3L = at(R0 + 8 * MAT, "w3_lo", [P, 8 * KT, D], F32R)
        W3R = at(R0 + 8 * MAT, "w3_raw", [P, 8 * KT, D])
        FREE = 16 * MAT
        GA = at(FREE, "gathered", [P, 4, D])
        GA2 = at(XSP_AT, "gathered_more", [P, 4, D])

        def gathered(r):
            return (GA, GA2)[r // 4 % 2][:, r % 4]

        AGGR = at(R4, "edge_sums", [P, NT, D])
        EA = at(R4 + NODE, "edge_attr_raw", [P, 2, D])
        EH = at(R4 + NODE + 4096, "edge_attr_split", [P, 2, 2, D], F32R)
        ZB3 = at(R3, "edge_z", [P, 2, D])
        MSG = at(R3 + 4096, "messages", [P, 2, 2, D], F32R)
        MSGF = at(R3 + 4096 + 4096, "message_whole", [P, D])
        OH3 = at(R3 + 12288, "onehot_dst_r", [P, 4, 2, P], F32R)
        WE = at(FREE + 8192, "w_edge_split", [P, 2, D], F32R)
        WER = at(FREE + 8192, "w_edge_raw", [P, 2, D])
        BE = at(R2 + 14336, "b_edge", [P, D])
        TAB = at(XSP_AT + 4096, "table_rows", [P, 2, D])
        TABD = nc.dram_tensor("x3_table", [NP, D], F32)
        X3D = nc.dram_tensor("x3_spill", [NT, P, D], F32)
        IOT3 = at(R2 + 16384, "iota_int3", [P, NP], I32)
        V1A = at(XSP_AT, "bias1_gamma1", [P, 2, 2 * D])
        V1B = at(FREE, "beta1", [P, 2 * D])
        V2A = at(FREE + 4096, "vectors2_first", [P, 4, D])
        V2B = at(R3 + 8192, "vectors2_last", [P, 3, D])
        Y1 = at(R3, "y1_or_m", [P, 2 * D])
        Y2B = at(R3 + 4096, "y2_or_y", [P, D])
        X3A = at(R3 + 16384, "x3_for_h0", [P, D])
        Y2R = at(R3 + 18432, "x3_plus_y2", [P, D])
        X3B = at(R3 + 14336, "x3_for_residual", [P, D])
        OUTB = at(R3 + 6144, "out_tile", [P, D])
        S4 = at(R4 + NODE, "split4", [P, 2, D], F32R)
        S8 = at(R4 + NODE + 4096, "split8", [P, 2, 2 * D], F32R)

        big = ctx.enter_context(nc.psum_tensor("banks", [P, 8, 512], F32))
        pb = [big[:, i, :] for i in range(8)]

        T_L1 = NT
        T_L2 = 2 * NT
        T_MLP1 = 3 * NT
        T_MLP2 = 4 * NT
        HT_MLP1 = NE * NT
        HT_MLP2 = (NE + 1) * NT
        F_L1 = NT
        F_GA = 2 * NT
        F_L2 = (2 + NE) * NT
        R_EX = NT
        R_L2 = (1 + NE) * NT
        R_MLP1 = (2 + NE) * NT
        R_MLP2 = (3 + NE) * NT
        A_L1 = NT
        A_EX = 2 * NT
        A_L2 = (2 + NE) * NT
        SC_L2 = NT
        W_L2 = 1
        W_EDGE = 2
        W_MLP = 3
        N_L1 = NT
        N_L2 = 2 * NT
        N_MLP1 = 3 * NT
        N_MLP2 = 4 * NT
        O_MLP1 = NT
        O_MLP2 = 2 * NT
        B_MLP1 = NT
        B_MLP2 = 2 * NT
        GEN_T = ET
        GEN_M = ET * 3 // 4
        GEN_U = ET - 1
        GEN_W = NT
        GEN_G = ET // 4
        GEN_EA = 16 * (ET // 8)
        GEN_GA = 16 * (ET // 8)

        s_x = sem("x_loaded")
        s_ed = sem("edges_loaded")
        s_w = sem("w_loaded")
        s_b0 = sem("bias0_loaded")
        s_cst = sem("constants")
        s_iota = sem("iota_int_ready")
        s_bnd = sem("bounds_ready")
        s_bndf = sem("bounds_f32_ready")
        s_dve = sem("dve_setup")
        s_viol = sem("violations_ready")
        s_vsum = sem("violations_summed")
        s_flag = sem("flag_ready")
        s_fence = sem("fence")
        s_oh = sem("onehots_ready")
        s_ohu = sem("onehots_used")
        s_win = sem("window_done")
        s_wev = sem("window_copied")
        s_tr = sem("adj_transposed")
        s_tra = sem("adj_copied_act")
        s_trv = sem("adj_copied_dve")
        s_deg = sem("degrees_ready")
        s_degp = sem("deg_src_plus1")
        s_onesr = sem("ones_r_ready")
        s_degm = sem("deg_src_row_summed")
        s_degr = sem("deg_src_row_ready")
        s_degc = sem("deg_src_columns")
        s_dis = sem("deg_inv_sqrt_ready")
        w_hi = sem("weights_hi")
        w_lo = sem("weights_split")
        s_idr = sem("identity_r_ready")
        rows_t = sem("node_rows_transposed")
        rows_hi = sem("rows_hi")
        rows_lo = sem("rows_split")
        lin1 = sem("first_linear_done")
        s_l0f = sem("l0_feat_ready")
        feat_hi = sem("features_hi")
        feat_lo = sem("features_ready")
        agg = sem("aggregated")
        s_l0r = sem("l0_resid_ready")
        n_stats = sem("norm_stats")
        n_var = sem("norm_var")
        n_eps = sem("norm_var_eps")
        n_rstd = sem("norm_rstd")
        x_ready = sem("layer_output_ready")
        s_be = sem("b_edge_loaded")
        s_we = sem("w_edge_loaded")
        s_io3 = sem("iota3_int")
        s_io3c = sem("iota3_ready")
        s_tab = sem("table_rows_ready")
        s_tst = [sem(f"table_stored_{i}") for i in range(2)]
        s_x3s = sem("x3_stored")
        s_w3 = sem("w3_loaded")
        s_w3l = sem("w3_last_ready")
        s_ea = [sem(f"edge_attr_loaded_{i}") for i in range(2)]
        s_eh = sem("edge_attr_hi")
        s_el = sem("edge_attr_ready")
        s_ix = sem("gather_index_ready")
        s_ga = [sem(f"gathered_{i}") for i in range(8)]
        s_em = sem("edge_embedded")
        s_z = sem("edge_z_ready")
        s_mh = sem("message_hi")
        s_ml = sem("message_ready")
        s_sc = sem("message_summed")
        s_w3d = sem("edge_window_done")
        s_w3e = sem("edge_window_copied")
        s_eps = sem("eps_loaded")
        s_ope = sem("one_plus_eps_ready")
        s_v1a = sem("vectors1_loaded")
        s_v1b = sem("beta1_loaded")
        s_v2a = sem("vectors2_first_loaded")
        s_v2b = sem("vectors2_last_loaded")
        s_xa = sem("x3_for_h0_loaded")
        s_xb = sem("x3_for_residual_loaded")
        n_xs = sem("x3_scaled")
        n_h0 = sem("h0_ready")
        n_y1b = sem("y1_biased")
        n_y1s = sem("y1_stats")
        n_y1v = sem("y1_var")
        n_y1e = sem("y1_var_eps")
        n_y1p = sem("y1_rstd")
        n_y1g = sem("y1_gamma")
        n_y1n = sem("y1_normed")
        n_y1 = sem("y1_gelu")
        gamma = sem("times_gamma")
        normed = sem("normed")
        n_y2 = sem("y2_gelu")
        res_add = sem("residual_added")
        n_rg = sem("residual_gamma")
        m_st = sem("out_tile_stored")
        s_spill = sem("x1_spilled")
        s_gw = sem("gate_loaded")
        s_gc = sem("gate_chain")
        s_gex = sem("gate_exp_ready")
        s_1x = sem("l1_xt_ready")
        s_1g = sem("l1_logits_done")
        agg_s = sem("aggregate_scaled")
        s_1b = sem("l1_agg_transposed")
        s_1c = sem("l1_at_ready")
        s_st = sem("expert_weights_loaded")
        s_ba = sem("expert_bias_first_loaded")
        s_bb = sem("expert_bias_second_loaded")
        s_w0h = sem("expert_w_first_hi")
        s_w0 = sem("expert_w_first_ready")
        s_w1h = sem("expert_w_second_hi")
        s_w1 = sem("expert_w_second_ready")
        hid_t = sem("hidden_rows_transposed")
        lin2 = sem("second_linear_done")
        s_h = sem("ex_h_ready")
        hid_hi = sem("hidden_hi")
        hid_lo = sem("hidden_split")
        s_r = sem("ex_r_ready")
        s_graw = sem("expert_g_copied")
        s_sth = sem("g_stored")
        s_str = sem("r_stored")
        s_x1 = sem("x1_reloaded")
        s_x1a = sem("x1_added")
        s_gin = [sem(f"g_loaded_{i}") for i in range(2)]
        s_rin = [sem(f"r_loaded_{i}") for i in range(5)]
        s_2t = sem("gather_scaled")
        s_2u = sem("gather_gated")
        s_2c = sem("gather_added")
        s_w2 = sem("w2_loaded")
        s_bc2 = sem("l2_vectors_loaded")
        biased = sem("linear_biased")
        s_3w = sem("l2_dve_steps")
        s_gate = sem("gate_weights_ready")
        o_stats = sem("outer_stats")
        o_var = sem("outer_var")
        o_eps = sem("outer_var_eps")
        o_rstd = sem("outer_rstd")

        block = ctx.enter_context(nc.Block())

        @block.sync
        def _(sp):
            sp.dma_start(DSTI[:], dst).then_inc(s_ed, 16)
            sp.dma_start(SRC[:], src).then_inc(s_ed, 16)
            sp.dma_start(X[:], x).then_inc(s_x, 16)
            sp.dma_start(STG[:], w0).then_inc(s_w, 16)
            sp.wait_ge(s_tr, 1)
            sp.dma_start(BC0[:], b0.partition_broadcast(P)).then_inc(s_b0, 16)
            sp.dma_start(GW[:], gate_w).then_inc(s_gw, 16)
            sp.dma_start(GBI[:], gate_b.partition_broadcast(P)).then_inc(s_gw, 16)
            for n in range(0, NT, 2):
                sp.wait_ge(x_ready, n + 2)
                sp.dma_start(X1D[:, n:n + 2, :], X[:, n:n + 2, :]).then_inc(s_spill, 16)
            for e in range(NE):
                if e == 0:
                    sp.wait_ge(s_spill, 16 * NT // 2)
                    sp.wait_ge(feat_lo, F_L1 + NT)
                    sp.wait_ge(rows_t, T_L1 + NT)
                else:
                    sp.wait_ge(s_w1, 2 * e)
                sp.dma_start(ST2[:], w1[e, 0]).then_inc(s_st, 16)
                if e >= 1:
                    sp.wait_ge(s_h, NT * e)
                    sp.dma_start(B1A[:], b1[e, 0].partition_broadcast(P)).then_inc(s_ba, 16)
                sp.wait_ge(s_w0, 2 * e + 2)
                sp.dma_start(ST2[:], w1[e, 1]).then_inc(s_st, 16)
                if e == 0:
                    sp.wait_ge(agg, A_L1 + NT)
                    sp.dma_start(B1A[:], b1[e, 0].partition_broadcast(P)).then_inc(s_ba, 16)
                need(sp, s_r, NT * e)
                sp.dma_start(B1B[:], b1[e, 1].partition_broadcast(P)).then_inc(s_bb, 16)
            def load_g(e):
                sp.wait_ge(s_sth, 16 * NT * (e + 1))
                for half in (0, 1):
                    ks = slice(half * NT // 2, (half + 1) * NT // 2)
                    need(sp, s_gin[half], 16 * e)
                    sp.dma_start((G2R, G1R)[e % 2][:, 1, ks], GD[:, e * NT + ks.start:e * NT + ks.stop, :]).then_inc(s_gin[half], 16)

            def load_r(m, slot):
                need(sp, s_2t, m - 4)
                sp.dma_start(RR[:, slot], RD[bass.ds(m, 1)].rearrange("a p f -> (a p) f")).then_inc(s_rin[slot], 16)

            sp.wait_ge(rows_lo, R_EX + NE * NT)
            load_g(0)
            sp.wait_ge(lin1, R_EX + NE * NT)
            sp.wait_ge(hid_t, NE * NT)
            for m in range(5):
                sp.wait_ge(s_str, 16 * (m + 1))
                load_r(m, m)
            sp.dma_start(X1R[:], X1D[:, :, :]).then_inc(s_x1, 16)
            sp.wait_ge(lin2, NE * NT)
            sp.wait_ge(hid_lo, NE * NT)
            sp.wait_ge(s_r, NE * NT)
            sp.wait_ge(s_str, 16 * NE * NT)
            load_g(1)
            for e in range(NE):
                for n in range(5 if e == 0 else 0, NT):
                    load_r(e * NT + n, n % 5)
                    if n == 0 and e == 1:
                        sp.wait_ge(s_x1a, NT)
                        sp.dma_start(WLR[:, :, 1], w2).then_inc(s_w2, 16)
                    if n == 5 and e in (1, 2):
                        sp.wait_ge(agg, A_EX + NT * e)
                        load_g(e + 1)
            sp.wait_ge(agg, A_EX + NE * NT)
            for i, row in enumerate((l2_bias, l2_gamma, l2_beta)):
                sp.dma_start(BC2[:, i], row.partition_broadcast(P)).then_inc(s_bc2, 16)

            sp.dma_start(BE[:], b_edge.partition_broadcast(P)).then_inc(s_be, 16)
            sp.dma_start(ope[:, 0:1], eps.partition_broadcast(P)).then_inc(s_eps, 16)
            sp.dma_start(WER[:, 1], w_edge).then_inc(s_we, 16)
            for n in range(NT):
                if n == NT - 1:
                    sp.wait_ge(lin1, R_L2 + NT)
                    for g in range(2):
                        sp.dma_start(EA[:, g], edge_attr[g]).then_inc(s_ea[g], 16)
                sp.wait_ge(x_ready, N_L2 + n + 1)
                sp.dma_start(X3D[n], X[:, n, :]).then_inc(s_x3s, 16)
                sp.wait_ge(s_tab, n + 1)
                sp.dma_start(TABD[n * P:(n + 1) * P, :], TAB[:, n % 2]).then_inc(s_tst[n % 2], 16)
            sp.wait_ge(s_x3s, 16 * NT)
            sp.dma_start(X3A[:], X3D[0]).then_inc(s_xa, 16)
            def load_attr(group, b):
                need(sp, s_el, group - 1)
                sp.dma_start(EA[:, b], edge_attr[bass.ds(group, 1)].rearrange("a p f -> (a p) f")).then_inc(s_ea[b], 16)

            def load_piece(q):
                need(sp, s_w3, 16 * q)
                sp.dma_start(W3R[:, bass.ds(q, 1)].rearrange("p a f -> p (a f)"),
                             w3[:, bass.ds(q, 1)].rearrange("p a f -> p (a f)")).then_inc(s_w3, 16)

            load_attr(2, 0)
            load_attr(3, 1)
            sp.wait_ge(s_io3c, 1)
            for i in range(4):
                load_attr(4 + i, i % 2)
                load_piece(i)
            with sp.Fori(2, 9) as k:
                for i in range(4):
                    load_attr(4 * k + i, i % 2)
                    load_piece(4 * (k - 1) + i)
            for group in range(36, ET // 4):
                load_attr(group, group % 2)
            sp.wait_ge(s_w3e, NT)
            general = sp.value_load(flag[0:1, 0:1], min_val=0, max_val=ET * P)
            with sp.If(general > ET * P - N_EDGES):
                with sp.Fori(0, NT) as d:
                    with sp.Fori(0, ET // 4) as g:
                        for i in range(4):
                            sp.wait_ge(s_sc, GEN_U + (d * (ET // 4) + g) * 4 + i)
                            sp.dma_start(EA[:, 0, 0:P], edge_attr[bass.ds(g, 1), :, i * P:(i + 1) * P].rearrange(
                                "a p f -> (a p) f")).then_inc(s_ea[0], 16)
                sp.wait_ge(s_w3e, GEN_W + NT)
                sp.nop()
            with sp.Else():
                sp.nop()
            sp.nop()
            for n in range(NT):
                if n >= 1:
                    sp.wait_ge(n_h0, n)
                    sp.dma_start(X3A[:], X3D[n]).then_inc(s_xa, 16)
                if n == 0:
                    for i in (0, 1):
                        sp.dma_start(V1A[:, i], v1[i].partition_broadcast(P)).then_inc(s_v1a, 16)
                    sp.dma_start(V1B[:], v1[2].partition_broadcast(P)).then_inc(s_v1b, 16)
                if n == 1:
                    for i in range(4):
                        sp.dma_start(V2A[:, i], v2[i].partition_broadcast(P)).then_inc(s_v2a, 16)
                    for i in range(3):
                        sp.dma_start(V2B[:, i], v2[4 + i].partition_broadcast(P)).then_inc(s_v2b, 16)
                if n >= 4:
                    sp.wait_ge(res_add, n - 4)
                    sp.dma_start(X3B[:], X3D[n - 4]).then_inc(s_xb, 16)
            for n in range(NT - 4, NT):
                sp.wait_ge(res_add, n)
                sp.dma_start(X3B[:], X3D[n]).then_inc(s_xb, 16)
            for n in range(NT):
                sp.wait_ge(res_add, NT)
                need(sp, res_add, n, B_MLP1)
                sp.dma_start(X3B[:], X3D[n]).then_inc(s_xb, 16)
                if n >= 1:
                    sp.wait_ge(x_ready, N_MLP2 + n)
                    sp.dma_start(out[:, n - 1, :], OUTB[:]).then_inc(m_st, 16)
            sp.wait_ge(x_ready, N_MLP2 + NT)
            sp.dma_start(out[:, NT - 1, :], OUTB[:]).then_inc(m_st, 16)
            sp.wait_ge(m_st, 16 * NT)

        @block.gpsimd
        def _(g):
            g.iota(IOTI[:], pattern=[[1, NP]], base=0, channel_multiplier=0).then_inc(s_iota, 1)
            g.memset(ident[:], 0.0).then_inc(s_cst, 1)
            g.memset(ones[:], 1.0).then_inc(s_cst, 1)
            g.memset(ZB[:], 0.0).then_inc(s_cst, 1)
            g.memset(cst[:, 0:1], EPS).then_inc(s_cst, 1)
            g.memset(cst[:, 1:2], -0.5).then_inc(s_cst, 1)
            g.memset(cst[:, 2:4], 1.0).then_inc(s_cst, 1)
            g.wait_ge(s_cst, 6)
            g.affine_select(out=ident[:], in_=ident[:], compare_op=ALU.not_equal, fill=1.0, base=0,
                            pattern=[[-1, P]], channel_multiplier=1).then_inc(s_cst, 1)
            g.wait_ge(s_dve, 1)
            L, H = BND[:, 0], BND[:, 1]
            g.iota(L[:, :, 0:MARGIN], pattern=[[P, NT], [0, MARGIN]], base=-P, channel_multiplier=0).then_inc(s_bnd, 1)
            g.iota(L[:, :, MARGIN:], pattern=[[P, NT], [0, EPW - MARGIN]], base=0, channel_multiplier=0).then_inc(s_bnd, 1)
            g.iota(H[:, :, 0:EPW - MARGIN], pattern=[[P, NT], [0, EPW - MARGIN]], base=P, channel_multiplier=0).then_inc(s_bnd, 1)
            g.iota(H[:, :, EPW - MARGIN:], pattern=[[P, NT], [0, MARGIN]], base=2 * P, channel_multiplier=0).then_inc(s_bnd, 1)
            g.wait_ge(s_degp, 1)
            g.tensor_tensor(dis[:], degs[:], cst[:, 1:2].to_broadcast([P, NT]), ALU.pow).then_inc(s_dis, 1)

            def rstd(n, b, since=0):
                need(g, n_var, n + 1, since)
                g.tensor_tensor(rst[:, b, 0:1], bmv[:, b, 1:2], cst[:, 0:1], ALU.add).then_inc(n_eps, 1)
                need(g, n_eps, n + 1, since)
                g.tensor_tensor(rst[:, b, 1:2], rst[:, b, 0:1], cst[:, 1:2], ALU.pow).then_inc(n_rstd, 1)

            def rstd_outer(n, b, since=0):
                need(g, o_var, n + 1, since)
                g.tensor_tensor(rst2[:, b, 0:1], bmv2[:, b, 1:2], cst[:, 0:1], ALU.add).then_inc(o_eps, 1)
                need(g, o_eps, n + 1, since)
                g.tensor_tensor(rst2[:, b, 1:2], rst2[:, b, 0:1], cst[:, 1:2], ALU.pow).then_inc(o_rstd, 1)
            tile_loop(g, rstd)

            with g.Fori(0, NE * NT) as m:
                g.wait_ge(s_graw, m + 1)
                g.dma_start(GD[:, bass.ds(m, 1), :].rearrange("p a f -> p (a f)"), GB[:]).then_inc(s_sth, 16)
                g.wait_ge(s_r, m + 1)
                g.dma_start(RD[bass.ds(m, 1)].rearrange("a p f -> (a p) f"), RB[:]).then_inc(s_str, 16)

            g.wait_ge(s_x1, 16)

            def x1_added(n, b):
                need(g, s_2u, n + 1)
                row = ACC[:, bass.ds(n, 1)].rearrange("p a f -> p (a f)")
                g.tensor_tensor(row, row, X1R[:, bass.ds(n, 1)].rearrange("p a f -> p (a f)"), ALU.add).then_inc(s_x1a, 1)
            tile_loop(g, x1_added)
            tile_loop(g, lambda n, b: rstd(n, b, N_L1))
            g.wait_ge(agg, A_EX + NE * NT)
            g.iota(IOT3[:], pattern=[[1, NP]], base=0, channel_multiplier=0).then_inc(s_io3, 1)

            def table(n):
                g.wait_ge(x_ready, N_L2 + n + 1)
                if n >= 2:
                    g.wait_ge(s_tst[n % 2], 16 * (n // 2))
                g.tensor_tensor(TAB[:, n % 2], X[:, n, :], BE[:], ALU.add).then_inc(s_tab, 1)

            g.wait_ge(s_be, 16)
            for n in range(NT + 2):
                if 1 <= n <= NT:
                    rstd_outer(n - 1, (n - 1) % 2)
                if n < NT:
                    rstd(n, n % 2, N_L2)
                if n >= 2:
                    table(n - 2)

            def attr_lo(i, b):
                need(g, s_eh, 2 * i + b + 1)
                g.tensor_tensor(EH[:, b, 1], EA[:, b], EH[:, b, 0].bitcast(F32), ALU.subtract).then_inc(s_el, 1)

            attr_lo(0, 0)
            g.wait_ge(s_tst[0], 16 * (NT // 2))
            g.wait_ge(s_tst[1], 16 * (NT // 2))

            def gathers(j):
                for r in range(2 * EPW):
                    t = 2 * EPW * j + r
                    need(g, s_z, t - 7)
                    at_ = r % 16
                    if r % 4 == 0:
                        g.sem_inc(s_fence, 1)
                        g.tensor_copy(IDXB[:, at_:at_ + 4], SRC[:, bass.ds(t, 4)]).then_inc(s_ix, 1)
                        need(g, s_ix, 8 * j + r // 4 + 1)
                    g.sem_inc(s_fence, 1)
                    g.indirect_dma_start(gathered(r), None, TABD[:, :],
                                         bass.IndirectOffsetOnAxis(ap=IDXB[:, at_:at_ + 1], axis=0)).then_inc(
                                             s_ga[r % 8], 16)
                    if r % 4 == 0 and not (isinstance(j, int) and j == 0 and r < 4):
                        attr_lo(4 * j + r // 8, (r // 4) % 2)
            window_loop(g, gathers)
            g.wait_ge(s_w3e, NT)
            general = g.value_load(flag[0:1, 0:1], min_val=0, max_val=ET * P)
            with g.If(general > ET * P - N_EDGES):
                with g.Fori(0, NT) as d:
                    with g.Fori(0, ET) as t:
                        g.wait_ge(s_sc, GEN_U + d * ET + t)
                        g.sem_inc(s_fence, 1)
                        g.tensor_copy(IDXB[:, 0:1], SRC[:, bass.ds(t, 1)]).then_inc(s_ix, 1)
                        g.wait_ge(s_ix, GEN_G + d * ET + t + 1)
                        g.sem_inc(s_fence, 1)
                        g.indirect_dma_start(GA[:, 0], None, TABD[:, :],
                                             bass.IndirectOffsetOnAxis(ap=IDXB[:, 0:1], axis=0)).then_inc(s_ga[0], 16)
                g.wait_ge(s_w3e, GEN_W + NT)
                g.nop()
            with g.Else():
                g.nop()
            g.nop()

            def rstd_wide(n):
                need(g, n_y1v, n + 1)
                g.tensor_tensor(rst1[:, 0:1], bmv1[:, 1:2], cst[:, 0:1], ALU.add).then_inc(n_y1e, 1)
                need(g, n_y1e, n + 1)
                g.tensor_tensor(rst1[:, 1:2], rst1[:, 0:1], cst[:, 1:2], ALU.pow).then_inc(n_y1p, 1)

            def h0(n):
                need(g, n_xs, n + 1)
                row = AGGR[:, bass.ds(n, 1)].rearrange("p a f -> p (a f)")
                g.tensor_tensor(row, X3A[:], row, ALU.add).then_inc(n_h0, 1)

            def last_w3_lo(q):
                need(g, w_hi, q + 1, W_MLP)
                row = lambda t: t[:, bass.ds(q, 1)].rearrange("p a f -> p (a f)")
                g.tensor_tensor(row(W3L), row(W3R), row(W3H).bitcast(F32), ALU.subtract).then_inc(s_w3l, 1)

            def add_x3(n):
                need(g, n_y2, n + 1)
                need(g, s_xb, 16 * (n + 1))
                need(g, x_ready, n, N_MLP1)
                g.tensor_tensor(Y2R[:], Y2B[:], X3B[:], ALU.add).then_inc(res_add, 1)

            def nodes(q, at):
                if at + 2 < NT:
                    h0(q + 2)
                if at < NT:
                    rstd_wide(q)
                if 3 <= at < NT + 3:
                    rstd_outer(q - 3, 0, O_MLP1)
                if at >= 2:
                    rstd(q - 2, 0, N_MLP1)
                if 2 <= at < NT + 2:
                    add_x3(q - 2)
                if at < NT - 2:
                    last_w3_lo(q + 24)
                if at >= NT + 2:
                    rstd_outer(q - 2, 0, O_MLP1)
            h0(0)
            h0(1)
            node_loop(g, nodes)

        @block.scalar
        def _(a):
            a.wait_ge(s_w, 16)
            nc.scalar.copy(W0H[:], STG[:]).then_inc(w_hi, 1)

            def windows(j):
                for b in (0, 1):
                    d = 2 * j + b
                    need(a, s_win, d + 1)
                    for c, w in ((0, 512), (1, 512), (2, 256)):
                        last = nc.scalar.copy(ADS[:, bass.ds(d, 1), 512 * c:512 * c + w].rearrange("p a f -> p (a f)"),
                                              pb[3 * b + c][:, 0:w])
                    last.then_inc(s_wev, 1)
            window_loop(a, windows)
            a.wait_ge(s_flag, 1)
            general = a.value_load(flag[0:1, 0:1], min_val=0, max_val=ET * P)
            with a.If(general > ET * P - N_EDGES):
                with a.Fori(0, NT) as d:
                    a.wait_ge(s_win, GEN_W + d + 1)
                    for c, w in ((0, 512), (1, 512), (2, 256)):
                        last = nc.scalar.copy(ADS[:, bass.ds(d, 1), 512 * c:512 * c + w].rearrange("p a f -> p (a f)"),
                                              pb[c][:, 0:w])
                    last.then_inc(s_wev, 1)
                a.nop()
            with a.Else():
                a.nop()
            a.nop()

            a.wait_ge(s_degm, 1)
            nc.scalar.copy(DROW[:], big[0:1, 3:6].rearrange("p a f -> p (a f)")[:, 0:NP]).then_inc(s_degr, 1)

            def transposed(n, b):
                need(a, s_tr, 3 * n + 1)
                nc.scalar.copy(ASD[:, 0:4, bass.ds(n * P, P)],
                               pb[3 * b].rearrange("p (k c) -> p k c", k=4)).then_inc(s_tra, 1)
            tile_loop(a, transposed)

            def l0(n, b):
                need(a, rows_t, n + 1)
                need(a, lin1, n - 1)
                nc.scalar.copy(XSP[:, b, 0, :], pb[6 + b]).then_inc(rows_hi, 1)
                if not (isinstance(n, int) and n == 0):
                    hi_of_feat(n - 1, 1 - b)

            def hi_of_feat(n, b):
                need(a, s_l0f, n + 1)
                nc.scalar.copy(G1H[:, bass.ds(n, 1), :].rearrange("p a f -> p (a f)"), FB[:, b, :]).then_inc(feat_hi, 1)
            tile_loop(a, l0)
            hi_of_feat(NT - 1, 1)

            a.wait_ge(agg, NT)
            def l1_x(n, b):
                need(a, x_ready, n + 1)
                nc.scalar.copy(G1H[:, bass.ds(n, 1), :].rearrange("p a f -> p (a f)"),
                               X[:, bass.ds(n, 1), :].rearrange("p a f -> p (a f)")).then_inc(feat_hi, 1)
                need(a, rows_t, n + 1, T_L1)
                nc.scalar.copy(XT[:, bass.ds(n, 1), :].rearrange("p a f -> p (a f)"), pb[b]).then_inc(s_1x, 1)
            tile_loop(a, l1_x)
            a.wait_ge(s_gc, 3)
            nc.scalar.activation(ex[:], lg[:], ACT.Exp).then_inc(s_gex, 1)

            def first_weights_hi(e):
                a.wait_ge(s_st, 32 * e + 16)
                a.wait_ge(lin1, R_EX + NT * e) if not isinstance(e, int) else need(a, lin1, NT * e, R_EX)
                for i in (0, 1):
                    nc.scalar.copy(WA[:, i, 0], ST2[:, i]).then_inc(s_w0h, 1)

            first_weights_hi(0)

            def l1_scaled(n, b):
                need(a, agg, n + 1, A_L1)
                need(a, s_1b, n - 1)
                nc.scalar.activation(AGB[:, b], pb[2 + b], ACT.Copy, scale=inv[:, bass.ds(n, 1)]).then_inc(agg_s, 1)
            tile_loop(a, l1_scaled)

            def second_weights_hi(e):
                a.wait_ge(s_st, 32 * e + 32)
                need(a, lin2, NT * e)
                for i in (0, 1):
                    nc.scalar.copy(WB[:, i, 0], ST2[:, i]).then_inc(s_w1h, 1)

            def xa_hi(m, n):
                need(a, lin1, m, R_EX)
                nc.scalar.copy(XA[:, 0, 0], XT[:, bass.ds(n, 1), :].rearrange("p a f -> p (a f)"))
                nc.scalar.copy(XA[:, 1, 0], AT[:, bass.ds(n, 1), :].rearrange("p a f -> p (a f)")).then_inc(rows_hi, 1)

            def hT_hi(m):
                need(a, hid_t, m + 1)
                nc.scalar.activation(HT[:, 0], pb[2], ACT.Relu).then_inc(hid_hi, 1)

            def g_hi(m):
                need(a, lin2, m + 1)
                need(a, s_sth, 16 * m)
                nc.scalar.copy(GB[:], pb[4]).then_inc(s_graw, 1)

            def expert(e, final):
                with a.Fori(1, NT - 1) as n:
                    m = e * NT + n
                    hT_hi(m - 1)
                    xa_hi(m + 1, n + 1)
                    g_hi(m - 1)
                m = e * NT + NT - 1
                hT_hi(m - 1)
                if not final:
                    xa_hi(m + 1, 0)
                    first_weights_hi(e + 1)
                g_hi(m - 1)
                if not final:
                    hT_hi(m)
                    xa_hi(m + 2, 1)
                    g_hi(m)
                    second_weights_hi(e + 1)

            def gather_hi(e, k):
                G, R = ((G2, G2R), (G1, G1R))[e % 2]
                if k % (NT // 2) == 0:
                    a.wait_ge(s_gin[2 * k // NT], 16 * (e + 1))
                nc.scalar.copy(G[:, 0, k], R[:, 1, k]).then_inc(feat_hi, 1)

            a.wait_ge(s_1c, NT)
            xa_hi(0, 0)
            a.wait_ge(agg, A_L1 + NT)
            second_weights_hi(0)
            xa_hi(1, 1)
            with a.Fori(0, NE - 1) as e:
                expert(e, False)
            expert(NE - 1, True)
            hT_hi(NE * NT - 1)
            for k in range(NT):
                gather_hi(0, k)
            g_hi(NE * NT - 1)

            def gated(m, e, n, b):
                need(a, s_2t, m + 1)
                g_of = gate[:, n:n + 1, e].rearrange("p a -> p a")
                if e == 0:
                    nc.scalar.activation(ACC[:, n], TU[:, 0, b], ACT.Relu, scale=g_of).then_inc(s_2u, 1)
                else:
                    need(a, s_2c, m - NT - 1)
                    nc.scalar.activation(TU[:, 1, b], TU[:, 0, b], ACT.Relu, scale=g_of).then_inc(s_2u, 1)

            def x2_hi(n):
                if n == 0:
                    a.wait_ge(agg, A_EX + (NE - 1) * NT)
                need(a, x_ready, n + 1, N_L1)
                nc.scalar.copy(G2[:, 0, n], X[:, n, :]).then_inc(feat_hi, 1)

            a.wait_ge(s_str, 16 * NE * NT)
            a.wait_ge(s_sth, 16 * NE * NT)
            for e in range(NE):
                if e == 2:
                    a.wait_ge(s_w2, 16)
                    nc.scalar.copy(WA[:, :, 0], WLR[:, :, 1]).then_inc(w_hi, 1)
                for n in range(NT):
                    if e + 1 < NE and n >= NT // 2:
                        gather_hi(e + 1, 2 * n - NT)
                        gather_hi(e + 1, 2 * n - NT + 1)
                    gated(e * NT + n, e, n, n % 2)
                    if e == NE - 1 and n >= 2:
                        x2_hi(n - 2)
            x2_hi(NT - 2)
            x2_hi(NT - 1)

            a.wait_ge(s_we, 16)
            nc.scalar.copy(WE[:, 0], WER[:, 1]).then_inc(w_hi, 1)

            def l2(n, b):
                need(a, agg, n + 1, A_L2)
                need(a, rows_t, n - 1, T_L2)
                nc.scalar.activation(AG2[:, b], pb[2 + b], ACT.Copy, scale=inv[:, bass.ds(n, 1)]).then_inc(agg_s, 1)
                need(a, rows_t, n + 1, T_L2)
                nc.scalar.copy(XA2[:, 0, 0], pb[0])
                nc.scalar.copy(XA2[:, 1, 0], pb[1]).then_inc(rows_hi, 1)
            tile_loop(a, l2)


            def attr_hi(i, b):
                a.wait_ge(s_ea[b], 16 * i + 16)
                need(a, s_em, 4 * (2 * i + b - 1))
                nc.scalar.copy(EH[:, b, 0], EA[:, b]).then_inc(s_eh, 1)

            def w3_hi(q):
                a.wait_ge(s_w3, 16 * (q + 1))
                nc.scalar.copy(W3H[:, bass.ds(q, 1)].rearrange("p k f -> p (k f)"),
                               W3R[:, bass.ds(q, 1)].rearrange("p k f -> p (k f)")).then_inc(w_hi, 1)

            def edges_hi(j):
                for r in range(2 * EPW):
                    t = 2 * EPW * j + r
                    need(a, s_z, t + 1)
                    need(a, s_sc, t - 1)
                    to = MSGF[:] if whole(r) else MSG[:, r % 2, 0]
                    nc.scalar.activation(to, ZB3[:, r % 2], ACT.Relu).then_inc(s_mh, 1)
                    if r % 4 == 3 and not (isinstance(j, int) and j == NT // 2 - 1 and r >= 2 * EPW - 5):
                        ahead = (r + 1) // 4 + 1
                        attr_hi(4 * j + ahead // 2, ahead % 2)
                    if r % 4 == 2 and not isinstance(j, int):
                        w3_hi(8 * (j - 1) + r // 4)
                    if r % EPW == MARGIN + 1 and not (isinstance(j, int) and j == 0 and r < EPW):
                        window_copy(2 * j + r // EPW - 1, (r // EPW + 1) % 2)

            def scaled_x3(n):
                need(a, s_xa, 16 * (n + 1))
                nc.scalar.activation(X3A[:], X3A[:], ACT.Copy, scale=ope[:, 1:2]).then_inc(n_xs, 1)

            def window_copy(d, b):
                need(a, s_w3d, d + 1)
                nc.scalar.copy(AGGR[:, bass.ds(d, 1)].rearrange("p a f -> p (a f)"), pb[4 + b]).then_inc(s_w3e, 1)
            a.wait_ge(lin1, R_L2 + NT)
            attr_hi(0, 0)
            attr_hi(0, 1)
            a.wait_ge(s_tab, NT)
            window_loop(a, edges_hi)
            window_copy(NT - 1, 1)
            a.wait_ge(s_ope, 1)
            scaled_x3(0)
            general = a.value_load(flag[0:1, 0:1], min_val=0, max_val=ET * P)
            with a.If(general > ET * P - N_EDGES):
                with a.Fori(0, NT) as d:
                    with a.Fori(0, ET) as t:
                        a.wait_ge(s_ea[0], GEN_EA + (d * ET + t) * 16 + 16)
                        nc.scalar.copy(EH[:, 0, 0, 0:P], EA[:, 0, 0:P]).then_inc(s_eh, 1)
                        a.wait_ge(s_z, GEN_T + d * ET + t + 1)
                        nc.scalar.activation(MSG[:, 0, 0], ZB3[:, 0], ACT.Relu).then_inc(s_mh, 1)
                    a.wait_ge(s_w3d, GEN_W + d + 1)
                    nc.scalar.copy(AGGR[:, bass.ds(d, 1)].rearrange("p a f -> p (a f)"), pb[4]).then_inc(s_w3e, 1)
                a.nop()
            with a.Else():
                a.nop()
            a.nop()

            def s4_hi(n):
                need(a, rows_t, n + 1, T_MLP1)
                nc.scalar.copy(S4[:, 0], pb[0]).then_inc(rows_hi, 1)

            def s8_hi(n):
                need(a, hid_t, n + 1, HT_MLP1)
                need(a, lin2, n, HT_MLP1)
                nc.scalar.copy(S8[:, 0], big[:, 1:3].rearrange("p a f -> p (a f)")).then_inc(hid_hi, 1)

            def nodes(q, at):
                if at + 1 < 2 * NT:
                    s4_hi(q + 1)
                if at + 2 < NT:
                    scaled_x3(q + 2)
                if NT <= at < 2 * NT:
                    need(a, lin1, q + 1, R_MLP1)
                    need(a, hid_t, q, HT_MLP1)
                    nc.scalar.activation(Y1[:], big[:, 3:5].rearrange("p a f -> p (a f)"), ACT.Gelu).then_inc(n_y1, 1)
                if 1 <= at <= 2 * NT:
                    s8_hi(q - 1)
                if at < NT:
                    need(a, n_y1n, q + 1)
                    nc.scalar.activation(Y1[:], Y1[:], ACT.Gelu).then_inc(n_y1, 1)
                if at < NT - 2:
                    w3_hi(q + 24)
                if 2 <= at < NT + 2:
                    need(a, normed, q - 1)
                    nc.scalar.activation(Y2B[:], Y2B[:], ACT.Gelu).then_inc(n_y2, 1)
            s4_hi(0)
            scaled_x3(1)
            node_loop(a, nodes)

        @block.vector
        def _(v):
            v.wait_ge(s_iota, 1)
            nc.vector.tensor_copy(IOTA[:], IOTI[:]).then_inc(s_dve, 1)
            v.wait_ge(s_ed, 32)
            nc.vector.tensor_copy(DST[:], DSTI[:]).then_inc(s_dve, 1)
            nc.vector.tensor_copy(SRCF[:], SRC[:]).then_inc(s_dve, 1)
            v.wait_ge(s_bnd, 4)
            nc.vector.tensor_copy(BNF[:], BND[:].rearrange("p a d t -> p a (d t)")).then_inc(s_bndf, 1)
            v.wait_ge(s_bndf, 1)
            v.wait_ge(s_dve, 3)
            nc.vector.tensor_tensor(VIO[:, 0, :], DST[:], BNF[:, 0, :], ALU.is_lt)
            nc.vector.tensor_tensor(VIO[:, 1, :], DST[:], BNF[:, 1, :], ALU.is_ge).then_inc(s_dve, 1)
            v.wait_ge(s_dve, 4)
            nc.vector.tensor_reduce(VSM[:, 0:1], VIO[:], axis=AX.XY, op=ALU.add).then_inc(s_viol, 1)

            def onehots(j):
                for r in range(2 * EPW):
                    t = 2 * EPW * j + r
                    need(v, s_ohu, t - 3)
                    nc.vector.tensor_scalar(OHS[:, r % 4, :], IOTA[:], SRCF[:, bass.ds(t, 1)], None, ALU.is_equal)
                    ws = shifts(j, r)
                    last = nc.vector.tensor_scalar(OHD[:, r % 4, 0:len(ws)].rearrange("p a f -> p (a f)"),
                                                   IOTA[:, bass.ds((2 * j + ws[0]) * P, len(ws) * P)],
                                                   DST[:, bass.ds(t, 1)], None, ALU.is_equal)
                    last.then_inc(s_oh, 1)
            window_loop(v, onehots)

            v.wait_ge(s_w, 16)
            v.wait_ge(w_hi, 1)
            nc.vector.tensor_tensor(W0L[:], STG[:], W0H[:].bitcast(F32), ALU.subtract).then_inc(w_lo, 1)
            v.wait_ge(s_cst, 7)
            nc.vector.tensor_copy(identr[:], ident[:]).then_inc(s_idr, 1)
            nc.vector.tensor_copy(onesr[:], ones[:]).then_inc(s_onesr, 1)
            v.wait_ge(s_vsum, 1)
            nc.vector.tensor_copy(flag[0:1, 0:1], pb[7][0:1, 0:1]).then_inc(s_flag, 1)
            v.wait_ge(s_flag, 1)
            general = v.value_load(flag[0:1, 0:1], min_val=0, max_val=ET * P)
            with v.If(general > ET * P - N_EDGES):
                v.wait_ge(s_win, NT)
                with v.Fori(0, NT) as d:
                    with v.Fori(0, ET) as t:
                        v.wait_ge(s_ohu, GEN_U + d * ET + t)
                        nc.vector.tensor_scalar(OHS[:, 0, :], IOTA[:], SRCF[:, bass.ds(t, 1)], None, ALU.is_equal)
                        nc.vector.tensor_scalar(OHD[:, 0, 0, :], IOTA[:, bass.ds(d * P, P)], DST[:, bass.ds(t, 1)],
                                                None, ALU.is_equal).then_inc(s_oh, 1)
                v.nop()
            with v.Else():
                v.nop()
            v.nop()

            def transposed(n, b):
                need(v, s_tr, 3 * n + 3)
                nc.vector.tensor_copy(ASD[:, 4:8, bass.ds(n * P, P)],
                                      pb[3 * b + 1].rearrange("p (k c) -> p k c", k=4))
                nc.vector.tensor_copy(ASD[:, 8:10, bass.ds(n * P, P)],
                                      pb[3 * b + 2][:, 0:256].rearrange("p (k c) -> p k c", k=2)).then_inc(s_trv, 1)
            tile_loop(v, transposed)
            v.wait_ge(s_degc, 1)
            nc.vector.tensor_scalar(degs[:], pb[7][:, 0:NT], 1.0, None, ALU.add).then_inc(s_degp, 1)
            v.wait_ge(s_b0, 16)

            def l0(n, b):
                need(v, rows_hi, n + 1)
                nc.vector.tensor_tensor(XSP[:, b, 1, :], pb[6 + b], XSP[:, b, 0, :].bitcast(F32),
                                        ALU.subtract).then_inc(rows_lo, 1)
                if not (isinstance(n, int) and n == 0):
                    feat(n - 1, 1 - b)

            def feat(n, b):
                need(v, lin1, n + 1)
                need(v, feat_lo, n - 1)
                nc.vector.tensor_tensor(TB[:, b, :], pb[2 + b], BC0[:], ALU.add).then_inc(s_l0r, 1)
                need(v, s_l0r, n + 1)
                if isinstance(n, int) and n == 0:
                    v.wait_ge(s_dis, 1)
                nc.vector.tensor_scalar(FB[:, b, :], TB[:, b, :], dis[:, bass.ds(n, 1)], None,
                                        ALU.mult).then_inc(s_l0f, 1)
                need(v, feat_hi, n + 1)
                nc.vector.tensor_tensor(G1L[:, bass.ds(n, 1), :].rearrange("p a f -> p (a f)"), FB[:, b, :],
                                        G1H[:, bass.ds(n, 1), :].rearrange("p a f -> p (a f)").bitcast(F32),
                                        ALU.subtract).then_inc(feat_lo, 1)
            tile_loop(v, l0)
            feat(NT - 1, 1)

            def resid(n, b):
                need(v, agg, n + 1)
                xn = X[:, bass.ds(n, 1), :].rearrange("p a f -> p (a f)")
                need(v, x_ready, n - 1)
                nc.vector.scalar_tensor_tensor(TB[:, b, :], pb[4 + b], dis[:, bass.ds(n, 1)], xn,
                                               ALU.mult, ALU.add).then_inc(s_l0r, 1)
                need(v, s_l0r, NT + n + 1)
                nc.vector.bn_stats(bst[:, b, 0, :], TB[:, b, :]).then_inc(n_stats, 1)
                need(v, n_stats, n + 1)
                v.sem_inc(s_fence, 1)
                nc.vector.bn_aggr(bmv[:, b, :], bst[:, b, 0, :]).then_inc(n_var, 1)
                nc.vector.tensor_reduce(degd[:, bass.ds(n, 1)], ADS[:, bass.ds(n, 1)].bitcast(F32), axis=AX.X,
                                        op=ALU.add).then_inc(s_deg, 1)
                if not (isinstance(n, int) and n == 0):
                    norm(n - 1, 1 - b)

            def norm(n, b):
                xn = X[:, bass.ds(n, 1), :].rearrange("p a f -> p (a f)")
                need(v, n_rstd, n + 1)
                nc.vector.tensor_scalar(xn, TB[:, b, :], bmv[:, b, 0:1], rst[:, b, 1:2], ALU.subtract,
                                        ALU.mult).then_inc(x_ready, 1)
            tile_loop(v, resid)
            norm(NT - 1, 1)

            v.wait_ge(s_deg, NT)
            nc.vector.tensor_scalar(degd[:], degd[:], 1.0, None, ALU.max).then_inc(s_deg, 1)
            v.wait_ge(s_deg, NT + 1)
            nc.vector.reciprocal(inv[:], degd[:]).then_inc(s_deg, 1)

            v.wait_ge(agg, NT)
            v.wait_ge(x_ready, NT)
            def x1_lo(n, b):
                need(v, feat_hi, n + 1, F_L1)
                nc.vector.tensor_tensor(G1L[:, bass.ds(n, 1), :].rearrange("p a f -> p (a f)"),
                                        X[:, bass.ds(n, 1), :].rearrange("p a f -> p (a f)"),
                                        G1H[:, bass.ds(n, 1), :].rearrange("p a f -> p (a f)").bitcast(F32),
                                        ALU.subtract).then_inc(feat_lo, 1)
            tile_loop(v, x1_lo)

            v.wait_ge(s_gw, 32)
            v.wait_ge(s_1g, NT)
            v.wait_ge(s_1x, NT)
            wide = [P, NT, NE]
            nc.vector.tensor_tensor(lg[:], pb[7][:, 0:NT * NE].rearrange("p (n e) -> p n e", e=NE),
                                    GBI[:].unsqueeze(1).to_broadcast(wide), ALU.add).then_inc(s_gc, 1)
            v.wait_ge(s_gc, 1)
            nc.vector.tensor_reduce(gm[:, 0], lg[:], axis=AX.X, op=ALU.max).then_inc(s_gc, 1)
            v.wait_ge(s_gc, 2)
            nc.vector.tensor_tensor(lg[:], lg[:], gm[:, 0].unsqueeze(2).to_broadcast(wide), ALU.subtract).then_inc(s_gc, 1)
            v.wait_ge(s_gex, 1)
            nc.vector.tensor_reduce(gm[:, 0], ex[:], axis=AX.X, op=ALU.add).then_inc(s_gc, 1)
            v.wait_ge(s_gc, 4)
            nc.vector.reciprocal(gm[:, 1], gm[:, 0]).then_inc(s_gc, 1)
            v.wait_ge(s_gc, 5)
            nc.vector.tensor_tensor(gv[:], ex[:], gm[:, 1].unsqueeze(2).to_broadcast(wide), ALU.mult).then_inc(s_gc, 1)
            v.wait_ge(s_gc, 6)
            steps = 6
            nc.vector.memset(lg[:], 0.0).then_inc(s_gc, 1)
            steps += 1
            for e in range(NE):
                for j in range(NE):
                    if j == e:
                        continue
                    v.wait_ge(s_gc, steps)
                    nc.vector.tensor_tensor(ex[:, :, 0:1], gv[:, :, j:j + 1], gv[:, :, e:e + 1],
                                            ALU.is_ge if j < e else ALU.is_gt).then_inc(s_gc, 1)
                    v.wait_ge(s_gc, steps + 1)
                    nc.vector.tensor_tensor(lg[:, :, e:e + 1], lg[:, :, e:e + 1], ex[:, :, 0:1], ALU.add).then_inc(s_gc, 1)
                    steps += 2
            v.wait_ge(s_gc, steps)
            nc.vector.scalar_tensor_tensor(gate[:], lg[:], 1.5, gv[:], ALU.is_lt, ALU.mult).then_inc(s_gate, 1)

            def first_weights_lo(e):
                for i in (0, 1):
                    v.wait_ge(s_w0h, 2 * e + i + 1)
                    nc.vector.tensor_tensor(WA[:, i, 1], ST2[:, i], WA[:, i, 0].bitcast(F32), ALU.subtract).then_inc(s_w0, 1)

            first_weights_lo(0)

            def l1_at(n, b):
                need(v, s_1b, n + 1)
                nc.vector.tensor_copy(AT[:, bass.ds(n, 1), :].rearrange("p a f -> p (a f)"), pb[4 + b]).then_inc(s_1c, 1)
            tile_loop(v, l1_at)

            def second_weights_lo(e):
                for i in (0, 1):
                    v.wait_ge(s_w1h, 2 * e + i + 1)
                    nc.vector.tensor_tensor(WB[:, i, 1], ST2[:, i], WB[:, i, 0].bitcast(F32), ALU.subtract).then_inc(s_w1, 1)

            def xa_lo(m, n):
                need(v, rows_hi, m + 1, R_EX)
                nc.vector.tensor_tensor(XA[:, 0, 1], XT[:, bass.ds(n, 1), :].rearrange("p a f -> p (a f)"),
                                        XA[:, 0, 0].bitcast(F32), ALU.subtract)
                nc.vector.tensor_tensor(XA[:, 1, 1], AT[:, bass.ds(n, 1), :].rearrange("p a f -> p (a f)"),
                                        XA[:, 1, 0].bitcast(F32), ALU.subtract).then_inc(rows_lo, 1)

            def hT_lo(m):
                need(v, hid_hi, m + 1)
                nc.vector.scalar_tensor_tensor(HT[:, 1], pb[2], 0.0, HT[:, 0].bitcast(F32), ALU.max,
                                               ALU.subtract).then_inc(hid_lo, 1)

            def h_biased(m):
                need(v, lin1, m + 1, R_EX)
                need(v, hid_t, m)
                nc.vector.tensor_tensor(HB[:], pb[0], B1A[:], ALU.add).then_inc(s_h, 1)

            def g_lo_and_r(m):
                need(v, lin2, m + 1)
                need(v, s_str, 16 * m)
                nc.vector.tensor_tensor(RB[:], pb[5], B1B[:], ALU.add).then_inc(s_r, 1)

            def expert(e, final):
                with v.Fori(1, NT - 1) as n:
                    m = e * NT + n
                    hT_lo(m - 1)
                    h_biased(m)
                    xa_lo(m + 1, n + 1)
                    g_lo_and_r(m - 1)
                m = e * NT + NT - 1
                hT_lo(m - 1)
                h_biased(m)
                if not final:
                    xa_lo(m + 1, 0)
                    first_weights_lo(e + 1)
                g_lo_and_r(m - 1)
                if not final:
                    hT_lo(m)
                    v.wait_ge(s_ba, 16 * (e + 2))
                    h_biased(m + 1)
                    xa_lo(m + 2, 1)
                    g_lo_and_r(m)
                    second_weights_lo(e + 1)
                    v.wait_ge(s_bb, 16 * (e + 2))

            def gather_lo(e, k):
                G, R = ((G2, G2R), (G1, G1R))[e % 2]
                v.wait_ge(feat_hi, F_GA + e * NT + k + 1)
                nc.vector.tensor_tensor(G[:, 1, k], R[:, 1, k], G[:, 0, k].bitcast(F32), ALU.subtract).then_inc(feat_lo, 1)

            xa_lo(0, 0)
            second_weights_lo(0)
            v.wait_ge(s_ba, 16)
            v.wait_ge(s_bb, 16)
            h_biased(0)
            xa_lo(1, 1)
            with v.Fori(0, NE - 1) as e:
                expert(e, False)
            expert(NE - 1, True)
            hT_lo(NE * NT - 1)
            for k in range(NT):
                gather_lo(0, k)
            g_lo_and_r(NE * NT - 1)

            def scaled(m, e, n, b):
                need(v, agg, m + 1, A_EX)
                need(v, s_2u, m - 1)
                k = (0 if isinstance(n, int) and n < 5 else 1)
                nc.vector.scalar_tensor_tensor(TU[:, 0, b], pb[b], inv[:, n:n + 1], RR[:, n % 5], ALU.mult,
                                               ALU.add).then_inc(s_2t, 1)

            def added(m, n, b):
                v.wait_ge(s_2u, m + 1)
                if m < 2 * NT:
                    v.wait_ge(s_x1a, n + 1)
                else:
                    v.wait_ge(s_2c, m - 2 * NT + 1)
                nc.vector.tensor_tensor(ACC[:, n, :], ACC[:, n, :], TU[:, 1, b], ALU.add).then_inc(s_2c, 1)

            def x1_stats(n):
                b = n % 2
                v.wait_ge(s_2c, (NE - 2) * NT + n + 1)
                nc.vector.bn_stats(bst[:, b, 0, :], ACC[:, n, :]).then_inc(n_stats, 1)
                v.wait_ge(n_stats, N_L1 + n + 1)
                nc.vector.bn_aggr(bmv[:, b, :], bst[:, b, 0, :]).then_inc(n_var, 1)

            def x2_norm(n):
                b = n % 2
                v.wait_ge(n_rstd, N_L1 + n + 1)
                nc.vector.tensor_scalar(X[:, n, :], ACC[:, n, :], bmv[:, b, 0:1], rst[:, b, 1:2], ALU.subtract,
                                        ALU.mult).then_inc(x_ready, 1)

            def x2_lo(n):
                v.wait_ge(feat_hi, F_L2 + n + 1)
                nc.vector.tensor_tensor(G2[:, 1, n], X[:, n, :], G2[:, 0, n].bitcast(F32), ALU.subtract).then_inc(feat_lo, 1)
            for e in range(NE):
                if e == 2:
                    v.wait_ge(w_hi, W_L2 + 1)
                    nc.vector.tensor_tensor(WA[:, :, 1], WLR[:, :, 1], WA[:, :, 0].bitcast(F32),
                                            ALU.subtract).then_inc(w_lo, 1)
                for n in range(NT):
                    m = e * NT + n
                    v.wait_ge(s_rin[n % 5], 16 * (2 * e + n // 5 + 1))
                    scaled(m, e, n, n % 2)
                    if e + 1 < NE and n >= NT // 2:
                        gather_lo(e + 1, 2 * n - NT)
                        gather_lo(e + 1, 2 * n - NT + 1)
                    if m > NT:
                        added(m - 1, (n - 1) % NT, (n - 1) % 2)
                    if e == NE - 1 and n >= 1:
                        x1_stats(n - 1)
                    if e == NE - 1 and n >= 2:
                        x2_norm(n - 2)
                    if e == NE - 1 and n >= 3:
                        x2_lo(n - 3)

            added(NE * NT - 1, NT - 1, 1)
            x1_stats(NT - 1)
            x2_norm(NT - 2)
            x2_lo(NT - 3)
            x2_norm(NT - 1)
            x2_lo(NT - 2)
            x2_lo(NT - 1)

            v.wait_ge(s_eps, 16)
            nc.vector.tensor_scalar(ope[:, 1:2], ope[:, 0:1], 1.0, None, ALU.add).then_inc(s_ope, 1)
            v.wait_ge(s_io3, 1)
            nc.vector.tensor_copy(IOTA[:], IOT3[:]).then_inc(s_io3c, 1)
            v.wait_ge(w_hi, W_EDGE + 1)
            nc.vector.tensor_tensor(WE[:, 1], WER[:, 1], WE[:, 0].bitcast(F32), ALU.subtract).then_inc(w_lo, 1)

            v.wait_ge(s_bc2, 48)

            def l2_split(n, b):
                need(v, rows_hi, n + 1, R_L2)
                nc.vector.tensor_tensor(XA2[:, 0, 1], pb[0], XA2[:, 0, 0].bitcast(F32), ALU.subtract)
                nc.vector.tensor_tensor(XA2[:, 1, 1], pb[1], XA2[:, 1, 0].bitcast(F32), ALU.subtract).then_inc(rows_lo, 1)
                if not (isinstance(n, int) and n == 0):
                    l2_bias_stats(n - 1, 1 - b)
                if not (isinstance(n, int) and n < 2):
                    l2_norm(n - 2, b)
                if not (isinstance(n, int) and n == 0):
                    l2_affine(n - 1, 1 - b)

            def l2_bias_stats(n, b):
                need(v, lin1, n + 1, R_L2)
                nc.vector.tensor_tensor(Y2[:, b], pb[4 + b], BC2[:, 0], ALU.add).then_inc(biased, 1)
                need(v, biased, n + 1)
                nc.vector.bn_stats(bst[:, b, 0, :], Y2[:, b]).then_inc(n_stats, 1)
                need(v, n_stats, n + 1, N_L2)
                v.sem_inc(s_fence, 1)
                nc.vector.bn_aggr(bmv[:, b, :], bst[:, b, 0, :]).then_inc(n_var, 1)

            def l2_affine(n, b):
                xn = X[:, bass.ds(n, 1), :].rearrange("p a f -> p (a f)")
                need(v, n_rstd, n + 1, N_L2)
                nc.vector.scalar_tensor_tensor(Z2[:, b], Y2[:, b], bmv[:, b, 0:1], BC2[:, 1], ALU.subtract,
                                               ALU.mult).then_inc(s_3w, 1)
                need(v, s_3w, 3 * n + 1)
                nc.vector.scalar_tensor_tensor(Z2[:, b], Z2[:, b], rst[:, b, 1:2], BC2[:, 2], ALU.mult,
                                               ALU.add).then_inc(s_3w, 1)
                need(v, s_3w, 3 * n + 2)
                nc.vector.tensor_tensor(Z2[:, b], Z2[:, b], xn, ALU.add).then_inc(s_3w, 1)
                need(v, s_3w, 3 * n + 3)
                nc.vector.bn_stats(bst[:, b, 1, :], Z2[:, b]).then_inc(o_stats, 1)
                need(v, o_stats, n + 1)
                v.sem_inc(s_fence, 1)
                nc.vector.bn_aggr(bmv2[:, b, :], bst[:, b, 1, :]).then_inc(o_var, 1)

            def l2_norm(n, b):
                xn = X[:, bass.ds(n, 1), :].rearrange("p a f -> p (a f)")
                need(v, o_rstd, n + 1)
                nc.vector.tensor_scalar(xn, Z2[:, b], bmv2[:, b, 0:1], rst2[:, b, 1:2], ALU.subtract,
                                        ALU.mult).then_inc(x_ready, 1)
            tile_loop(v, l2_split)
            l2_bias_stats(NT - 1, 1)
            l2_norm(NT - 2, 0)
            l2_affine(NT - 1, 1)
            l2_norm(NT - 1, 1)

            v.wait_ge(s_io3c, 1)
            v.wait_ge(s_x3s, 16 * NT)
            v.wait_ge(s_tab, NT)

            def w3_lo(q):
                need(v, w_hi, q + 1, W_MLP)
                flat = lambda ap: ap.rearrange("p k f -> p (k f)")
                nc.vector.tensor_tensor(flat(W3L[:, bass.ds(q, 1)]), flat(W3R[:, bass.ds(q, 1)]),
                                        flat(W3H[:, bass.ds(q, 1)]).bitcast(F32), ALU.subtract).then_inc(w_lo, 1)

            def message_lo(t, b):
                need(v, s_mh, t + 1)
                nc.vector.scalar_tensor_tensor(MSG[:, b, 1], ZB3[:, b], 0.0, MSG[:, b, 0].bitcast(F32), ALU.max,
                                               ALU.subtract).then_inc(s_ml, 1)

            def edges_lo(j):
                for r in range(2 * EPW):
                    t = 2 * EPW * j + r
                    need(v, s_sc, t - 3)
                    ws = shifts(j, r)
                    nc.vector.tensor_scalar(OH3[:, r % 4, 0:len(ws)].rearrange("p a f -> p (a f)"),
                                            IOTA[:, bass.ds((2 * j + ws[0]) * P, len(ws) * P)], DST[:, bass.ds(t, 1)],
                                            None, ALU.is_equal)
                    v.wait_ge(s_ga[r % 8], 16 * (4 * j + r // 8 + 1))
                    need(v, s_em, t + 1)
                    if whole(r - 2):
                        need(v, s_mh, t - 1)
                    else:
                        need(v, s_ml, splits(j, r - 2))
                    nc.vector.tensor_tensor(ZB3[:, r % 2], pb[r % 4], gathered(r), ALU.add).then_inc(s_z, 1)
                    if not (isinstance(j, int) and t == 0) and not whole(r - 1):
                        message_lo(t - 1, (r + 1) % 2)
                    if r % 4 == 3 and not isinstance(j, int):
                        w3_lo(8 * (j - 1) + r // 4)
            window_loop(v, edges_lo)
            message_lo(ET - 1, 1)

            v.wait_ge(s_w3e, NT)
            general = v.value_load(flag[0:1, 0:1], min_val=0, max_val=ET * P)
            with v.If(general > ET * P - N_EDGES):
                with v.Fori(0, NT) as d:
                    with v.Fori(0, ET) as t:
                        v.wait_ge(s_eh, GEN_G + d * ET + t + 1)
                        nc.vector.tensor_tensor(EH[:, 0, 1, 0:P], EA[:, 0, 0:P], EH[:, 0, 0, 0:P].bitcast(F32),
                                                ALU.subtract)
                        nc.vector.tensor_scalar(OH3[:, 0, 0], IOTA[:, bass.ds(d * P, P)], DST[:, bass.ds(t, 1)], None,
                                                ALU.is_equal).then_inc(s_el, 1)
                        v.wait_ge(s_ga[0], GEN_GA + (d * ET + t) * 16 + 16)
                        v.wait_ge(s_em, GEN_T + d * ET + t + 1)
                        nc.vector.tensor_tensor(ZB3[:, 0], pb[0], GA[:, 0], ALU.add).then_inc(s_z, 1)
                        v.wait_ge(s_mh, GEN_T + d * ET + t + 1)
                        nc.vector.scalar_tensor_tensor(MSG[:, 0, 1], ZB3[:, 0], 0.0, MSG[:, 0, 0].bitcast(F32), ALU.max,
                                                       ALU.subtract).then_inc(s_ml, 1)
                v.wait_ge(s_w3e, GEN_W + NT)
                v.nop()
            with v.Else():
                v.nop()
            v.nop()

            def tile_of(t, n):
                return t[:, bass.ds(n, 1)].rearrange("p a f -> p (a f)")

            def s4_lo(n):
                need(v, rows_hi, n + 1, R_MLP1)
                nc.vector.tensor_tensor(S4[:, 1], pb[0], S4[:, 0].bitcast(F32), ALU.subtract).then_inc(rows_lo, 1)

            def s8_lo(n):
                need(v, hid_hi, n + 1, HT_MLP1)
                nc.vector.tensor_tensor(S8[:, 1], big[:, 1:3].rearrange("p a f -> p (a f)"), S8[:, 0].bitcast(F32),
                                        ALU.subtract).then_inc(hid_lo, 1)

            def y1_bias(n):
                need(v, lin1, n + 1, R_MLP1)
                need(v, hid_t, n, HT_MLP1)
                nc.vector.tensor_tensor(Y1[:], big[:, 3:5].rearrange("p a f -> p (a f)"), V1A[:, 0], ALU.add).then_inc(n_y1b, 1)

            def y1_stats(n):
                need(v, n_y1b, n + 1)
                nc.vector.bn_stats(bst1[:, 0, :], Y1[:, 0:D])
                nc.vector.bn_stats(bst1[:, 1, :], Y1[:, D:]).then_inc(n_y1s, 1)
                need(v, n_y1s, n + 1)
                v.sem_inc(s_fence, 1)
                nc.vector.bn_aggr(bmv1[:], bst1[:].rearrange("p a f -> p (a f)")).then_inc(n_y1v, 1)

            def y1_norm(n):
                need(v, n_y1p, n + 1)
                nc.vector.scalar_tensor_tensor(Y1[:], Y1[:], bmv1[:, 0:1], V1A[:, 1], ALU.subtract,
                                               ALU.mult).then_inc(n_y1g, 1)
                need(v, n_y1g, n + 1)
                nc.vector.scalar_tensor_tensor(Y1[:], Y1[:], rst1[:, 1:2], V1B[:], ALU.mult,
                                               ALU.add).then_inc(n_y1n, 1)

            def own_stats(i):
                need(v, biased, i + 1, B_MLP1)
                nc.vector.bn_stats(bst[:, 0, 0, :], Y2B[:]).then_inc(n_stats, 1)
                need(v, n_stats, i + 1, N_MLP1)
                v.sem_inc(s_fence, 1)
                nc.vector.bn_aggr(bmv[:, 0, :], bst[:, 0, 0, :]).then_inc(n_var, 1)

            def outer_stats(i, row):
                need(v, res_add, i + 1)
                nc.vector.bn_stats(bst[:, 0, 1, :], row).then_inc(o_stats, 1)
                need(v, o_stats, i + 1, O_MLP1)
                v.sem_inc(s_fence, 1)
                nc.vector.bn_aggr(bmv2[:, 0, :], bst[:, 0, 1, :]).then_inc(o_var, 1)

            def affine(i, gamma_row, beta_row):
                need(v, n_rstd, i + 1, N_MLP1)
                nc.vector.scalar_tensor_tensor(Y2B[:], Y2B[:], bmv[:, 0, 0:1], gamma_row, ALU.subtract,
                                               ALU.mult).then_inc(gamma, 1)
                need(v, gamma, i + 1)
                nc.vector.scalar_tensor_tensor(Y2B[:], Y2B[:], rst[:, 0, 1:2], beta_row, ALU.mult,
                                               ALU.add).then_inc(normed, 1)

            def y2_stats(n):
                need(v, lin2, n + 1, HT_MLP1)
                need(v, res_add, n)
                nc.vector.tensor_tensor(Y2B[:], pb[5], V2A[:, 0], ALU.add).then_inc(biased, 1)
                own_stats(n)

            def h4(n):
                need(v, o_rstd, n + 1, O_MLP1)
                nc.vector.scalar_tensor_tensor(Y2R[:], Y2R[:], bmv2[:, 0, 0:1], V2A[:, 3], ALU.subtract,
                                               ALU.mult).then_inc(n_rg, 1)
                need(v, n_rg, n + 1)
                nc.vector.scalar_tensor_tensor(tile_of(AGGR, n), Y2R[:], rst2[:, 0, 1:2], V2B[:, 0], ALU.mult,
                                               ALU.add).then_inc(x_ready, 1)

            def y_stats(i):
                need(v, lin2, i + 1, HT_MLP1)
                if not (isinstance(i, int) and i == NT):
                    need(v, x_ready, i, N_MLP1)
                nc.vector.tensor_tensor(Y2B[:], pb[5], tile_of(AGGR, i - NT), ALU.add).then_inc(biased, 1)
                own_stats(i)

            def y_out(i):
                affine(i, V2B[:, 1], V2B[:, 2])
                need(v, normed, i + 1)
                need(v, s_xb, 16 * (i + 1))
                nc.vector.tensor_tensor(Y2B[:], Y2B[:], X3B[:], ALU.add).then_inc(res_add, 1)
                outer_stats(i, Y2B[:])
                need(v, o_rstd, i + 1, O_MLP1)
                need(v, m_st, 16 * (i - NT))
                nc.vector.tensor_scalar(OUTB[:], Y2B[:], bmv2[:, 0, 0:1], rst2[:, 0, 1:2], ALU.subtract,
                                        ALU.mult).then_inc(x_ready, 1)

            def nodes(q, at):
                if at < NT:
                    y1_bias(q)
                if at + 1 < 2 * NT:
                    s4_lo(q + 1)
                if at < NT:
                    y1_stats(q)
                if 3 <= at < NT + 3:
                    outer_stats(q - 3, Y2R[:])
                if at == 2:
                    v.wait_ge(s_v2a, 64)
                    v.wait_ge(s_v2b, 48)
                if 2 <= at < NT + 2:
                    y2_stats(q - 2)
                if at >= NT + 2:
                    y_stats(q - 2)
                if 1 <= at <= 2 * NT:
                    s8_lo(q - 1)
                if at < NT:
                    y1_norm(q)
                if 3 <= at < NT + 3:
                    h4(q - 3)
                if 2 <= at < NT + 2:
                    affine(q - 2, V2A[:, 1], V2A[:, 2])
                if at >= NT + 2:
                    y_out(q - 2)
            s4_lo(0)
            v.wait_ge(s_v1a, 32)
            v.wait_ge(s_v1b, 16)
            node_loop(v, nodes)

        @block.tensor
        def _(pe):
            pe.wait_ge(s_cst, 7)
            pe.wait_ge(s_viol, 1)
            nc.tensor.matmul(pb[7][0:1, 0:1], ones[:, 0:1], VSM[:, 0:1], start=True, stop=True).then_inc(s_vsum, 1)

            def windows(j):
                for r in range(2 * EPW):
                    t = 2 * EPW * j + r
                    need(pe, s_oh, t + 1)
                    for i, s in enumerate(shifts(j, r)):
                        first, final = opens(j, r, s), closes(j, r, s)
                        if first:
                            need(pe, s_wev, 2 * j + s - 1)
                        for c, w in ((0, 512), (1, 512), (2, 256)):
                            last = nc.tensor.matmul(pb[3 * (s % 2) + c][:, 0:w], OHD[:, r % 4, i, :],
                                                    OHS[:, r % 4, 512 * c:512 * c + w], start=first, stop=final)
                        if final:
                            last.then_inc(s_win, 1)
                    if not final:
                        last.then_inc(s_ohu, 1)
            window_loop(pe, windows)

            pe.wait_ge(s_flag, 1)
            pe.wait_ge(s_wev, NT)
            general = pe.value_load(flag[0:1, 0:1], min_val=0, max_val=ET * P)
            with pe.If(general > ET * P - N_EDGES):
                with pe.Fori(0, NT) as d:
                    pe.wait_ge(s_wev, GEN_W + d)
                    for c, w in ((0, 512), (1, 512), (2, 256)):
                        nc.tensor.matmul(pb[c][:, 0:w], ZB[:], IOTA[:, 512 * c:512 * c + w], start=True, stop=False)
                    with pe.Fori(0, ET) as t:
                        pe.wait_ge(s_oh, GEN_T + d * ET + t + 1)
                        for c, w in ((0, 512), (1, 512), (2, 256)):
                            last = nc.tensor.matmul(pb[c][:, 0:w], OHD[:, 0, 0, :], OHS[:, 0, 512 * c:512 * c + w],
                                                    start=False, stop=False)
                        last.then_inc(s_ohu, 1)
                    for c, w in ((0, 512), (1, 512), (2, 256)):
                        last = nc.tensor.matmul(pb[c][:, 0:w], ZB[:], IOTA[:, 512 * c:512 * c + w], start=False, stop=True)
                    last.then_inc(s_win, 1)
                pe.wait_ge(s_wev, GEN_W + NT)
                pe.nop()
            with pe.Else():
                pe.nop()
            pe.nop()

            pe.wait_ge(s_onesr, 1)
            for c, w in ((0, 512), (1, 512), (2, 256)):
                for d in range(NT):
                    last = nc.tensor.matmul(pb[3 + c][0:2, 0:w], onesr[:], ADS[:, d, 512 * c:512 * c + w],
                                            start=d == 0, stop=d == NT - 1)
            last.then_inc(s_degm, 1)
            for d in range(NT):
                if d == 1:
                    pe.wait_ge(s_degr, 1)
                if d >= 2:
                    pe.wait_ge(s_tra, d - 1)
                    pe.wait_ge(s_trv, d - 1)
                for k in range(NT):
                    last = nc.tensor.transpose(pb[3 * (d % 2) + k // 4][:, P * (k % 4):P * (k % 4 + 1)],
                                               ADS[:, d, k * P:(k + 1) * P].bitcast(F32), ident[:])
                    if k in (3, 7, 9):
                        last.then_inc(s_tr, 1)

            def l0_transpose(n):
                if n == 0:
                    pe.wait_ge(s_x, 16)
                if n >= 2:
                    pe.wait_ge(rows_lo, n - 1)
                for k in range(KT):
                    last = nc.tensor.transpose(pb[6 + n % 2][:, P * k:P * (k + 1)], X[:, n, k * P:(k + 1) * P], ident[:])
                last.then_inc(rows_t, 1)

            for k in range(NT):
                last = nc.tensor.matmul(pb[7][:, k:k + 1], DROW[0:1, k * P:(k + 1) * P], ones[0:1, 0:1], start=True, stop=True)
            last.then_inc(s_degc, 1)
            l0_transpose(0)
            pe.wait_ge(s_degp, 1)
            l0_transpose(1)
            pe.wait_ge(s_tra, NT)
            pe.wait_ge(s_trv, NT)
            for n in range(NT):
                if 1 <= n < NT - 1:
                    l0_transpose(n + 1)
                b = n % 2
                if n == 0:
                    pe.wait_ge(w_lo, 1)
                pe.wait_ge(rows_lo, n + 1)
                if n >= 2:
                    pe.wait_ge(s_l0f, n - 1)
                for k in range(KT):
                    xh, xl = XSP[:, b, 0, k * P:(k + 1) * P], XSP[:, b, 1, k * P:(k + 1) * P]
                    nc.tensor.matmul(pb[2 + b], xh, W0H[:, k, :], start=k == 0, stop=False)
                    nc.tensor.matmul(pb[2 + b], xh, W0L[:, k, :], start=False, stop=False)
                    last = nc.tensor.matmul(pb[2 + b], xl, W0H[:, k, :], start=False, stop=k == KT - 1)
                last.then_inc(lin1, 1)

            pe.wait_ge(s_idr, 1)
            for n in range(NT):
                b = 4 + n % 2
                if n >= 2:
                    pe.wait_ge(s_l0r, NT + n - 1)
                for k in range(NT):
                    if n == 0:
                        pe.wait_ge(feat_lo, k + 1)
                    for g in (G1H, G1L):
                        nc.tensor.matmul(pb[b], ADS[:, k, n * P:(n + 1) * P], g[:, k, :], start=k == 0 and g is G1H,
                                         stop=False)
                nc.tensor.matmul(pb[b], identr[:], G1H[:, n, :], start=False, stop=False)
                nc.tensor.matmul(pb[b], identr[:], G1L[:, n, :], start=False, stop=True).then_inc(agg, 1)

            pe.wait_ge(s_gw, 32)
            for n in range(NT):
                pe.wait_ge(x_ready, n + 1)
                if n >= 2:
                    pe.wait_ge(s_1x, n - 1)
                for k in range(KT):
                    last = nc.tensor.transpose(pb[n % 2][:, P * k:P * (k + 1)], X[:, n, k * P:(k + 1) * P], ident[:])
                last.then_inc(rows_t, 1)
            for n in range(NT):
                pe.wait_ge(s_1x, n + 1)
                for k in range(KT):
                    last = nc.tensor.matmul(pb[7][:, n * NE:(n + 1) * NE], XT[:, n, k * P:(k + 1) * P], GW[:, k, :],
                                            start=k == 0, stop=k == KT - 1)
                last.then_inc(s_1g, 1)

            def l1_agg_transpose(n):
                pe.wait_ge(agg_s, n + 1)
                if n >= 2:
                    pe.wait_ge(s_1c, n - 1)
                for k in range(KT):
                    last = nc.tensor.transpose(pb[4 + n % 2][:, P * k:P * (k + 1)], AGB[:, n % 2, k * P:(k + 1) * P], ident[:])
                last.then_inc(s_1b, 1)

            for n in range(NT):
                if n >= 2:
                    pe.wait_ge(agg_s, n - 1)
                for k in range(NT):
                    if n == 0:
                        pe.wait_ge(feat_lo, F_L1 + k + 1)
                    for g in (G1H, G1L):
                        last = nc.tensor.matmul(pb[2 + n % 2], ASD[:, k, n * P:(n + 1) * P], g[:, k, :],
                                                start=k == 0 and g is G1H, stop=k == NT - 1 and g is G1L)
                last.then_inc(agg, 1)
                if n >= 1:
                    l1_agg_transpose(n - 1)
            l1_agg_transpose(NT - 1)

            def split_product(out, xh, xl, w, start, stop):
                wh, wl = w
                for k in range(KT):
                    c = slice(k * P, (k + 1) * P)
                    nc.tensor.matmul(out, xh[:, c], wh[:, k, :], start=start and k == 0, stop=False)
                    nc.tensor.matmul(out, xh[:, c], wl[:, k, :], start=False, stop=False)
                    last = nc.tensor.matmul(out, xl[:, c], wh[:, k, :], start=False, stop=stop and k == KT - 1)
                return last

            def first_layer(m, new=None):
                need(pe, rows_lo, m + 1, R_EX)
                if new is not None:
                    pe.wait_ge(s_w0, 2 * new + 1)
                split_product(pb[0], XA[:, 0, 0], XA[:, 0, 1], (WA[:, 0, 0], WA[:, 0, 1]), True, False)
                if new is not None:
                    pe.wait_ge(s_w0, 2 * new + 2)
                split_product(pb[0], XA[:, 1, 0], XA[:, 1, 1], (WA[:, 1, 0], WA[:, 1, 1]), False, True).then_inc(lin1, 1)

            def transpose_h(m):
                need(pe, s_h, m + 1)
                for k in range(KT):
                    last = nc.tensor.transpose(pb[2][:, P * k:P * (k + 1)], HB[:, k * P:(k + 1) * P], ident[:])
                last.then_inc(hid_t, 1)

            def second_layer(m, new=None):
                need(pe, hid_lo, m + 1)
                need(pe, s_r, m)
                if m is not None:
                    need(pe, s_graw, m)
                if new is not None:
                    pe.wait_ge(s_w1, 2 * new + 1)
                split_product(pb[4], HT[:, 0], HT[:, 1], (WB[:, 0, 0], WB[:, 0, 1]), True, True)
                if new is not None:
                    pe.wait_ge(s_w1, 2 * new + 2)
                split_product(pb[5], HT[:, 0], HT[:, 1], (WB[:, 1, 0], WB[:, 1, 1]), True, True).then_inc(lin2, 1)

            def expert(e, final):
                m = e * NT + 1
                transpose_h(m - 1)
                first_layer(m)
                second_layer(m - 1, e)
                with pe.Fori(2, NT) as n:
                    transpose_h(e * NT + n - 1)
                    first_layer(e * NT + n)
                    second_layer(e * NT + n - 1)
                if not final:
                    m = e * NT + NT
                    transpose_h(m - 1)
                    first_layer(m, e + 1)
                    second_layer(m - 1)

            first_layer(0, 0)
            with pe.Fori(0, NE - 1) as e:
                expert(e, False)
            expert(NE - 1, True)
            transpose_h(NE * NT - 1)
            second_layer(NE * NT - 1)

            for e in range(NE):
                G = (G2, G1)[e % 2]
                for n in range(NT):
                    m = e * NT + n
                    need(pe, s_2t, m - 1)
                    for k in range(NT):
                        if n == 0:
                            pe.wait_ge(feat_lo, F_GA + e * NT + k + 1)
                        for half in (0, 1):
                            last = nc.tensor.matmul(pb[m % 2], ASD[:, k, n * P:(n + 1) * P], G[:, half, k],
                                                    start=k == 0 and half == 0, stop=k == NT - 1 and half == 1)
                    last.then_inc(agg, 1)

            def l2_transpose(n):
                pe.wait_ge(agg_s, SC_L2 + n + 1)
                if n >= 1:
                    pe.wait_ge(rows_lo, R_L2 + n)
                for k in range(KT):
                    nc.tensor.transpose(pb[0][:, P * k:P * (k + 1)], X[:, n, k * P:(k + 1) * P], ident[:])
                for k in range(KT):
                    last = nc.tensor.transpose(pb[1][:, P * k:P * (k + 1)], AG2[:, n % 2, k * P:(k + 1) * P], ident[:])
                last.then_inc(rows_t, 1)

            def l2_linear(n):
                pe.wait_ge(rows_lo, R_L2 + n + 1)
                if n >= 2:
                    pe.wait_ge(biased, n - 1)
                split_product(pb[4 + n % 2], XA2[:, 0, 0], XA2[:, 0, 1], (WA[:, 0, 0], WA[:, 0, 1]), True, False)
                split_product(pb[4 + n % 2], XA2[:, 1, 0], XA2[:, 1, 1], (WA[:, 1, 0], WA[:, 1, 1]), False, True).then_inc(lin1, 1)

            pe.wait_ge(s_2t, NE * NT)
            pe.wait_ge(w_lo, W_L2 + 1)
            for n in range(NT):
                if n >= 1:
                    l2_transpose(n - 1)
                if n >= 2:
                    pe.wait_ge(agg_s, SC_L2 + n - 1)
                for k in range(NT):
                    if n == 0:
                        pe.wait_ge(feat_lo, F_L2 + k + 1)
                    for half in (0, 1):
                        last = nc.tensor.matmul(pb[2 + n % 2], ASD[:, k, n * P:(n + 1) * P], G2[:, half, k],
                                                start=k == 0 and half == 0, stop=k == NT - 1 and half == 1)
                last.then_inc(agg, 1)
                if n >= 1:
                    l2_linear(n - 1)
            l2_transpose(NT - 1)
            l2_linear(NT - 1)

            def scatter(j):
                for r in range(2 * EPW):
                    t = 2 * EPW * j + r
                    if not (isinstance(j, int) and t + AHEAD >= ET):
                        embed_at(j, r + AHEAD)
                    if whole(r):
                        need(pe, s_mh, t + 1)
                    else:
                        need(pe, s_ml, splits(j, r))
                    for i, w in enumerate(shifts(j, r)):
                        first, final = opens(j, r, w), closes(j, r, w)
                        if first:
                            need(pe, s_w3e, 2 * j + w - 1)
                        if whole(r):
                            last = nc.tensor.matmul(pb[4 + w % 2], OH3[:, r % 4, i].bitcast(F32),
                                                    MSGF[:], start=first, stop=final)
                        else:
                            nc.tensor.matmul(pb[4 + w % 2], OH3[:, r % 4, i], MSG[:, r % 2, 0], start=first, stop=False)
                            last = nc.tensor.matmul(pb[4 + w % 2], OH3[:, r % 4, i], MSG[:, r % 2, 1], start=False,
                                                    stop=final)
                        if final:
                            last.then_inc(s_w3d, 1)
                    if not final:
                        last.then_inc(s_sc, 1)

            def embed_at(j, r):
                t = 2 * EPW * j + r
                if r % 4 == 0:
                    need(pe, s_el, 8 * j + r // 4 + 1)
                need(pe, s_z, t - 3)
                b, c = (r // 4) % 2, slice((r % 4) * P, (r % 4 + 1) * P)
                nc.tensor.matmul(pb[r % 4], EH[:, b, 0, c], WE[:, 0], start=True, stop=False)
                nc.tensor.matmul(pb[r % 4], EH[:, b, 0, c], WE[:, 1], start=False, stop=False)
                nc.tensor.matmul(pb[r % 4], EH[:, b, 1, c], WE[:, 0], start=False, stop=True).then_inc(s_em, 1)

            pe.wait_ge(w_lo, W_EDGE + 1)
            pe.wait_ge(biased, NT)
            for r in range(AHEAD):
                embed_at(0, r)
            window_loop(pe, scatter)

            pe.wait_ge(s_w3e, NT)
            general = pe.value_load(flag[0:1, 0:1], min_val=0, max_val=ET * P)
            with pe.If(general > ET * P - N_EDGES):
                with pe.Fori(0, NT) as d:
                    pe.wait_ge(s_w3e, GEN_W + d)
                    nc.tensor.matmul(pb[4], ZB[:], IOTA[:, 0:512], start=True, stop=False)
                    with pe.Fori(0, ET) as t:
                        pe.wait_ge(s_el, GEN_G + d * ET + t + 1)
                        nc.tensor.matmul(pb[0], EH[:, 0, 0, 0:P], WE[:, 0], start=True, stop=False)
                        nc.tensor.matmul(pb[0], EH[:, 0, 0, 0:P], WE[:, 1], start=False, stop=False)
                        nc.tensor.matmul(pb[0], EH[:, 0, 1, 0:P], WE[:, 0], start=False, stop=True).then_inc(s_em, 1)
                        pe.wait_ge(s_ml, GEN_M + d * ET + t + 1)
                        nc.tensor.matmul(pb[4], OH3[:, 0, 0], MSG[:, 0, 0], start=False, stop=False)
                        nc.tensor.matmul(pb[4], OH3[:, 0, 0], MSG[:, 0, 1], start=False, stop=False).then_inc(s_sc, 1)
                    nc.tensor.matmul(pb[4], ZB[:], IOTA[:, 0:512], start=False, stop=True).then_inc(s_w3d, 1)
                pe.wait_ge(s_w3e, GEN_W + NT)
                pe.nop()
            with pe.Else():
                pe.nop()
            pe.nop()

            def matrix(q):
                return W3H[:, q * KT:(q + 1) * KT], W3L[:, q * KT:(q + 1) * KT]

            def up_product(first_matrix):
                split_product(pb[3], S4[:, 0], S4[:, 1], matrix(first_matrix), True, True)
                return split_product(pb[4], S4[:, 0], S4[:, 1], matrix(first_matrix + 1), True, True)

            def down_product(half, first_matrix):
                x = slice(half * D, (half + 1) * D)
                return split_product(pb[5], S8[:, 0, x], S8[:, 1, x], matrix(first_matrix + half), half == 0, half == 1)

            def transpose_row(n, done):
                for k in range(KT):
                    last = nc.tensor.transpose(pb[0][:, P * k:P * (k + 1)], AGGR[:, n, k * P:(k + 1) * P], ident[:])
                last.then_inc(done, 1)

            def transpose_wide(done):
                for k in range(2 * KT):
                    last = nc.tensor.transpose(pb[1 + k // KT][:, P * (k % KT):P * (k % KT + 1)],
                                               Y1[:, k * P:(k + 1) * P], ident[:])
                last.then_inc(done, 1)

            pe.wait_ge(w_lo, W_MLP + 6 * KT)
            pe.wait_ge(n_h0, 1)
            transpose_row(0, rows_t)
            for q in range(2 * NT + 2):
                if q < 2 * NT:
                    pe.wait_ge(rows_lo, R_MLP1 + q + 1)
                    if 1 <= q <= NT:
                        pe.wait_ge(n_y1b, q)
                    if q > NT:
                        pe.wait_ge(n_y1, q)
                    up_product(0 if q < NT else 4).then_inc(lin1, 1)
                if q + 1 < NT:
                    pe.wait_ge(n_h0, q + 2)
                    transpose_row(q + 1, rows_t)
                elif q + 1 < 2 * NT:
                    pe.wait_ge(x_ready, N_MLP1 + q + 2 - NT)
                    transpose_row(q + 1 - NT, rows_t)
                if q >= 2:
                    pe.wait_ge(hid_lo, HT_MLP1 + q - 1)
                    if q == NT + 2:
                        pe.wait_ge(s_w3l, 2 * KT)
                    if q >= 3:
                        pe.wait_ge(biased, B_MLP1 + q - 2)
                    down_product(0, 2 if q < NT + 2 else 6)
                if 1 <= q <= 2 * NT:
                    pe.wait_ge(n_y1, q)
                    transpose_wide(hid_t)
                if q >= 2:
                    down_product(1, 2 if q < NT + 2 else 6).then_inc(lin2, 1)


_INS = ["x", "src", "dst", "w0", "b0", "gate_w", "gate_b", "w1", "b1", "w2", "l2_bias", "l2_gamma", "l2_beta",
        "edge_attr", "w_edge", "b_edge", "eps", "w3", "v1", "v2"]


def kernel(**inputs):
    import numpy as _np
    import concourse.bacc as _bacc
    from concourse import mybir as _mybir
    from concourse.bass_utils import run_bass_kernel_spmd as _run

    def edges(a, fill):
        padded = _np.full(ET * P, fill, _np.int32)
        padded[:N_EDGES] = a
        return _np.ascontiguousarray(padded.reshape(ET, P).T)

    def matrix(w):
        return _np.ascontiguousarray(w.reshape(KT, P, D).transpose(1, 0, 2))

    wl, wr = _np.asarray(inputs["L1_gnn_Wl"]), _np.asarray(inputs["L1_gnn_Wr"])
    w1 = _np.stack([_np.stack([_np.stack([matrix(wr[e, 0]), matrix(wl[e, 0])], axis=1),
                               _np.stack([matrix(wl[e, 1]), matrix(wr[e, 1])], axis=1)]) for e in range(NE)])
    w3 = []
    for up, down in (("L3_gnn_W1", "L3_gnn_W2"), ("L3_gnn_M1", "L3_gnn_M2")):
        u, d = _np.asarray(inputs[up]), _np.asarray(inputs[down])
        w3 += [matrix(u[:, :D]), matrix(u[:, D:]), matrix(d[:D]), matrix(d[D:])]
    w3 = _np.stack(w3, axis=1)
    attr = _np.zeros((ET * P, P), _np.float32)
    attr[:N_EDGES] = inputs["edge_attr_128"]
    xp = _np.zeros((NP, D), _np.float32)
    xp[:N_NODES] = inputs["x"]
    data = {
        "x": _np.ascontiguousarray(xp.reshape(NT, P, D).transpose(1, 0, 2)),
        "src": edges(_np.asarray(inputs["src"]), 0), "dst": edges(_np.asarray(inputs["dst"]), NO_NODE),
        "w0": matrix(_np.asarray(inputs["L0_gnn_W"]).T), "b0": _np.asarray(inputs["L0_gnn_b"]),
        "gate_w": _np.asarray(inputs["L1_gnn_gate_W"]).reshape(KT, P, NE).transpose(1, 0, 2),
        "gate_b": _np.asarray(inputs["L1_gnn_gate_b"]),
        "w1": w1, "b1": _np.asarray(inputs["L1_gnn_bl"]),
        "w2": _np.stack([matrix(_np.asarray(inputs["L2_gnn_W_self"]).T),
                         matrix(_np.asarray(inputs["L2_gnn_W_neigh"]).T)], axis=1),
        "l2_bias": _np.asarray(inputs["L2_gnn_bias"]), "l2_gamma": _np.asarray(inputs["L2_gnn_gamma"]),
        "l2_beta": _np.asarray(inputs["L2_gnn_beta"]),
        "edge_attr": _np.ascontiguousarray(attr.reshape(ET // 4, 4 * P, P).transpose(0, 2, 1)),
        "w_edge": _np.asarray(inputs["L3_gnn_W_edge"]), "b_edge": _np.asarray(inputs["L3_gnn_b_edge"]),
        "eps": _np.asarray(inputs["L3_gnn_eps"]).reshape(1), "w3": w3.reshape(P, 8 * KT, D),
        "v1": _np.stack([_np.asarray(inputs["L3_gnn_" + n]) for n in ("b1", "g1", "be1")]),
        "v2": _np.stack([_np.asarray(inputs["L3_gnn_" + n]) for n in ("b2", "g2", "be2", "gA", "bA", "gB", "bB")]),
    }
    nc = _bacc.Bacc("TRN2", target_bir_lowering=False, num_devices=1)
    arrays, args = {}, []
    for name in _INS:
        a = _np.ascontiguousarray(data[name])
        arrays[f"in_{name}_dram"] = a
        args.append(nc.dram_tensor(f"in_{name}_dram", a.shape, _mybir.dt.from_np(a.dtype), kind="ExternalInput").ap())
    out = nc.dram_tensor("out_dram", (P, NT, D), _mybir.dt.float32, kind="ExternalOutput").ap()
    build(nc, *args, out)
    r = _run(nc, [arrays], core_ids=[0])
    y = r.results[0]["out_dram"]
    return _np.ascontiguousarray(y.transpose(1, 0, 2).reshape(NP, D)[:N_NODES])
```

```python
import numpy as np
import concourse.bass as bass
from concourse import mybir
from contextlib import ExitStack

F32 = mybir.dt.float32
F32R = mybir.dt.float32r
F16 = mybir.dt.float16
BF16 = mybir.dt.bfloat16
I32 = mybir.dt.int32
ALU = mybir.AluOpType
ACT = mybir.ActivationFunctionType
AX = mybir.AxisListType

P = 128
N_NODES = 1250
NT = 10
NP = NT * P
N_EDGES = 20000
ET = 160
EPW = ET // NT
MARGIN = 2
NO_NODE = 4096
D = 512
KT = D // P
NE = 4
AHEAD = 3
EPS = 1e-5


def shifts(j, r):
    own, at = divmod(r, EPW)
    ws = [own]
    if at < MARGIN and not (isinstance(j, int) and 2 * j + own == 0):
        ws.insert(0, own - 1)
    if at >= EPW - MARGIN and not (isinstance(j, int) and 2 * j + own == NT - 1):
        ws.append(own + 1)
    return ws


def opens(j, r, s):
    if isinstance(j, int) and 2 * j + s == 0:
        return r == 0
    return r == EPW * s - MARGIN


def closes(j, r, s):
    if isinstance(j, int) and 2 * j + s == NT - 1:
        return r == 2 * EPW - 1
    return r == EPW * (s + 1) + MARGIN - 1


def whole(r):
    return r % 4 == 1


def splits(j, r):
    return 2 * EPW * 3 // 4 * j + (sum(not whole(i) for i in range(r + 1)) if r >= -1 else -1)


def need(eng, sem, value, since=0):
    if isinstance(value, int) and value <= 0:
        return
    eng.wait_ge(sem, since + value)


def tile_loop(eng, step):
    for n in (0, 1):
        step(n, n)
    with eng.Fori(1, NT // 2 - 1) as i:
        step(2 * i, 0)
        step(2 * i + 1, 1)
    for n in (NT - 2, NT - 1):
        step(n, n % 2)


def node_loop(eng, step):
    for q in range(3):
        step(q, q)
    with eng.Fori(3, NT - 2) as q:
        step(q, 3)
    for q in range(NT - 2, NT + 3):
        step(q, q)
    with eng.Fori(NT + 3, 2 * NT - 1) as q:
        step(q, NT + 3)
    for q in range(2 * NT - 1, 2 * NT + 2):
        step(q, q)


def window_loop(eng, step):
    step(0)
    with eng.Fori(1, NT // 2 - 1) as j:
        step(j)
    step(NT // 2 - 1)


def build(nc, x, src, dst, w0, b0, gate_w, gate_b, w1, b1, w2, l2_bias, l2_gamma, l2_beta,
          edge_attr, w_edge, b_edge, eps, w3, v1, v2, out):
    ctx = ExitStack()
    with ctx:
        base = (nc.sbuf_base + 63) // 64 * 64
        assert nc.sbuf_usable_end - base >= 212800

        def at(offset, name, shape, dt=F32):
            return nc.alloc_sbuf_tensor_at(name, shape, dt, offset=base + offset)

        def sem(name):
            return ctx.enter_context(nc.semaphore(name))

        MAT = KT * D * 4
        NODE = NT * D * 4
        ADJ = NT * NP * 4
        ADJ_AT, ADJ2_AT = 0, ADJ
        G_AT = ADJ2_AT + ADJ
        X_AT = G_AT + 2 * NODE
        W_AT = X_AT + NODE
        SMALL_AT = W_AT + 4 * MAT
        adj_src_dst = at(ADJ_AT, "adj_src_dst", [P, NT, NP], F32R)
        adj_dst_src = at(ADJ2_AT, "adj_dst_src", [P, NT, NP], F32R)
        g1_hi = at(G_AT, "g1_hi", [P, NT, D], F32R)
        g1_lo = at(G_AT + NODE, "g1_lo", [P, NT, D], F32R)
        onehot_src = at(G_AT, "onehot_src", [P, 4, NP], BF16)
        onehot_dst = at(G_AT + 4 * NP * 2, "onehot_dst", [P, 4, 2, P], BF16)
        x_nodes = at(X_AT, "x_nodes", [P, NT, D])
        w0_hi = at(W_AT, "w0_hi", [P, KT, D], F32R)
        w0_lo = at(W_AT + MAT, "w0_lo", [P, KT, D], F32R)
        w_stage = at(W_AT + 2 * MAT, "w_stage", [P, KT, D])
        feat_rows = at(W_AT + 3 * MAT, "feat", [P, 2, D])
        resid_rows = at(W_AT + 3 * MAT + 4096, "resid", [P, 2, D])
        small = [SMALL_AT]

        def keep(name, shape, dt=F32):
            nbytes = int(np.prod(shape[1:])) * (2 if dt in (F16, BF16) else 4)
            t = at(small[0], name, shape, dt)
            small[0] += (nbytes + 31) // 32 * 32
            assert small[0] <= 212800, small[0]
            return t

        src_index = keep("src_index", [P, ET], I32)
        dst_f32 = keep("dst_f32", [P, ET])
        src_f32 = at(G_AT + 36864 + 640, "src_f32", [P, ET])
        iota_nodes = keep("iota_nodes", [P, NP], F16)
        bias_row0 = at(small[0] - NP * 2, "bias0", [P, D])
        ident = keep("ident", [P, P])
        ident_r = keep("ident_r", [P, P], F32R)
        zeros = keep("zeros_bf16", [P, P], BF16)
        ones = keep("ones", [P, 2])
        ones_r = keep("ones_r", [P, 2], F32R)
        consts = keep("consts", [P, 4])
        deg_inv_sqrt = keep("deg_inv_sqrt", [P, NT])
        deg_inv = keep("deg_inv", [P, NT])
        deg_src = keep("deg_src", [P, NT])
        deg_dst = keep("deg_dst", [P, NT])
        stats_of_rows = keep("bn_stats", [P, 2, 2, 6])
        bn_mean_var = keep("bn_mean_var", [P, 2, 2])
        rstd_of_rows = keep("rstd", [P, 2, 2])
        outer_mean_var = keep("outer_mean_var", [P, 2, 2])
        outer_rstd = keep("outer_rstd", [P, 2, 2])
        flag = keep("flag", [1, 2], I32)
        gate_w_sb = keep("gate_w", [P, KT, NE])
        gate_bias_row = keep("gate_bias", [P, NE])
        gate_logits = keep("gate_logits", [P, NT, NE])
        gate_exp = keep("gate_exp", [P, NT, NE])
        gate_values = keep("gate_values", [P, NT, NE])
        gate_max = keep("gate_max", [P, 2, NT])
        gate_weights = keep("gate_weights", [P, NT, NE])
        gather_index = keep("gather_index", [P, 16], I32)
        one_plus_eps = keep("one_plus_eps", [P, 2])
        bn_stats1 = keep("bn_stats1", [P, 2, 6])
        bn_mean_var1 = keep("bn_mean_var1", [P, 2])
        rstd1 = keep("rstd1", [P, 2])
        XSP_AT = small[0]
        deg_src_row = at(XSP_AT + 8192 - NP * 4, "deg_src_row", [1, NP])
        x_split = keep("x_split", [P, 2, 2, D], F32R)
        iota_int = at(G_AT + 16384, "iota_int", [P, NP], I32)
        bounds = at(G_AT + 16384, "bounds", [P, 2, NT, EPW], I32)
        bounds_f32 = at(G_AT + 24576, "bounds_f32", [P, 2, NT * EPW])
        violation_flags = at(G_AT + 28672, "violations", [P, 2, ET])
        violation_sums = at(G_AT + 32768, "violation_sums", [P, 2])
        dst_int = at(G_AT + 36864, "dst_int", [P, ET], I32)

        x1_t = at(ADJ2_AT, "x1_transposed", [P, NT, D])
        agg1_transposed = at(ADJ2_AT + NODE, "agg1_transposed", [P, NT, D])
        SPARE = ADJ2_AT + 2 * NODE
        x_agg_split = at(SPARE, "x_agg_split", [P, 2, 2, D], F32R)
        h_nodes = at(SPARE + 8192, "h_nodes", [P, D])
        agg_nodes = at(XSP_AT, "agg_nodes", [P, 2, D])
        w_first = at(W_AT, "w_first", [P, 2, 2, KT, D], F32R)
        w_second = at(G_AT, "w_second", [P, 2, 2, KT, D], F32R)
        w_stage2 = at(X_AT, "w_stage2", [P, 2, KT, D])
        r_out = at(X_AT + 2 * MAT, "r_out", [P, D])
        h_transposed = at(G_AT + 4 * MAT, "h_transposed", [P, 2, D], F32R)
        bias1_first = at(G_AT + 4 * MAT + 4096, "bias1_first", [P, D])
        bias1_second = at(G_AT + 4 * MAT + 6144, "bias1_second", [P, D])
        g_out = at(XSP_AT + 6144, "g_out", [P, D])
        g2 = at(ADJ2_AT, "g2", [P, 2, NT, D], F32R)
        g1_again = at(G_AT, "g1_again", [P, 2, NT, D], F32R)
        r_ring = at(SPARE, "r_ring", [P, 5, D])
        g2_raw = at(ADJ2_AT, "g2_raw", [P, 2, NT, D])
        g1_raw = at(G_AT, "g1_raw", [P, 2, NT, D])
        x1_again = at(W_AT, "x1_again", [P, NT, D])
        gated_sum = x_nodes
        gated_rows = at(XSP_AT, "gated", [P, 2, 2, D])
        w2_raw = at(W_AT, "w2_raw", [P, 2, 2, KT, D])
        agg2_nodes = at(XSP_AT, "agg2_nodes", [P, 2, D])
        x_agg_split2 = at(SPARE, "x_agg_split2", [P, 2, 2, D], F32R)
        bias_gamma_beta2 = at(G_AT, "bias_gamma_beta2", [P, 3, D])
        y2 = at(G_AT + 6144, "y2", [P, 2, D])
        z2 = at(G_AT + 6144 + 4096, "z2", [P, 2, D])
        x1_spill = nc.dram_tensor("x1_spill", [P, NT, D], F32)
        g_spill = nc.dram_tensor("g_spill", [P, NE * NT, D], F32)
        r_spill = nc.dram_tensor("r_spill", [NE * NT, P, D], F32)

        w3_upper = at(ADJ_AT, "w3_hi", [P, 8 * KT, D], F32R)
        w3_lower = at(ADJ_AT + 8 * MAT, "w3_lo", [P, 8 * KT, D], F32R)
        w3_raw = at(ADJ_AT + 8 * MAT, "w3_raw", [P, 8 * KT, D])
        FREE = 16 * MAT
        gathered_rows = at(FREE, "gathered", [P, 4, D])
        gathered_more = at(XSP_AT, "gathered_more", [P, 4, D])

        def gathered(r):
            return (gathered_rows, gathered_more)[r // 4 % 2][:, r % 4]

        edge_sums = at(W_AT, "edge_sums", [P, NT, D])
        edge_attr_raw = at(W_AT + NODE, "edge_attr_raw", [P, 2, D])
        edge_attr_split = at(W_AT + NODE + 4096, "edge_attr_split", [P, 2, 2, D], F32R)
        edge_z = at(X_AT, "edge_z", [P, 2, D])
        messages = at(X_AT + 4096, "messages", [P, 2, 2, D], F32R)
        message_whole = at(X_AT + 4096 + 4096, "message_whole", [P, D])
        onehot_dst_r = at(X_AT + 12288, "onehot_dst_r", [P, 4, 2, P], F32R)
        w_edge_split = at(FREE + 8192, "w_edge_split", [P, 2, D], F32R)
        w_edge_raw = at(FREE + 8192, "w_edge_raw", [P, 2, D])
        b_edge_row = at(G_AT + 14336, "b_edge", [P, D])
        table_rows = at(XSP_AT + 4096, "table_rows", [P, 2, D])
        x3_table = nc.dram_tensor("x3_table", [NP, D], F32)
        x3_spill = nc.dram_tensor("x3_spill", [NT, P, D], F32)
        iota_int3 = at(G_AT + 16384, "iota_int3", [P, NP], I32)
        bias1_gamma1 = at(XSP_AT, "bias1_gamma1", [P, 2, 2 * D])
        beta1 = at(FREE, "beta1", [P, 2 * D])
        vectors2_first = at(FREE + 4096, "vectors2_first", [P, 4, D])
        vectors2_last = at(X_AT + 8192, "vectors2_last", [P, 3, D])
        y1_or_m = at(X_AT, "y1_or_m", [P, 2 * D])
        y2_or_y = at(X_AT + 4096, "y2_or_y", [P, D])
        x3_for_h0 = at(X_AT + 16384, "x3_for_h0", [P, D])
        x3_plus_y2 = at(X_AT + 18432, "x3_plus_y2", [P, D])
        x3_for_residual = at(X_AT + 14336, "x3_for_residual", [P, D])
        out_tile = at(X_AT + 6144, "out_tile", [P, D])
        split4 = at(W_AT + NODE, "split4", [P, 2, D], F32R)
        split8 = at(W_AT + NODE + 4096, "split8", [P, 2, 2 * D], F32R)

        psum_all = ctx.enter_context(nc.psum_tensor("banks", [P, 8, 512], F32))
        psum_bank = [psum_all[:, i, :] for i in range(8)]

        T_L1, T_L2, T_MLP1 = NT, 2 * NT, 3 * NT
        HT_MLP1 = NE * NT
        F_L1, F_GA, F_L2 = NT, 2 * NT, (2 + NE) * NT
        R_EX, R_L2, R_MLP1 = NT, (1 + NE) * NT, (2 + NE) * NT
        A_L1, A_EX, A_L2 = NT, 2 * NT, (2 + NE) * NT
        SC_L2 = NT
        W_L2, W_EDGE, W_MLP = 1, 2, 3
        N_L1, N_L2, N_MLP1, N_MLP2 = NT, 2 * NT, 3 * NT, 4 * NT
        O_MLP1 = NT
        B_MLP1 = NT
        GEN_T, GEN_U, GEN_M = ET, ET - 1, sum(not whole(t) for t in range(ET))
        GEN_W = NT
        GEN_G = ET // 4
        GEN_EA, GEN_GA = 16 * (ET // 8), 16 * (ET // 8)

        x_loaded = sem("x_loaded")
        edges_loaded = sem("edges_loaded")
        w_loaded = sem("w_loaded")
        bias0_loaded = sem("bias0_loaded")
        constants = sem("constants")
        iota_int_ready = sem("iota_int_ready")
        bounds_ready = sem("bounds_ready")
        bounds_f32_ready = sem("bounds_f32_ready")
        dve_setup = sem("dve_setup")
        violations_ready = sem("violations_ready")
        violations_summed = sem("violations_summed")
        flag_ready = sem("flag_ready")
        fence = sem("fence")
        onehots_ready = sem("onehots_ready")
        onehots_used = sem("onehots_used")
        window_done = sem("window_done")
        window_copied = sem("window_copied")
        adj_transposed = sem("adj_transposed")
        adj_copied_act = sem("adj_copied_act")
        adj_copied_dve = sem("adj_copied_dve")
        degrees_ready = sem("degrees_ready")
        deg_src_plus1 = sem("deg_src_plus1")
        ones_r_ready = sem("ones_r_ready")
        deg_src_row_summed = sem("deg_src_row_summed")
        deg_src_row_ready = sem("deg_src_row_ready")
        deg_src_columns = sem("deg_src_columns")
        deg_inv_sqrt_ready = sem("deg_inv_sqrt_ready")
        weights_hi = sem("weights_hi")
        weights_split = sem("weights_split")
        identity_r_ready = sem("identity_r_ready")
        node_rows_transposed = sem("node_rows_transposed")
        rows_hi = sem("rows_hi")
        rows_split = sem("rows_split")
        first_linear_done = sem("first_linear_done")
        l0_feat_ready = sem("l0_feat_ready")
        features_hi = sem("features_hi")
        features_ready = sem("features_ready")
        aggregated = sem("aggregated")
        l0_resid_ready = sem("l0_resid_ready")
        norm_stats = sem("norm_stats")
        norm_var = sem("norm_var")
        norm_var_eps = sem("norm_var_eps")
        norm_rstd = sem("norm_rstd")
        layer_output_ready = sem("layer_output_ready")
        b_edge_loaded = sem("b_edge_loaded")
        w_edge_loaded = sem("w_edge_loaded")
        iota3_int = sem("iota3_int")
        iota3_ready = sem("iota3_ready")
        table_rows_ready = sem("table_rows_ready")
        table_rows_stored = [sem(f"table_stored_{i}") for i in range(2)]
        x3_stored = sem("x3_stored")
        w3_loaded = sem("w3_loaded")
        w3_last_ready = sem("w3_last_ready")
        edge_attr_arrived = [sem(f"edge_attr_loaded_{i}") for i in range(2)]
        edge_attr_hi = sem("edge_attr_hi")
        edge_attr_ready = sem("edge_attr_ready")
        gather_index_ready = sem("gather_index_ready")
        rows_gathered = [sem(f"gathered_{i}") for i in range(8)]
        edge_embedded = sem("edge_embedded")
        edge_z_ready = sem("edge_z_ready")
        message_hi = sem("message_hi")
        message_ready = sem("message_ready")
        message_summed = sem("message_summed")
        edge_window_done = sem("edge_window_done")
        edge_window_copied = sem("edge_window_copied")
        eps_loaded = sem("eps_loaded")
        one_plus_eps_ready = sem("one_plus_eps_ready")
        vectors1_loaded = sem("vectors1_loaded")
        beta1_loaded = sem("beta1_loaded")
        vectors2_first_loaded = sem("vectors2_first_loaded")
        vectors2_last_loaded = sem("vectors2_last_loaded")
        x3_for_h0_loaded = sem("x3_for_h0_loaded")
        x3_for_residual_loaded = sem("x3_for_residual_loaded")
        x3_scaled = sem("x3_scaled")
        h0_ready = sem("h0_ready")
        y1_biased = sem("y1_biased")
        y1_stats_done = sem("y1_stats")
        y1_var = sem("y1_var")
        y1_var_eps = sem("y1_var_eps")
        y1_rstd = sem("y1_rstd")
        y1_gamma = sem("y1_gamma")
        y1_normed = sem("y1_normed")
        y1_gelu = sem("y1_gelu")
        times_gamma = sem("times_gamma")
        normed = sem("normed")
        y2_gelu = sem("y2_gelu")
        residual_added = sem("residual_added")
        residual_gamma = sem("residual_gamma")
        out_tile_stored = sem("out_tile_stored")
        x1_spilled = sem("x1_spilled")
        gate_loaded = sem("gate_loaded")
        gate_chain = sem("gate_chain")
        gate_exp_ready = sem("gate_exp_ready")
        l1_xt_ready = sem("l1_xt_ready")
        l1_logits_done = sem("l1_logits_done")
        aggregate_scaled = sem("aggregate_scaled")
        l1_agg_transposed = sem("l1_agg_transposed")
        l1_at_ready = sem("l1_at_ready")
        expert_weights_loaded = sem("expert_weights_loaded")
        expert_bias_first_loaded = sem("expert_bias_first_loaded")
        expert_bias_second_loaded = sem("expert_bias_second_loaded")
        expert_w_first_hi = sem("expert_w_first_hi")
        expert_w_first_ready = sem("expert_w_first_ready")
        expert_w_second_hi = sem("expert_w_second_hi")
        expert_w_second_ready = sem("expert_w_second_ready")
        hidden_rows_transposed = sem("hidden_rows_transposed")
        second_linear_done = sem("second_linear_done")
        ex_h_ready = sem("ex_h_ready")
        hidden_hi = sem("hidden_hi")
        hidden_split = sem("hidden_split")
        ex_r_ready = sem("ex_r_ready")
        expert_g_copied = sem("expert_g_copied")
        g_stored = sem("g_stored")
        r_stored = sem("r_stored")
        x1_reloaded = sem("x1_reloaded")
        x1_added_done = sem("x1_added")
        g_arrived = [sem(f"g_loaded_{i}") for i in range(2)]
        r_arrived = [sem(f"r_loaded_{i}") for i in range(5)]
        gather_scaled = sem("gather_scaled")
        gather_gated = sem("gather_gated")
        gather_added = sem("gather_added")
        w2_loaded = sem("w2_loaded")
        l2_vectors_loaded = sem("l2_vectors_loaded")
        linear_biased = sem("linear_biased")
        l2_dve_steps = sem("l2_dve_steps")
        gate_weights_ready = sem("gate_weights_ready")
        outer_stats_done = sem("outer_stats")
        outer_var = sem("outer_var")
        outer_var_eps = sem("outer_var_eps")
        outer_rstd_done = sem("outer_rstd")

        block = ctx.enter_context(nc.Block())

        @block.sync
        def _(sp):
            sp.dma_start(dst_int[:], dst).then_inc(edges_loaded, 16)
            sp.dma_start(src_index[:], src).then_inc(edges_loaded, 16)
            sp.dma_start(x_nodes[:], x).then_inc(x_loaded, 16)
            sp.dma_start(w_stage[:], w0).then_inc(w_loaded, 16)
            sp.wait_ge(adj_transposed, 1)
            sp.dma_start(bias_row0[:], b0.partition_broadcast(P)).then_inc(bias0_loaded, 16)
            sp.dma_start(gate_w_sb[:], gate_w).then_inc(gate_loaded, 16)
            sp.dma_start(gate_bias_row[:], gate_b.partition_broadcast(P)).then_inc(gate_loaded, 16)
            for n in range(0, NT, 2):
                sp.wait_ge(layer_output_ready, n + 2)
                sp.dma_start(x1_spill[:, n:n + 2, :], x_nodes[:, n:n + 2, :]).then_inc(x1_spilled, 16)
            for e in range(NE):
                if e == 0:
                    sp.wait_ge(x1_spilled, 16 * NT // 2)
                    sp.wait_ge(features_ready, F_L1 + NT)
                    sp.wait_ge(node_rows_transposed, T_L1 + NT)
                else:
                    sp.wait_ge(expert_w_second_ready, 2 * e)
                sp.dma_start(w_stage2[:], w1[e, 0]).then_inc(expert_weights_loaded, 16)
                if e >= 1:
                    sp.wait_ge(ex_h_ready, NT * e)
                    sp.dma_start(bias1_first[:], b1[e, 0].partition_broadcast(P)).then_inc(expert_bias_first_loaded, 16)
                sp.wait_ge(expert_w_first_ready, 2 * e + 2)
                sp.dma_start(w_stage2[:], w1[e, 1]).then_inc(expert_weights_loaded, 16)
                if e == 0:
                    sp.wait_ge(aggregated, A_L1 + NT)
                    sp.dma_start(bias1_first[:], b1[e, 0].partition_broadcast(P)).then_inc(expert_bias_first_loaded, 16)
                need(sp, ex_r_ready, NT * e)
                sp.dma_start(bias1_second[:], b1[e, 1].partition_broadcast(P)).then_inc(expert_bias_second_loaded, 16)
            def load_g(e):
                sp.wait_ge(g_stored, 16 * NT * (e + 1))
                for half in (0, 1):
                    ks = slice(half * NT // 2, (half + 1) * NT // 2)
                    need(sp, g_arrived[half], 16 * e)
                    sp.dma_start((g2_raw, g1_raw)[e % 2][:, 1, ks], g_spill[:, e * NT + ks.start:e * NT + ks.stop, :]).then_inc(g_arrived[half], 16)

            def load_r(m, slot):
                need(sp, gather_scaled, m - 4)
                sp.dma_start(r_ring[:, slot], r_spill[bass.ds(m, 1)].rearrange("a p f -> (a p) f")).then_inc(r_arrived[slot], 16)

            sp.wait_ge(rows_split, R_EX + NE * NT)
            load_g(0)
            sp.wait_ge(first_linear_done, R_EX + NE * NT)
            sp.wait_ge(hidden_rows_transposed, NE * NT)
            for m in range(5):
                sp.wait_ge(r_stored, 16 * (m + 1))
                load_r(m, m)
            sp.dma_start(x1_again[:], x1_spill[:, :, :]).then_inc(x1_reloaded, 16)
            sp.wait_ge(second_linear_done, NE * NT)
            sp.wait_ge(hidden_split, NE * NT)
            sp.wait_ge(ex_r_ready, NE * NT)
            sp.wait_ge(r_stored, 16 * NE * NT)
            load_g(1)
            for e in range(NE):
                for n in range(5 if e == 0 else 0, NT):
                    load_r(e * NT + n, n % 5)
                    if n == 0 and e == 1:
                        sp.wait_ge(x1_added_done, NT)
                        sp.dma_start(w2_raw[:, :, 1], w2).then_inc(w2_loaded, 16)
                    if n == 5 and e in (1, 2):
                        sp.wait_ge(aggregated, A_EX + NT * e)
                        load_g(e + 1)
            sp.wait_ge(aggregated, A_EX + NE * NT)
            for i, row in enumerate((l2_bias, l2_gamma, l2_beta)):
                sp.dma_start(bias_gamma_beta2[:, i], row.partition_broadcast(P)).then_inc(l2_vectors_loaded, 16)

            sp.dma_start(b_edge_row[:], b_edge.partition_broadcast(P)).then_inc(b_edge_loaded, 16)
            sp.dma_start(one_plus_eps[:, 0:1], eps.partition_broadcast(P)).then_inc(eps_loaded, 16)
            sp.dma_start(w_edge_raw[:, 1], w_edge).then_inc(w_edge_loaded, 16)
            for n in range(NT):
                if n == NT - 1:
                    sp.wait_ge(first_linear_done, R_L2 + NT)
                    for g in range(2):
                        sp.dma_start(edge_attr_raw[:, g], edge_attr[g]).then_inc(edge_attr_arrived[g], 16)
                sp.wait_ge(layer_output_ready, N_L2 + n + 1)
                sp.dma_start(x3_spill[n], x_nodes[:, n, :]).then_inc(x3_stored, 16)
                sp.wait_ge(table_rows_ready, n + 1)
                sp.dma_start(x3_table[n * P:(n + 1) * P, :], table_rows[:, n % 2]).then_inc(table_rows_stored[n % 2], 16)
            sp.wait_ge(x3_stored, 16 * NT)
            sp.dma_start(x3_for_h0[:], x3_spill[0]).then_inc(x3_for_h0_loaded, 16)
            def load_attr(group, b):
                need(sp, edge_attr_ready, group - 1)
                sp.dma_start(edge_attr_raw[:, b], edge_attr[bass.ds(group, 1)].rearrange("a p f -> (a p) f")).then_inc(edge_attr_arrived[b], 16)

            def load_piece(q):
                need(sp, w3_loaded, 16 * q)
                sp.dma_start(w3_raw[:, bass.ds(q, 1)].rearrange("p a f -> p (a f)"),
                             w3[:, bass.ds(q, 1)].rearrange("p a f -> p (a f)")).then_inc(w3_loaded, 16)

            load_attr(2, 0)
            load_attr(3, 1)
            sp.wait_ge(iota3_ready, 1)
            for i in range(4):
                load_attr(4 + i, i % 2)
                load_piece(i)
            with sp.Fori(2, 9) as k:
                for i in range(4):
                    load_attr(4 * k + i, i % 2)
                    load_piece(4 * (k - 1) + i)
            for group in range(36, ET // 4):
                load_attr(group, group % 2)
            sp.wait_ge(edge_window_copied, NT)
            general = sp.value_load(flag[0:1, 0:1], min_val=0, max_val=ET * P)
            with sp.If(general > ET * P - N_EDGES):
                with sp.Fori(0, NT) as d:
                    with sp.Fori(0, ET // 4) as g:
                        for i in range(4):
                            sp.wait_ge(message_summed, GEN_U + (d * (ET // 4) + g) * 4 + i)
                            sp.dma_start(edge_attr_raw[:, 0, 0:P], edge_attr[bass.ds(g, 1), :, i * P:(i + 1) * P].rearrange(
                                "a p f -> (a p) f")).then_inc(edge_attr_arrived[0], 16)
                sp.wait_ge(edge_window_copied, GEN_W + NT)
                sp.nop()
            with sp.Else():
                sp.nop()
            sp.nop()
            for n in range(NT):
                if n >= 1:
                    sp.wait_ge(h0_ready, n)
                    sp.dma_start(x3_for_h0[:], x3_spill[n]).then_inc(x3_for_h0_loaded, 16)
                if n == 0:
                    for i in (0, 1):
                        sp.dma_start(bias1_gamma1[:, i], v1[i].partition_broadcast(P)).then_inc(vectors1_loaded, 16)
                    sp.dma_start(beta1[:], v1[2].partition_broadcast(P)).then_inc(beta1_loaded, 16)
                if n == 1:
                    for i in range(4):
                        sp.dma_start(vectors2_first[:, i], v2[i].partition_broadcast(P)).then_inc(vectors2_first_loaded, 16)
                    for i in range(3):
                        sp.dma_start(vectors2_last[:, i], v2[4 + i].partition_broadcast(P)).then_inc(vectors2_last_loaded, 16)
                if n >= 4:
                    sp.wait_ge(residual_added, n - 4)
                    sp.dma_start(x3_for_residual[:], x3_spill[n - 4]).then_inc(x3_for_residual_loaded, 16)
            for n in range(NT - 4, NT):
                sp.wait_ge(residual_added, n)
                sp.dma_start(x3_for_residual[:], x3_spill[n]).then_inc(x3_for_residual_loaded, 16)
            for n in range(NT):
                sp.wait_ge(residual_added, NT)
                need(sp, residual_added, n, B_MLP1)
                sp.dma_start(x3_for_residual[:], x3_spill[n]).then_inc(x3_for_residual_loaded, 16)
                if n >= 1:
                    sp.wait_ge(layer_output_ready, N_MLP2 + n)
                    sp.dma_start(out[:, n - 1, :], out_tile[:]).then_inc(out_tile_stored, 16)
            sp.wait_ge(layer_output_ready, N_MLP2 + NT)
            sp.dma_start(out[:, NT - 1, :], out_tile[:]).then_inc(out_tile_stored, 16)
            sp.wait_ge(out_tile_stored, 16 * NT)

        @block.gpsimd
        def _(g):
            g.iota(iota_int[:], pattern=[[1, NP]], base=0, channel_multiplier=0).then_inc(iota_int_ready, 1)
            g.memset(ident[:], 0.0).then_inc(constants, 1)
            g.memset(ones[:], 1.0).then_inc(constants, 1)
            g.memset(zeros[:], 0.0).then_inc(constants, 1)
            g.memset(consts[:, 0:1], EPS).then_inc(constants, 1)
            g.memset(consts[:, 1:2], -0.5).then_inc(constants, 1)
            g.memset(consts[:, 2:4], 1.0).then_inc(constants, 1)
            g.wait_ge(constants, 6)
            g.affine_select(out=ident[:], in_=ident[:], compare_op=ALU.not_equal, fill=1.0, base=0,
                            pattern=[[-1, P]], channel_multiplier=1).then_inc(constants, 1)
            g.wait_ge(dve_setup, 1)
            L, H = bounds[:, 0], bounds[:, 1]
            g.iota(L[:, :, 0:MARGIN], pattern=[[P, NT], [0, MARGIN]], base=-P, channel_multiplier=0).then_inc(bounds_ready, 1)
            g.iota(L[:, :, MARGIN:], pattern=[[P, NT], [0, EPW - MARGIN]], base=0, channel_multiplier=0).then_inc(bounds_ready, 1)
            g.iota(H[:, :, 0:EPW - MARGIN], pattern=[[P, NT], [0, EPW - MARGIN]], base=P, channel_multiplier=0).then_inc(bounds_ready, 1)
            g.iota(H[:, :, EPW - MARGIN:], pattern=[[P, NT], [0, MARGIN]], base=2 * P, channel_multiplier=0).then_inc(bounds_ready, 1)
            g.wait_ge(deg_src_plus1, 1)
            g.tensor_tensor(deg_inv_sqrt[:], deg_src[:], consts[:, 1:2].to_broadcast([P, NT]), ALU.pow).then_inc(deg_inv_sqrt_ready, 1)

            def rstd(n, b, since=0):
                need(g, norm_var, n + 1, since)
                g.tensor_tensor(rstd_of_rows[:, b, 0:1], bn_mean_var[:, b, 1:2], consts[:, 0:1], ALU.add).then_inc(norm_var_eps, 1)
                need(g, norm_var_eps, n + 1, since)
                g.tensor_tensor(rstd_of_rows[:, b, 1:2], rstd_of_rows[:, b, 0:1], consts[:, 1:2], ALU.pow).then_inc(norm_rstd, 1)

            def rstd_outer(n, b, since=0):
                need(g, outer_var, n + 1, since)
                g.tensor_tensor(outer_rstd[:, b, 0:1], outer_mean_var[:, b, 1:2], consts[:, 0:1], ALU.add).then_inc(outer_var_eps, 1)
                need(g, outer_var_eps, n + 1, since)
                g.tensor_tensor(outer_rstd[:, b, 1:2], outer_rstd[:, b, 0:1], consts[:, 1:2], ALU.pow).then_inc(outer_rstd_done, 1)
            tile_loop(g, rstd)

            with g.Fori(0, NE * NT) as m:
                g.wait_ge(expert_g_copied, m + 1)
                g.dma_start(g_spill[:, bass.ds(m, 1), :].rearrange("p a f -> p (a f)"), g_out[:]).then_inc(g_stored, 16)
                g.wait_ge(ex_r_ready, m + 1)
                g.dma_start(r_spill[bass.ds(m, 1)].rearrange("a p f -> (a p) f"), r_out[:]).then_inc(r_stored, 16)

            g.wait_ge(x1_reloaded, 16)

            def x1_added(n, b):
                need(g, gather_gated, n + 1)
                row = gated_sum[:, bass.ds(n, 1)].rearrange("p a f -> p (a f)")
                g.tensor_tensor(row, row, x1_again[:, bass.ds(n, 1)].rearrange("p a f -> p (a f)"), ALU.add).then_inc(x1_added_done, 1)
            tile_loop(g, x1_added)
            tile_loop(g, lambda n, b: rstd(n, b, N_L1))
            g.wait_ge(aggregated, A_EX + NE * NT)
            g.iota(iota_int3[:], pattern=[[1, NP]], base=0, channel_multiplier=0).then_inc(iota3_int, 1)

            def table(n):
                g.wait_ge(layer_output_ready, N_L2 + n + 1)
                if n >= 2:
                    g.wait_ge(table_rows_stored[n % 2], 16 * (n // 2))
                g.tensor_tensor(table_rows[:, n % 2], x_nodes[:, n, :], b_edge_row[:], ALU.add).then_inc(table_rows_ready, 1)

            g.wait_ge(b_edge_loaded, 16)
            for n in range(NT + 2):
                if 1 <= n <= NT:
                    rstd_outer(n - 1, (n - 1) % 2)
                if n < NT:
                    rstd(n, n % 2, N_L2)
                if n >= 2:
                    table(n - 2)

            def attr_lo(i, b):
                need(g, edge_attr_hi, 2 * i + b + 1)
                g.tensor_tensor(edge_attr_split[:, b, 1], edge_attr_raw[:, b], edge_attr_split[:, b, 0].bitcast(F32), ALU.subtract).then_inc(edge_attr_ready, 1)

            attr_lo(0, 0)
            g.wait_ge(table_rows_stored[0], 16 * (NT // 2))
            g.wait_ge(table_rows_stored[1], 16 * (NT // 2))

            def gathers(j):
                for r in range(2 * EPW):
                    t = 2 * EPW * j + r
                    need(g, edge_z_ready, t - 7)
                    at_ = r % 16
                    if r % 4 == 0:
                        g.sem_inc(fence, 1)
                        g.tensor_copy(gather_index[:, at_:at_ + 4], src_index[:, bass.ds(t, 4)]).then_inc(gather_index_ready, 1)
                        need(g, gather_index_ready, 8 * j + r // 4 + 1)
                    g.sem_inc(fence, 1)
                    g.indirect_dma_start(gathered(r), None, x3_table[:, :],
                                         bass.IndirectOffsetOnAxis(ap=gather_index[:, at_:at_ + 1], axis=0)).then_inc(
                                             rows_gathered[r % 8], 16)
                    if r % 4 == 0 and not (isinstance(j, int) and j == 0 and r < 4):
                        attr_lo(4 * j + r // 8, (r // 4) % 2)
            window_loop(g, gathers)
            g.wait_ge(edge_window_copied, NT)
            general = g.value_load(flag[0:1, 0:1], min_val=0, max_val=ET * P)
            with g.If(general > ET * P - N_EDGES):
                with g.Fori(0, NT) as d:
                    with g.Fori(0, ET) as t:
                        g.wait_ge(message_summed, GEN_U + d * ET + t)
                        g.sem_inc(fence, 1)
                        g.tensor_copy(gather_index[:, 0:1], src_index[:, bass.ds(t, 1)]).then_inc(gather_index_ready, 1)
                        g.wait_ge(gather_index_ready, GEN_G + d * ET + t + 1)
                        g.sem_inc(fence, 1)
                        g.indirect_dma_start(gathered_rows[:, 0], None, x3_table[:, :],
                                             bass.IndirectOffsetOnAxis(ap=gather_index[:, 0:1], axis=0)).then_inc(rows_gathered[0], 16)
                g.wait_ge(edge_window_copied, GEN_W + NT)
                g.nop()
            with g.Else():
                g.nop()
            g.nop()

            def rstd_wide(n):
                need(g, y1_var, n + 1)
                g.tensor_tensor(rstd1[:, 0:1], bn_mean_var1[:, 1:2], consts[:, 0:1], ALU.add).then_inc(y1_var_eps, 1)
                need(g, y1_var_eps, n + 1)
                g.tensor_tensor(rstd1[:, 1:2], rstd1[:, 0:1], consts[:, 1:2], ALU.pow).then_inc(y1_rstd, 1)

            def h0(n):
                need(g, x3_scaled, n + 1)
                row = edge_sums[:, bass.ds(n, 1)].rearrange("p a f -> p (a f)")
                g.tensor_tensor(row, x3_for_h0[:], row, ALU.add).then_inc(h0_ready, 1)

            def last_w3_lo(q):
                need(g, weights_hi, q + 1, W_MLP)
                row = lambda t: t[:, bass.ds(q, 1)].rearrange("p a f -> p (a f)")
                g.tensor_tensor(row(w3_lower), row(w3_raw), row(w3_upper).bitcast(F32), ALU.subtract).then_inc(w3_last_ready, 1)

            def add_x3(n):
                need(g, y2_gelu, n + 1)
                need(g, x3_for_residual_loaded, 16 * (n + 1))
                need(g, layer_output_ready, n, N_MLP1)
                g.tensor_tensor(x3_plus_y2[:], y2_or_y[:], x3_for_residual[:], ALU.add).then_inc(residual_added, 1)

            def nodes(q, at):
                if at + 2 < NT:
                    h0(q + 2)
                if at < NT:
                    rstd_wide(q)
                if 3 <= at < NT + 3:
                    rstd_outer(q - 3, 0, O_MLP1)
                if at >= 2:
                    rstd(q - 2, 0, N_MLP1)
                if 2 <= at < NT + 2:
                    add_x3(q - 2)
                if at < NT - 2:
                    last_w3_lo(q + 24)
                if at >= NT + 2:
                    rstd_outer(q - 2, 0, O_MLP1)
            h0(0)
            h0(1)
            node_loop(g, nodes)

        @block.scalar
        def _(a):
            a.wait_ge(w_loaded, 16)
            nc.scalar.copy(w0_hi[:], w_stage[:]).then_inc(weights_hi, 1)

            def windows(j):
                for b in (0, 1):
                    d = 2 * j + b
                    need(a, window_done, d + 1)
                    for c, w in ((0, 512), (1, 512), (2, 256)):
                        last = nc.scalar.copy(adj_dst_src[:, bass.ds(d, 1), 512 * c:512 * c + w].rearrange("p a f -> p (a f)"),
                                              psum_bank[3 * b + c][:, 0:w])
                    last.then_inc(window_copied, 1)
            window_loop(a, windows)
            a.wait_ge(flag_ready, 1)
            general = a.value_load(flag[0:1, 0:1], min_val=0, max_val=ET * P)
            with a.If(general > ET * P - N_EDGES):
                with a.Fori(0, NT) as d:
                    a.wait_ge(window_done, GEN_W + d + 1)
                    for c, w in ((0, 512), (1, 512), (2, 256)):
                        last = nc.scalar.copy(adj_dst_src[:, bass.ds(d, 1), 512 * c:512 * c + w].rearrange("p a f -> p (a f)"),
                                              psum_bank[c][:, 0:w])
                    last.then_inc(window_copied, 1)
                a.nop()
            with a.Else():
                a.nop()
            a.nop()

            a.wait_ge(deg_src_row_summed, 1)
            nc.scalar.copy(deg_src_row[:], psum_all[0:1, 3:6].rearrange("p a f -> p (a f)")[:, 0:NP]).then_inc(deg_src_row_ready, 1)

            def transposed(n, b):
                need(a, adj_transposed, 3 * n + 1)
                nc.scalar.copy(adj_src_dst[:, 0:4, bass.ds(n * P, P)],
                               psum_bank[3 * b].rearrange("p (k c) -> p k c", k=4)).then_inc(adj_copied_act, 1)
            tile_loop(a, transposed)

            def l0(n, b):
                need(a, node_rows_transposed, n + 1)
                need(a, first_linear_done, n - 1)
                nc.scalar.copy(x_split[:, b, 0, :], psum_bank[6 + b]).then_inc(rows_hi, 1)
                if not (isinstance(n, int) and n == 0):
                    hi_of_feat(n - 1, 1 - b)

            def hi_of_feat(n, b):
                need(a, l0_feat_ready, n + 1)
                nc.scalar.copy(g1_hi[:, bass.ds(n, 1), :].rearrange("p a f -> p (a f)"), feat_rows[:, b, :]).then_inc(features_hi, 1)
            tile_loop(a, l0)
            hi_of_feat(NT - 1, 1)

            a.wait_ge(aggregated, NT)
            def l1_x(n, b):
                need(a, layer_output_ready, n + 1)
                nc.scalar.copy(g1_hi[:, bass.ds(n, 1), :].rearrange("p a f -> p (a f)"),
                               x_nodes[:, bass.ds(n, 1), :].rearrange("p a f -> p (a f)")).then_inc(features_hi, 1)
                need(a, node_rows_transposed, n + 1, T_L1)
                nc.scalar.copy(x1_t[:, bass.ds(n, 1), :].rearrange("p a f -> p (a f)"), psum_bank[b]).then_inc(l1_xt_ready, 1)
            tile_loop(a, l1_x)
            a.wait_ge(gate_chain, 3)
            nc.scalar.activation(gate_exp[:], gate_logits[:], ACT.Exp).then_inc(gate_exp_ready, 1)

            def first_weights_hi(e):
                a.wait_ge(expert_weights_loaded, 32 * e + 16)
                a.wait_ge(first_linear_done, R_EX + NT * e) if not isinstance(e, int) else need(a, first_linear_done, NT * e, R_EX)
                for i in (0, 1):
                    nc.scalar.copy(w_first[:, i, 0], w_stage2[:, i]).then_inc(expert_w_first_hi, 1)

            first_weights_hi(0)

            def xa_hi(m, n):
                need(a, first_linear_done, m, R_EX)
                nc.scalar.copy(x_agg_split[:, 0, 0], x1_t[:, bass.ds(n, 1), :].rearrange("p a f -> p (a f)"))
                nc.scalar.copy(x_agg_split[:, 1, 0], agg1_transposed[:, bass.ds(n, 1), :].rearrange("p a f -> p (a f)")).then_inc(rows_hi, 1)

            def l1_scaled(n, b):
                if isinstance(n, int) and n == NT - 1:
                    a.wait_ge(l1_at_ready, 1)
                    xa_hi(0, 0)
                need(a, aggregated, n + 1, A_L1)
                need(a, l1_agg_transposed, n - 1)
                nc.scalar.activation(agg_nodes[:, b], psum_bank[2 + b], ACT.Copy, scale=deg_inv[:, bass.ds(n, 1)]).then_inc(aggregate_scaled, 1)
            tile_loop(a, l1_scaled)

            def second_weights_hi(e):
                a.wait_ge(expert_weights_loaded, 32 * e + 32)
                need(a, second_linear_done, NT * e)
                for i in (0, 1):
                    nc.scalar.copy(w_second[:, i, 0], w_stage2[:, i]).then_inc(expert_w_second_hi, 1)

            def hT_hi(m):
                need(a, hidden_rows_transposed, m + 1)
                nc.scalar.activation(h_transposed[:, 0], psum_bank[2], ACT.Relu).then_inc(hidden_hi, 1)

            def g_hi(m):
                need(a, second_linear_done, m + 1)
                need(a, g_stored, 16 * m)
                nc.scalar.copy(g_out[:], psum_bank[4]).then_inc(expert_g_copied, 1)

            def expert(e, final):
                with a.Fori(1, NT - 1) as n:
                    m = e * NT + n
                    hT_hi(m - 1)
                    xa_hi(m + 1, n + 1)
                    g_hi(m - 1)
                m = e * NT + NT - 1
                hT_hi(m - 1)
                if not final:
                    xa_hi(m + 1, 0)
                    first_weights_hi(e + 1)
                g_hi(m - 1)
                if not final:
                    hT_hi(m)
                    xa_hi(m + 2, 1)
                    g_hi(m)
                    second_weights_hi(e + 1)

            def gather_hi(e, k):
                G, R = ((g2, g2_raw), (g1_again, g1_raw))[e % 2]
                if k % (NT // 2) == 0:
                    a.wait_ge(g_arrived[2 * k // NT], 16 * (e + 1))
                nc.scalar.copy(G[:, 0, k], R[:, 1, k]).then_inc(features_hi, 1)

            a.wait_ge(aggregated, A_L1 + NT)
            second_weights_hi(0)
            a.wait_ge(l1_at_ready, NT)
            xa_hi(1, 1)
            with a.Fori(0, NE - 1) as e:
                expert(e, False)
            expert(NE - 1, True)
            hT_hi(NE * NT - 1)
            for k in range(NT):
                gather_hi(0, k)
            g_hi(NE * NT - 1)

            def gated(m, e, n, b):
                need(a, gather_scaled, m + 1)
                g_of = gate_weights[:, n:n + 1, e].rearrange("p a -> p a")
                if e == 0:
                    nc.scalar.activation(gated_sum[:, n], gated_rows[:, 0, b], ACT.Relu, scale=g_of).then_inc(gather_gated, 1)
                else:
                    need(a, gather_added, m - NT - 1)
                    nc.scalar.activation(gated_rows[:, 1, b], gated_rows[:, 0, b], ACT.Relu, scale=g_of).then_inc(gather_gated, 1)

            def x2_hi(n):
                if n == 0:
                    a.wait_ge(aggregated, A_EX + (NE - 1) * NT)
                need(a, layer_output_ready, n + 1, N_L1)
                nc.scalar.copy(g2[:, 0, n], x_nodes[:, n, :]).then_inc(features_hi, 1)

            a.wait_ge(r_stored, 16 * NE * NT)
            a.wait_ge(g_stored, 16 * NE * NT)
            for e in range(NE):
                if e == 2:
                    a.wait_ge(w2_loaded, 16)
                    nc.scalar.copy(w_first[:, :, 0], w2_raw[:, :, 1]).then_inc(weights_hi, 1)
                for n in range(NT):
                    if e + 1 < NE and n >= NT // 2:
                        gather_hi(e + 1, 2 * n - NT)
                        gather_hi(e + 1, 2 * n - NT + 1)
                    gated(e * NT + n, e, n, n % 2)
                    if e == NE - 1 and n >= 2:
                        x2_hi(n - 2)
            x2_hi(NT - 2)
            x2_hi(NT - 1)

            a.wait_ge(w_edge_loaded, 16)
            nc.scalar.copy(w_edge_split[:, 0], w_edge_raw[:, 1]).then_inc(weights_hi, 1)

            def l2(n, b):
                need(a, aggregated, n + 1, A_L2)
                need(a, node_rows_transposed, n - 1, T_L2)
                nc.scalar.activation(agg2_nodes[:, b], psum_bank[2 + b], ACT.Copy, scale=deg_inv[:, bass.ds(n, 1)]).then_inc(aggregate_scaled, 1)
                need(a, node_rows_transposed, n + 1, T_L2)
                nc.scalar.copy(x_agg_split2[:, 0, 0], psum_bank[0])
                nc.scalar.copy(x_agg_split2[:, 1, 0], psum_bank[1]).then_inc(rows_hi, 1)
            tile_loop(a, l2)


            def attr_hi(i, b):
                a.wait_ge(edge_attr_arrived[b], 16 * i + 16)
                need(a, edge_embedded, 4 * (2 * i + b - 1))
                nc.scalar.copy(edge_attr_split[:, b, 0], edge_attr_raw[:, b]).then_inc(edge_attr_hi, 1)

            def w3_hi(q):
                a.wait_ge(w3_loaded, 16 * (q + 1))
                nc.scalar.copy(w3_upper[:, bass.ds(q, 1)].rearrange("p k f -> p (k f)"),
                               w3_raw[:, bass.ds(q, 1)].rearrange("p k f -> p (k f)")).then_inc(weights_hi, 1)

            def edges_hi(j):
                for r in range(2 * EPW):
                    t = 2 * EPW * j + r
                    need(a, edge_z_ready, t + 1)
                    need(a, message_summed, t - 1)
                    to = message_whole[:] if whole(r) else messages[:, r % 2, 0]
                    nc.scalar.activation(to, edge_z[:, r % 2], ACT.Relu).then_inc(message_hi, 1)
                    if r % 4 == 3 and not (isinstance(j, int) and j == NT // 2 - 1 and r >= 2 * EPW - 5):
                        ahead = (r + 1) // 4 + 1
                        attr_hi(4 * j + ahead // 2, ahead % 2)
                    if r % 4 == 2 and not isinstance(j, int):
                        w3_hi(8 * (j - 1) + r // 4)
                    if r % EPW == MARGIN + 1 and not (isinstance(j, int) and j == 0 and r < EPW):
                        window_copy(2 * j + r // EPW - 1, (r // EPW + 1) % 2)

            def scaled_x3(n):
                need(a, x3_for_h0_loaded, 16 * (n + 1))
                nc.scalar.activation(x3_for_h0[:], x3_for_h0[:], ACT.Copy, scale=one_plus_eps[:, 1:2]).then_inc(x3_scaled, 1)

            def window_copy(d, b):
                need(a, edge_window_done, d + 1)
                nc.scalar.copy(edge_sums[:, bass.ds(d, 1)].rearrange("p a f -> p (a f)"), psum_bank[4 + b]).then_inc(edge_window_copied, 1)
            a.wait_ge(first_linear_done, R_L2 + NT)
            attr_hi(0, 0)
            attr_hi(0, 1)
            a.wait_ge(table_rows_ready, NT)
            window_loop(a, edges_hi)
            window_copy(NT - 1, 1)
            a.wait_ge(one_plus_eps_ready, 1)
            scaled_x3(0)
            general = a.value_load(flag[0:1, 0:1], min_val=0, max_val=ET * P)
            with a.If(general > ET * P - N_EDGES):
                with a.Fori(0, NT) as d:
                    with a.Fori(0, ET) as t:
                        a.wait_ge(edge_attr_arrived[0], GEN_EA + (d * ET + t) * 16 + 16)
                        nc.scalar.copy(edge_attr_split[:, 0, 0, 0:P], edge_attr_raw[:, 0, 0:P]).then_inc(edge_attr_hi, 1)
                        a.wait_ge(edge_z_ready, GEN_T + d * ET + t + 1)
                        nc.scalar.activation(messages[:, 0, 0], edge_z[:, 0], ACT.Relu).then_inc(message_hi, 1)
                    a.wait_ge(edge_window_done, GEN_W + d + 1)
                    nc.scalar.copy(edge_sums[:, bass.ds(d, 1)].rearrange("p a f -> p (a f)"), psum_bank[4]).then_inc(edge_window_copied, 1)
                a.nop()
            with a.Else():
                a.nop()
            a.nop()

            def s4_hi(n):
                need(a, node_rows_transposed, n + 1, T_MLP1)
                nc.scalar.copy(split4[:, 0], psum_bank[0]).then_inc(rows_hi, 1)

            def s8_hi(n):
                need(a, hidden_rows_transposed, n + 1, HT_MLP1)
                need(a, second_linear_done, n, HT_MLP1)
                nc.scalar.copy(split8[:, 0], psum_all[:, 1:3].rearrange("p a f -> p (a f)")).then_inc(hidden_hi, 1)

            def nodes(q, at):
                if at + 1 < 2 * NT:
                    s4_hi(q + 1)
                if at + 2 < NT:
                    scaled_x3(q + 2)
                if NT <= at < 2 * NT:
                    need(a, first_linear_done, q + 1, R_MLP1)
                    need(a, hidden_rows_transposed, q, HT_MLP1)
                    nc.scalar.activation(y1_or_m[:], psum_all[:, 3:5].rearrange("p a f -> p (a f)"), ACT.Gelu).then_inc(y1_gelu, 1)
                if 1 <= at <= 2 * NT:
                    s8_hi(q - 1)
                if at < NT:
                    need(a, y1_normed, q + 1)
                    nc.scalar.activation(y1_or_m[:], y1_or_m[:], ACT.Gelu).then_inc(y1_gelu, 1)
                if at < NT - 2:
                    w3_hi(q + 24)
                if 2 <= at < NT + 2:
                    need(a, normed, q - 1)
                    nc.scalar.activation(y2_or_y[:], y2_or_y[:], ACT.Gelu).then_inc(y2_gelu, 1)
            s4_hi(0)
            scaled_x3(1)
            node_loop(a, nodes)

        @block.vector
        def _(v):
            v.wait_ge(iota_int_ready, 1)
            nc.vector.tensor_copy(iota_nodes[:], iota_int[:]).then_inc(dve_setup, 1)
            v.wait_ge(edges_loaded, 32)
            nc.vector.tensor_copy(dst_f32[:], dst_int[:]).then_inc(dve_setup, 1)
            nc.vector.tensor_copy(src_f32[:], src_index[:]).then_inc(dve_setup, 1)
            def violations():
                v.wait_ge(bounds_ready, 4)
                nc.vector.tensor_copy(bounds_f32[:], bounds[:].rearrange("p a d t -> p a (d t)")).then_inc(bounds_f32_ready, 1)
                v.wait_ge(bounds_f32_ready, 1)
                v.wait_ge(dve_setup, 3)
                nc.vector.tensor_tensor(violation_flags[:, 0, :], dst_f32[:], bounds_f32[:, 0, :], ALU.is_lt)
                nc.vector.tensor_tensor(violation_flags[:, 1, :], dst_f32[:], bounds_f32[:, 1, :], ALU.is_ge).then_inc(dve_setup, 1)
                v.wait_ge(dve_setup, 4)
                nc.vector.tensor_reduce(violation_sums[:, 0:1], violation_flags[:], axis=AX.XY, op=ALU.add).then_inc(violations_ready, 1)

            def onehots(j):
                for r in range(2 * EPW):
                    t = 2 * EPW * j + r
                    need(v, onehots_used, t - 3)
                    nc.vector.tensor_scalar(onehot_src[:, r % 4, :], iota_nodes[:], src_f32[:, bass.ds(t, 1)], None, ALU.is_equal)
                    ws = shifts(j, r)
                    last = nc.vector.tensor_scalar(onehot_dst[:, r % 4, 0:len(ws)].rearrange("p a f -> p (a f)"),
                                                   iota_nodes[:, bass.ds((2 * j + ws[0]) * P, len(ws) * P)],
                                                   dst_f32[:, bass.ds(t, 1)], None, ALU.is_equal)
                    last.then_inc(onehots_ready, 1)
                if isinstance(j, int) and j == 0:
                    violations()
            v.wait_ge(dve_setup, 3)
            window_loop(v, onehots)

            v.wait_ge(w_loaded, 16)
            v.wait_ge(weights_hi, 1)
            nc.vector.tensor_tensor(w0_lo[:], w_stage[:], w0_hi[:].bitcast(F32), ALU.subtract).then_inc(weights_split, 1)
            v.wait_ge(constants, 7)
            nc.vector.tensor_copy(ident_r[:], ident[:]).then_inc(identity_r_ready, 1)
            nc.vector.tensor_copy(ones_r[:], ones[:]).then_inc(ones_r_ready, 1)
            v.wait_ge(violations_summed, 1)
            nc.vector.tensor_copy(flag[0:1, 0:1], psum_bank[7][0:1, 0:1]).then_inc(flag_ready, 1)
            v.wait_ge(flag_ready, 1)
            general = v.value_load(flag[0:1, 0:1], min_val=0, max_val=ET * P)
            with v.If(general > ET * P - N_EDGES):
                v.wait_ge(window_done, NT)
                with v.Fori(0, NT) as d:
                    with v.Fori(0, ET) as t:
                        v.wait_ge(onehots_used, GEN_U + d * ET + t)
                        nc.vector.tensor_scalar(onehot_src[:, 0, :], iota_nodes[:], src_f32[:, bass.ds(t, 1)], None, ALU.is_equal)
                        nc.vector.tensor_scalar(onehot_dst[:, 0, 0, :], iota_nodes[:, bass.ds(d * P, P)], dst_f32[:, bass.ds(t, 1)],
                                                None, ALU.is_equal).then_inc(onehots_ready, 1)
                v.nop()
            with v.Else():
                v.nop()
            v.nop()

            def transposed(n, b):
                need(v, adj_transposed, 3 * n + 3)
                nc.vector.tensor_copy(adj_src_dst[:, 4:8, bass.ds(n * P, P)],
                                      psum_bank[3 * b + 1].rearrange("p (k c) -> p k c", k=4))
                nc.vector.tensor_copy(adj_src_dst[:, 8:10, bass.ds(n * P, P)],
                                      psum_bank[3 * b + 2][:, 0:256].rearrange("p (k c) -> p k c", k=2)).then_inc(adj_copied_dve, 1)
            tile_loop(v, transposed)
            v.wait_ge(deg_src_columns, 1)
            nc.vector.tensor_scalar(deg_src[:], psum_bank[7][:, 0:NT], 1.0, None, ALU.add).then_inc(deg_src_plus1, 1)
            v.wait_ge(bias0_loaded, 16)

            def l0(n, b):
                need(v, rows_hi, n + 1)
                nc.vector.tensor_tensor(x_split[:, b, 1, :], psum_bank[6 + b], x_split[:, b, 0, :].bitcast(F32),
                                        ALU.subtract).then_inc(rows_split, 1)
                if not (isinstance(n, int) and n == 0):
                    feat(n - 1, 1 - b)

            def feat(n, b):
                need(v, first_linear_done, n + 1)
                need(v, features_ready, n - 1)
                nc.vector.tensor_tensor(resid_rows[:, b, :], psum_bank[2 + b], bias_row0[:], ALU.add).then_inc(l0_resid_ready, 1)
                need(v, l0_resid_ready, n + 1)
                if isinstance(n, int) and n == 0:
                    v.wait_ge(deg_inv_sqrt_ready, 1)
                nc.vector.tensor_scalar(feat_rows[:, b, :], resid_rows[:, b, :], deg_inv_sqrt[:, bass.ds(n, 1)], None,
                                        ALU.mult).then_inc(l0_feat_ready, 1)
                need(v, features_hi, n + 1)
                nc.vector.tensor_tensor(g1_lo[:, bass.ds(n, 1), :].rearrange("p a f -> p (a f)"), feat_rows[:, b, :],
                                        g1_hi[:, bass.ds(n, 1), :].rearrange("p a f -> p (a f)").bitcast(F32),
                                        ALU.subtract).then_inc(features_ready, 1)
            tile_loop(v, l0)
            feat(NT - 1, 1)

            def resid(n, b):
                need(v, aggregated, n + 1)
                xn = x_nodes[:, bass.ds(n, 1), :].rearrange("p a f -> p (a f)")
                need(v, layer_output_ready, n - 1)
                nc.vector.scalar_tensor_tensor(resid_rows[:, b, :], psum_bank[4 + b], deg_inv_sqrt[:, bass.ds(n, 1)], xn,
                                               ALU.mult, ALU.add).then_inc(l0_resid_ready, 1)
                need(v, l0_resid_ready, NT + n + 1)
                nc.vector.bn_stats(stats_of_rows[:, b, 0, :], resid_rows[:, b, :]).then_inc(norm_stats, 1)
                need(v, norm_stats, n + 1)
                v.sem_inc(fence, 1)
                nc.vector.bn_aggr(bn_mean_var[:, b, :], stats_of_rows[:, b, 0, :]).then_inc(norm_var, 1)
                nc.vector.tensor_reduce(deg_dst[:, bass.ds(n, 1)], adj_dst_src[:, bass.ds(n, 1)].bitcast(F32), axis=AX.X,
                                        op=ALU.add).then_inc(degrees_ready, 1)
                if not (isinstance(n, int) and n == 0):
                    norm(n - 1, 1 - b)

            def norm(n, b):
                xn = x_nodes[:, bass.ds(n, 1), :].rearrange("p a f -> p (a f)")
                need(v, norm_rstd, n + 1)
                nc.vector.tensor_scalar(xn, resid_rows[:, b, :], bn_mean_var[:, b, 0:1], rstd_of_rows[:, b, 1:2], ALU.subtract,
                                        ALU.mult).then_inc(layer_output_ready, 1)
            tile_loop(v, resid)
            norm(NT - 1, 1)

            v.wait_ge(degrees_ready, NT)
            nc.vector.tensor_scalar(deg_dst[:], deg_dst[:], 1.0, None, ALU.max).then_inc(degrees_ready, 1)
            v.wait_ge(degrees_ready, NT + 1)
            nc.vector.reciprocal(deg_inv[:], deg_dst[:]).then_inc(degrees_ready, 1)

            v.wait_ge(aggregated, NT)
            v.wait_ge(layer_output_ready, NT)
            def x1_lo(n, b):
                need(v, features_hi, n + 1, F_L1)
                nc.vector.tensor_tensor(g1_lo[:, bass.ds(n, 1), :].rearrange("p a f -> p (a f)"),
                                        x_nodes[:, bass.ds(n, 1), :].rearrange("p a f -> p (a f)"),
                                        g1_hi[:, bass.ds(n, 1), :].rearrange("p a f -> p (a f)").bitcast(F32),
                                        ALU.subtract).then_inc(features_ready, 1)
            tile_loop(v, x1_lo)

            v.wait_ge(gate_loaded, 32)
            v.wait_ge(l1_logits_done, NT)
            v.wait_ge(l1_xt_ready, NT)
            wide = [P, NT, NE]
            nc.vector.tensor_tensor(gate_logits[:], psum_bank[7][:, 0:NT * NE].rearrange("p (n e) -> p n e", e=NE),
                                    gate_bias_row[:].unsqueeze(1).to_broadcast(wide), ALU.add).then_inc(gate_chain, 1)
            v.wait_ge(gate_chain, 1)
            nc.vector.tensor_reduce(gate_max[:, 0], gate_logits[:], axis=AX.X, op=ALU.max).then_inc(gate_chain, 1)
            v.wait_ge(gate_chain, 2)
            nc.vector.tensor_tensor(gate_logits[:], gate_logits[:], gate_max[:, 0].unsqueeze(2).to_broadcast(wide), ALU.subtract).then_inc(gate_chain, 1)
            v.wait_ge(gate_exp_ready, 1)
            nc.vector.tensor_reduce(gate_max[:, 0], gate_exp[:], axis=AX.X, op=ALU.add).then_inc(gate_chain, 1)
            v.wait_ge(gate_chain, 4)
            nc.vector.reciprocal(gate_max[:, 1], gate_max[:, 0]).then_inc(gate_chain, 1)
            v.wait_ge(gate_chain, 5)
            nc.vector.tensor_tensor(gate_values[:], gate_exp[:], gate_max[:, 1].unsqueeze(2).to_broadcast(wide), ALU.mult).then_inc(gate_chain, 1)
            v.wait_ge(gate_chain, 6)
            steps = 6
            nc.vector.memset(gate_logits[:], 0.0).then_inc(gate_chain, 1)
            steps += 1
            for e in range(NE):
                for j in range(NE):
                    if j == e:
                        continue
                    v.wait_ge(gate_chain, steps)
                    nc.vector.tensor_tensor(gate_exp[:, :, 0:1], gate_values[:, :, j:j + 1], gate_values[:, :, e:e + 1],
                                            ALU.is_ge if j < e else ALU.is_gt).then_inc(gate_chain, 1)
                    v.wait_ge(gate_chain, steps + 1)
                    nc.vector.tensor_tensor(gate_logits[:, :, e:e + 1], gate_logits[:, :, e:e + 1], gate_exp[:, :, 0:1], ALU.add).then_inc(gate_chain, 1)
                    steps += 2
            v.wait_ge(gate_chain, steps)
            nc.vector.scalar_tensor_tensor(gate_weights[:], gate_logits[:], 1.5, gate_values[:], ALU.is_lt, ALU.mult).then_inc(gate_weights_ready, 1)

            def first_weights_lo(e):
                for i in (0, 1):
                    v.wait_ge(expert_w_first_hi, 2 * e + i + 1)
                    nc.vector.tensor_tensor(w_first[:, i, 1], w_stage2[:, i], w_first[:, i, 0].bitcast(F32), ALU.subtract).then_inc(expert_w_first_ready, 1)

            first_weights_lo(0)

            def xa_lo(m, n):
                need(v, rows_hi, m + 1, R_EX)
                nc.vector.tensor_tensor(x_agg_split[:, 0, 1], x1_t[:, bass.ds(n, 1), :].rearrange("p a f -> p (a f)"),
                                        x_agg_split[:, 0, 0].bitcast(F32), ALU.subtract)
                nc.vector.tensor_tensor(x_agg_split[:, 1, 1], agg1_transposed[:, bass.ds(n, 1), :].rearrange("p a f -> p (a f)"),
                                        x_agg_split[:, 1, 0].bitcast(F32), ALU.subtract).then_inc(rows_split, 1)

            def l1_at(n, b):
                if isinstance(n, int) and n == NT - 1:
                    xa_lo(0, 0)
                need(v, l1_agg_transposed, n + 1)
                nc.vector.tensor_copy(agg1_transposed[:, bass.ds(n, 1), :].rearrange("p a f -> p (a f)"), psum_bank[4 + b]).then_inc(l1_at_ready, 1)
            tile_loop(v, l1_at)

            def second_weights_lo(e):
                for i in (0, 1):
                    v.wait_ge(expert_w_second_hi, 2 * e + i + 1)
                    nc.vector.tensor_tensor(w_second[:, i, 1], w_stage2[:, i], w_second[:, i, 0].bitcast(F32), ALU.subtract).then_inc(expert_w_second_ready, 1)

            def hT_lo(m):
                need(v, hidden_hi, m + 1)
                nc.vector.scalar_tensor_tensor(h_transposed[:, 1], psum_bank[2], 0.0, h_transposed[:, 0].bitcast(F32), ALU.max,
                                               ALU.subtract).then_inc(hidden_split, 1)

            def h_biased(m):
                need(v, first_linear_done, m + 1, R_EX)
                need(v, hidden_rows_transposed, m)
                nc.vector.tensor_tensor(h_nodes[:], psum_bank[0], bias1_first[:], ALU.add).then_inc(ex_h_ready, 1)

            def g_lo_and_r(m):
                need(v, second_linear_done, m + 1)
                need(v, r_stored, 16 * m)
                nc.vector.tensor_tensor(r_out[:], psum_bank[5], bias1_second[:], ALU.add).then_inc(ex_r_ready, 1)

            def expert(e, final):
                with v.Fori(1, NT - 1) as n:
                    m = e * NT + n
                    hT_lo(m - 1)
                    h_biased(m)
                    xa_lo(m + 1, n + 1)
                    g_lo_and_r(m - 1)
                m = e * NT + NT - 1
                hT_lo(m - 1)
                h_biased(m)
                if not final:
                    xa_lo(m + 1, 0)
                    first_weights_lo(e + 1)
                g_lo_and_r(m - 1)
                if not final:
                    hT_lo(m)
                    v.wait_ge(expert_bias_first_loaded, 16 * (e + 2))
                    h_biased(m + 1)
                    xa_lo(m + 2, 1)
                    g_lo_and_r(m)
                    second_weights_lo(e + 1)
                    v.wait_ge(expert_bias_second_loaded, 16 * (e + 2))

            def gather_lo(e, k):
                G, R = ((g2, g2_raw), (g1_again, g1_raw))[e % 2]
                v.wait_ge(features_hi, F_GA + e * NT + k + 1)
                nc.vector.tensor_tensor(G[:, 1, k], R[:, 1, k], G[:, 0, k].bitcast(F32), ALU.subtract).then_inc(features_ready, 1)

            second_weights_lo(0)
            v.wait_ge(expert_bias_first_loaded, 16)
            v.wait_ge(expert_bias_second_loaded, 16)
            h_biased(0)
            xa_lo(1, 1)
            with v.Fori(0, NE - 1) as e:
                expert(e, False)
            expert(NE - 1, True)
            hT_lo(NE * NT - 1)
            for k in range(NT):
                gather_lo(0, k)
            g_lo_and_r(NE * NT - 1)

            def scaled(m, e, n, b):
                need(v, aggregated, m + 1, A_EX)
                need(v, gather_gated, m - 1)
                k = (0 if isinstance(n, int) and n < 5 else 1)
                nc.vector.scalar_tensor_tensor(gated_rows[:, 0, b], psum_bank[b], deg_inv[:, n:n + 1], r_ring[:, n % 5], ALU.mult,
                                               ALU.add).then_inc(gather_scaled, 1)

            def added(m, n, b):
                v.wait_ge(gather_gated, m + 1)
                if m < 2 * NT:
                    v.wait_ge(x1_added_done, n + 1)
                else:
                    v.wait_ge(gather_added, m - 2 * NT + 1)
                nc.vector.tensor_tensor(gated_sum[:, n, :], gated_sum[:, n, :], gated_rows[:, 1, b], ALU.add).then_inc(gather_added, 1)

            def x1_stats(n):
                b = n % 2
                v.wait_ge(gather_added, (NE - 2) * NT + n + 1)
                nc.vector.bn_stats(stats_of_rows[:, b, 0, :], gated_sum[:, n, :]).then_inc(norm_stats, 1)
                v.wait_ge(norm_stats, N_L1 + n + 1)
                nc.vector.bn_aggr(bn_mean_var[:, b, :], stats_of_rows[:, b, 0, :]).then_inc(norm_var, 1)

            def x2_norm(n):
                b = n % 2
                v.wait_ge(norm_rstd, N_L1 + n + 1)
                nc.vector.tensor_scalar(x_nodes[:, n, :], gated_sum[:, n, :], bn_mean_var[:, b, 0:1], rstd_of_rows[:, b, 1:2], ALU.subtract,
                                        ALU.mult).then_inc(layer_output_ready, 1)

            def x2_lo(n):
                v.wait_ge(features_hi, F_L2 + n + 1)
                nc.vector.tensor_tensor(g2[:, 1, n], x_nodes[:, n, :], g2[:, 0, n].bitcast(F32), ALU.subtract).then_inc(features_ready, 1)
            for e in range(NE):
                if e == 2:
                    v.wait_ge(weights_hi, W_L2 + 1)
                    nc.vector.tensor_tensor(w_first[:, :, 1], w2_raw[:, :, 1], w_first[:, :, 0].bitcast(F32),
                                            ALU.subtract).then_inc(weights_split, 1)
                for n in range(NT):
                    m = e * NT + n
                    v.wait_ge(r_arrived[n % 5], 16 * (2 * e + n // 5 + 1))
                    scaled(m, e, n, n % 2)
                    if e + 1 < NE and n >= NT // 2:
                        gather_lo(e + 1, 2 * n - NT)
                        gather_lo(e + 1, 2 * n - NT + 1)
                    if m > NT:
                        added(m - 1, (n - 1) % NT, (n - 1) % 2)
                    if e == NE - 1 and n >= 1:
                        x1_stats(n - 1)
                    if e == NE - 1 and n >= 2:
                        x2_norm(n - 2)
                    if e == NE - 1 and n >= 3:
                        x2_lo(n - 3)

            added(NE * NT - 1, NT - 1, 1)
            x1_stats(NT - 1)
            x2_norm(NT - 2)
            x2_lo(NT - 3)
            x2_norm(NT - 1)
            x2_lo(NT - 2)
            x2_lo(NT - 1)

            v.wait_ge(eps_loaded, 16)
            nc.vector.tensor_scalar(one_plus_eps[:, 1:2], one_plus_eps[:, 0:1], 1.0, None, ALU.add).then_inc(one_plus_eps_ready, 1)
            v.wait_ge(iota3_int, 1)
            nc.vector.tensor_copy(iota_nodes[:], iota_int3[:]).then_inc(iota3_ready, 1)
            v.wait_ge(weights_hi, W_EDGE + 1)
            nc.vector.tensor_tensor(w_edge_split[:, 1], w_edge_raw[:, 1], w_edge_split[:, 0].bitcast(F32), ALU.subtract).then_inc(weights_split, 1)

            v.wait_ge(l2_vectors_loaded, 48)

            def l2_split(n, b):
                need(v, rows_hi, n + 1, R_L2)
                nc.vector.tensor_tensor(x_agg_split2[:, 0, 1], psum_bank[0], x_agg_split2[:, 0, 0].bitcast(F32), ALU.subtract)
                nc.vector.tensor_tensor(x_agg_split2[:, 1, 1], psum_bank[1], x_agg_split2[:, 1, 0].bitcast(F32), ALU.subtract).then_inc(rows_split, 1)
                if not (isinstance(n, int) and n == 0):
                    l2_bias_stats(n - 1, 1 - b)
                if not (isinstance(n, int) and n < 2):
                    l2_norm(n - 2, b)
                if not (isinstance(n, int) and n == 0):
                    l2_affine(n - 1, 1 - b)

            def l2_bias_stats(n, b):
                need(v, first_linear_done, n + 1, R_L2)
                nc.vector.tensor_tensor(y2[:, b], psum_bank[4 + b], bias_gamma_beta2[:, 0], ALU.add).then_inc(linear_biased, 1)
                need(v, linear_biased, n + 1)
                nc.vector.bn_stats(stats_of_rows[:, b, 0, :], y2[:, b]).then_inc(norm_stats, 1)
                need(v, norm_stats, n + 1, N_L2)
                v.sem_inc(fence, 1)
                nc.vector.bn_aggr(bn_mean_var[:, b, :], stats_of_rows[:, b, 0, :]).then_inc(norm_var, 1)

            def l2_affine(n, b):
                xn = x_nodes[:, bass.ds(n, 1), :].rearrange("p a f -> p (a f)")
                need(v, norm_rstd, n + 1, N_L2)
                nc.vector.scalar_tensor_tensor(z2[:, b], y2[:, b], bn_mean_var[:, b, 0:1], bias_gamma_beta2[:, 1], ALU.subtract,
                                               ALU.mult).then_inc(l2_dve_steps, 1)
                need(v, l2_dve_steps, 3 * n + 1)
                nc.vector.scalar_tensor_tensor(z2[:, b], z2[:, b], rstd_of_rows[:, b, 1:2], bias_gamma_beta2[:, 2], ALU.mult,
                                               ALU.add).then_inc(l2_dve_steps, 1)
                need(v, l2_dve_steps, 3 * n + 2)
                nc.vector.tensor_tensor(z2[:, b], z2[:, b], xn, ALU.add).then_inc(l2_dve_steps, 1)
                need(v, l2_dve_steps, 3 * n + 3)
                nc.vector.bn_stats(stats_of_rows[:, b, 1, :], z2[:, b]).then_inc(outer_stats_done, 1)
                need(v, outer_stats_done, n + 1)
                v.sem_inc(fence, 1)
                nc.vector.bn_aggr(outer_mean_var[:, b, :], stats_of_rows[:, b, 1, :]).then_inc(outer_var, 1)

            def l2_norm(n, b):
                xn = x_nodes[:, bass.ds(n, 1), :].rearrange("p a f -> p (a f)")
                need(v, outer_rstd_done, n + 1)
                nc.vector.tensor_scalar(xn, z2[:, b], outer_mean_var[:, b, 0:1], outer_rstd[:, b, 1:2], ALU.subtract,
                                        ALU.mult).then_inc(layer_output_ready, 1)
            tile_loop(v, l2_split)
            l2_bias_stats(NT - 1, 1)
            l2_norm(NT - 2, 0)
            l2_affine(NT - 1, 1)
            l2_norm(NT - 1, 1)

            v.wait_ge(iota3_ready, 1)
            v.wait_ge(x3_stored, 16 * NT)
            v.wait_ge(table_rows_ready, NT)

            def w3_lo(q):
                need(v, weights_hi, q + 1, W_MLP)
                flat = lambda ap: ap.rearrange("p k f -> p (k f)")
                nc.vector.tensor_tensor(flat(w3_lower[:, bass.ds(q, 1)]), flat(w3_raw[:, bass.ds(q, 1)]),
                                        flat(w3_upper[:, bass.ds(q, 1)]).bitcast(F32), ALU.subtract).then_inc(weights_split, 1)

            def message_lo(t, b):
                need(v, message_hi, t + 1)
                nc.vector.scalar_tensor_tensor(messages[:, b, 1], edge_z[:, b], 0.0, messages[:, b, 0].bitcast(F32), ALU.max,
                                               ALU.subtract).then_inc(message_ready, 1)

            def edges_lo(j):
                for r in range(2 * EPW):
                    t = 2 * EPW * j + r
                    need(v, message_summed, t - 3)
                    ws = shifts(j, r)
                    nc.vector.tensor_scalar(onehot_dst_r[:, r % 4, 0:len(ws)].rearrange("p a f -> p (a f)"),
                                            iota_nodes[:, bass.ds((2 * j + ws[0]) * P, len(ws) * P)], dst_f32[:, bass.ds(t, 1)],
                                            None, ALU.is_equal)
                    v.wait_ge(rows_gathered[r % 8], 16 * (4 * j + r // 8 + 1))
                    need(v, edge_embedded, t + 1)
                    if whole(r - 2):
                        need(v, message_hi, t - 1)
                    else:
                        need(v, message_ready, splits(j, r - 2))
                    nc.vector.tensor_tensor(edge_z[:, r % 2], psum_bank[r % 4], gathered(r), ALU.add).then_inc(edge_z_ready, 1)
                    if not (isinstance(j, int) and t == 0) and not whole(r - 1):
                        message_lo(t - 1, (r + 1) % 2)
                    if r % 4 == 3 and not isinstance(j, int):
                        w3_lo(8 * (j - 1) + r // 4)
            window_loop(v, edges_lo)
            message_lo(ET - 1, 1)

            v.wait_ge(edge_window_copied, NT)
            general = v.value_load(flag[0:1, 0:1], min_val=0, max_val=ET * P)
            with v.If(general > ET * P - N_EDGES):
                with v.Fori(0, NT) as d:
                    with v.Fori(0, ET) as t:
                        v.wait_ge(edge_attr_hi, GEN_G + d * ET + t + 1)
                        nc.vector.tensor_tensor(edge_attr_split[:, 0, 1, 0:P], edge_attr_raw[:, 0, 0:P], edge_attr_split[:, 0, 0, 0:P].bitcast(F32),
                                                ALU.subtract)
                        nc.vector.tensor_scalar(onehot_dst_r[:, 0, 0], iota_nodes[:, bass.ds(d * P, P)], dst_f32[:, bass.ds(t, 1)], None,
                                                ALU.is_equal).then_inc(edge_attr_ready, 1)
                        v.wait_ge(rows_gathered[0], GEN_GA + (d * ET + t) * 16 + 16)
                        v.wait_ge(edge_embedded, GEN_T + d * ET + t + 1)
                        nc.vector.tensor_tensor(edge_z[:, 0], psum_bank[0], gathered_rows[:, 0], ALU.add).then_inc(edge_z_ready, 1)
                        v.wait_ge(message_hi, GEN_T + d * ET + t + 1)
                        nc.vector.scalar_tensor_tensor(messages[:, 0, 1], edge_z[:, 0], 0.0, messages[:, 0, 0].bitcast(F32), ALU.max,
                                                       ALU.subtract).then_inc(message_ready, 1)
                v.wait_ge(edge_window_copied, GEN_W + NT)
                v.nop()
            with v.Else():
                v.nop()
            v.nop()

            def tile_of(t, n):
                return t[:, bass.ds(n, 1)].rearrange("p a f -> p (a f)")

            def s4_lo(n):
                need(v, rows_hi, n + 1, R_MLP1)
                nc.vector.tensor_tensor(split4[:, 1], psum_bank[0], split4[:, 0].bitcast(F32), ALU.subtract).then_inc(rows_split, 1)

            def s8_lo(n):
                need(v, hidden_hi, n + 1, HT_MLP1)
                nc.vector.tensor_tensor(split8[:, 1], psum_all[:, 1:3].rearrange("p a f -> p (a f)"), split8[:, 0].bitcast(F32),
                                        ALU.subtract).then_inc(hidden_split, 1)

            def y1_bias(n):
                need(v, first_linear_done, n + 1, R_MLP1)
                need(v, hidden_rows_transposed, n, HT_MLP1)
                nc.vector.tensor_tensor(y1_or_m[:], psum_all[:, 3:5].rearrange("p a f -> p (a f)"), bias1_gamma1[:, 0], ALU.add).then_inc(y1_biased, 1)

            def y1_stats(n):
                need(v, y1_biased, n + 1)
                nc.vector.bn_stats(bn_stats1[:, 0, :], y1_or_m[:, 0:D])
                nc.vector.bn_stats(bn_stats1[:, 1, :], y1_or_m[:, D:]).then_inc(y1_stats_done, 1)
                need(v, y1_stats_done, n + 1)
                v.sem_inc(fence, 1)
                nc.vector.bn_aggr(bn_mean_var1[:], bn_stats1[:].rearrange("p a f -> p (a f)")).then_inc(y1_var, 1)

            def y1_norm(n):
                need(v, y1_rstd, n + 1)
                nc.vector.scalar_tensor_tensor(y1_or_m[:], y1_or_m[:], bn_mean_var1[:, 0:1], bias1_gamma1[:, 1], ALU.subtract,
                                               ALU.mult).then_inc(y1_gamma, 1)
                need(v, y1_gamma, n + 1)
                nc.vector.scalar_tensor_tensor(y1_or_m[:], y1_or_m[:], rstd1[:, 1:2], beta1[:], ALU.mult,
                                               ALU.add).then_inc(y1_normed, 1)

            def own_stats(i):
                need(v, linear_biased, i + 1, B_MLP1)
                nc.vector.bn_stats(stats_of_rows[:, 0, 0, :], y2_or_y[:]).then_inc(norm_stats, 1)
                need(v, norm_stats, i + 1, N_MLP1)
                v.sem_inc(fence, 1)
                nc.vector.bn_aggr(bn_mean_var[:, 0, :], stats_of_rows[:, 0, 0, :]).then_inc(norm_var, 1)

            def outer_stats(i, row):
                need(v, residual_added, i + 1)
                nc.vector.bn_stats(stats_of_rows[:, 0, 1, :], row).then_inc(outer_stats_done, 1)
                need(v, outer_stats_done, i + 1, O_MLP1)
                v.sem_inc(fence, 1)
                nc.vector.bn_aggr(outer_mean_var[:, 0, :], stats_of_rows[:, 0, 1, :]).then_inc(outer_var, 1)

            def affine(i, gamma_row, beta_row):
                need(v, norm_rstd, i + 1, N_MLP1)
                nc.vector.scalar_tensor_tensor(y2_or_y[:], y2_or_y[:], bn_mean_var[:, 0, 0:1], gamma_row, ALU.subtract,
                                               ALU.mult).then_inc(times_gamma, 1)
                need(v, times_gamma, i + 1)
                nc.vector.scalar_tensor_tensor(y2_or_y[:], y2_or_y[:], rstd_of_rows[:, 0, 1:2], beta_row, ALU.mult,
                                               ALU.add).then_inc(normed, 1)

            def y2_stats(n):
                need(v, second_linear_done, n + 1, HT_MLP1)
                need(v, residual_added, n)
                nc.vector.tensor_tensor(y2_or_y[:], psum_bank[5], vectors2_first[:, 0], ALU.add).then_inc(linear_biased, 1)
                own_stats(n)

            def h4(n):
                need(v, outer_rstd_done, n + 1, O_MLP1)
                nc.vector.scalar_tensor_tensor(x3_plus_y2[:], x3_plus_y2[:], outer_mean_var[:, 0, 0:1], vectors2_first[:, 3], ALU.subtract,
                                               ALU.mult).then_inc(residual_gamma, 1)
                need(v, residual_gamma, n + 1)
                nc.vector.scalar_tensor_tensor(tile_of(edge_sums, n), x3_plus_y2[:], outer_rstd[:, 0, 1:2], vectors2_last[:, 0], ALU.mult,
                                               ALU.add).then_inc(layer_output_ready, 1)

            def y_stats(i):
                need(v, second_linear_done, i + 1, HT_MLP1)
                if not (isinstance(i, int) and i == NT):
                    need(v, layer_output_ready, i, N_MLP1)
                nc.vector.tensor_tensor(y2_or_y[:], psum_bank[5], tile_of(edge_sums, i - NT), ALU.add).then_inc(linear_biased, 1)
                own_stats(i)

            def y_out(i):
                affine(i, vectors2_last[:, 1], vectors2_last[:, 2])
                need(v, normed, i + 1)
                need(v, x3_for_residual_loaded, 16 * (i + 1))
                nc.vector.tensor_tensor(y2_or_y[:], y2_or_y[:], x3_for_residual[:], ALU.add).then_inc(residual_added, 1)
                outer_stats(i, y2_or_y[:])
                need(v, outer_rstd_done, i + 1, O_MLP1)
                need(v, out_tile_stored, 16 * (i - NT))
                nc.vector.tensor_scalar(out_tile[:], y2_or_y[:], outer_mean_var[:, 0, 0:1], outer_rstd[:, 0, 1:2], ALU.subtract,
                                        ALU.mult).then_inc(layer_output_ready, 1)

            def nodes(q, at):
                if at < NT:
                    y1_bias(q)
                if at + 1 < 2 * NT:
                    s4_lo(q + 1)
                if at < NT:
                    y1_stats(q)
                if 3 <= at < NT + 3:
                    outer_stats(q - 3, x3_plus_y2[:])
                if at == 2:
                    v.wait_ge(vectors2_first_loaded, 64)
                    v.wait_ge(vectors2_last_loaded, 48)
                if 2 <= at < NT + 2:
                    y2_stats(q - 2)
                if at >= NT + 2:
                    y_stats(q - 2)
                if 1 <= at <= 2 * NT:
                    s8_lo(q - 1)
                if at < NT:
                    y1_norm(q)
                if 3 <= at < NT + 3:
                    h4(q - 3)
                if 2 <= at < NT + 2:
                    affine(q - 2, vectors2_first[:, 1], vectors2_first[:, 2])
                if at >= NT + 2:
                    y_out(q - 2)
            s4_lo(0)
            v.wait_ge(vectors1_loaded, 32)
            v.wait_ge(beta1_loaded, 16)
            node_loop(v, nodes)

        @block.tensor
        def _(pe):
            pe.wait_ge(constants, 7)

            def windows(j):
                if isinstance(j, int) and j == NT // 2 - 1:
                    pe.wait_ge(violations_ready, 1)
                    nc.tensor.matmul(psum_bank[7][0:1, 0:1], ones[:, 0:1], violation_sums[:, 0:1], start=True, stop=True).then_inc(violations_summed, 1)
                for r in range(2 * EPW):
                    t = 2 * EPW * j + r
                    need(pe, onehots_ready, t + 1)
                    for i, s in enumerate(shifts(j, r)):
                        first, final = opens(j, r, s), closes(j, r, s)
                        if first:
                            need(pe, window_copied, 2 * j + s - 1)
                        for c, w in ((0, 512), (1, 512), (2, 256)):
                            last = nc.tensor.matmul(psum_bank[3 * (s % 2) + c][:, 0:w], onehot_dst[:, r % 4, i, :],
                                                    onehot_src[:, r % 4, 512 * c:512 * c + w], start=first, stop=final)
                        if final:
                            last.then_inc(window_done, 1)
                    if not final:
                        last.then_inc(onehots_used, 1)
            window_loop(pe, windows)

            pe.wait_ge(flag_ready, 1)
            pe.wait_ge(window_copied, NT)
            general = pe.value_load(flag[0:1, 0:1], min_val=0, max_val=ET * P)
            with pe.If(general > ET * P - N_EDGES):
                with pe.Fori(0, NT) as d:
                    pe.wait_ge(window_copied, GEN_W + d)
                    for c, w in ((0, 512), (1, 512), (2, 256)):
                        nc.tensor.matmul(psum_bank[c][:, 0:w], zeros[:], iota_nodes[:, 512 * c:512 * c + w], start=True, stop=False)
                    with pe.Fori(0, ET) as t:
                        pe.wait_ge(onehots_ready, GEN_T + d * ET + t + 1)
                        for c, w in ((0, 512), (1, 512), (2, 256)):
                            last = nc.tensor.matmul(psum_bank[c][:, 0:w], onehot_dst[:, 0, 0, :], onehot_src[:, 0, 512 * c:512 * c + w],
                                                    start=False, stop=False)
                        last.then_inc(onehots_used, 1)
                    for c, w in ((0, 512), (1, 512), (2, 256)):
                        last = nc.tensor.matmul(psum_bank[c][:, 0:w], zeros[:], iota_nodes[:, 512 * c:512 * c + w], start=False, stop=True)
                    last.then_inc(window_done, 1)
                pe.wait_ge(window_copied, GEN_W + NT)
                pe.nop()
            with pe.Else():
                pe.nop()
            pe.nop()

            pe.wait_ge(ones_r_ready, 1)
            for c, w in ((0, 512), (1, 512), (2, 256)):
                for d in range(NT):
                    last = nc.tensor.matmul(psum_bank[3 + c][0:2, 0:w], ones_r[:], adj_dst_src[:, d, 512 * c:512 * c + w],
                                            start=d == 0, stop=d == NT - 1)
            last.then_inc(deg_src_row_summed, 1)
            for d in range(NT):
                if d == 1:
                    pe.wait_ge(deg_src_row_ready, 1)
                if d >= 2:
                    pe.wait_ge(adj_copied_act, d - 1)
                    pe.wait_ge(adj_copied_dve, d - 1)
                for k in range(NT):
                    last = nc.tensor.transpose(psum_bank[3 * (d % 2) + k // 4][:, P * (k % 4):P * (k % 4 + 1)],
                                               adj_dst_src[:, d, k * P:(k + 1) * P].bitcast(F32), ident[:])
                    if k in (3, 7, 9):
                        last.then_inc(adj_transposed, 1)

            def l0_transpose(n):
                if n == 0:
                    pe.wait_ge(x_loaded, 16)
                if n >= 2:
                    pe.wait_ge(rows_split, n - 1)
                for k in range(KT):
                    last = nc.tensor.transpose(psum_bank[6 + n % 2][:, P * k:P * (k + 1)], x_nodes[:, n, k * P:(k + 1) * P], ident[:])
                last.then_inc(node_rows_transposed, 1)

            for k in range(NT):
                last = nc.tensor.matmul(psum_bank[7][:, k:k + 1], deg_src_row[0:1, k * P:(k + 1) * P], ones[0:1, 0:1], start=True, stop=True)
            last.then_inc(deg_src_columns, 1)
            l0_transpose(0)
            pe.wait_ge(deg_src_plus1, 1)
            l0_transpose(1)
            pe.wait_ge(adj_copied_act, NT)
            pe.wait_ge(adj_copied_dve, NT)
            for n in range(NT):
                if 1 <= n < NT - 1:
                    l0_transpose(n + 1)
                b = n % 2
                if n == 0:
                    pe.wait_ge(weights_split, 1)
                pe.wait_ge(rows_split, n + 1)
                if n >= 2:
                    pe.wait_ge(l0_feat_ready, n - 1)
                for k in range(KT):
                    xh, xl = x_split[:, b, 0, k * P:(k + 1) * P], x_split[:, b, 1, k * P:(k + 1) * P]
                    nc.tensor.matmul(psum_bank[2 + b], xh, w0_hi[:, k, :], start=k == 0, stop=False)
                    nc.tensor.matmul(psum_bank[2 + b], xh, w0_lo[:, k, :], start=False, stop=False)
                    last = nc.tensor.matmul(psum_bank[2 + b], xl, w0_hi[:, k, :], start=False, stop=k == KT - 1)
                last.then_inc(first_linear_done, 1)

            pe.wait_ge(identity_r_ready, 1)
            for n in range(NT):
                b = 4 + n % 2
                if n >= 2:
                    pe.wait_ge(l0_resid_ready, NT + n - 1)
                for k in range(NT):
                    if n == 0:
                        pe.wait_ge(features_ready, k + 1)
                    for g in (g1_hi, g1_lo):
                        nc.tensor.matmul(psum_bank[b], adj_dst_src[:, k, n * P:(n + 1) * P], g[:, k, :], start=k == 0 and g is g1_hi,
                                         stop=False)
                nc.tensor.matmul(psum_bank[b], ident_r[:], g1_hi[:, n, :], start=False, stop=False)
                nc.tensor.matmul(psum_bank[b], ident_r[:], g1_lo[:, n, :], start=False, stop=True).then_inc(aggregated, 1)

            pe.wait_ge(gate_loaded, 32)
            for n in range(NT):
                pe.wait_ge(layer_output_ready, n + 1)
                if n >= 2:
                    pe.wait_ge(l1_xt_ready, n - 1)
                for k in range(KT):
                    last = nc.tensor.transpose(psum_bank[n % 2][:, P * k:P * (k + 1)], x_nodes[:, n, k * P:(k + 1) * P], ident[:])
                last.then_inc(node_rows_transposed, 1)
            for n in range(NT):
                pe.wait_ge(l1_xt_ready, n + 1)
                for k in range(KT):
                    last = nc.tensor.matmul(psum_bank[7][:, n * NE:(n + 1) * NE], x1_t[:, n, k * P:(k + 1) * P], gate_w_sb[:, k, :],
                                            start=k == 0, stop=k == KT - 1)
                last.then_inc(l1_logits_done, 1)

            def l1_agg_transpose(n):
                pe.wait_ge(aggregate_scaled, n + 1)
                if n >= 2:
                    pe.wait_ge(l1_at_ready, n - 1)
                for k in range(KT):
                    last = nc.tensor.transpose(psum_bank[4 + n % 2][:, P * k:P * (k + 1)], agg_nodes[:, n % 2, k * P:(k + 1) * P], ident[:])
                last.then_inc(l1_agg_transposed, 1)

            for n in range(NT):
                if n >= 2:
                    pe.wait_ge(aggregate_scaled, n - 1)
                for k in range(NT):
                    if n == 0:
                        pe.wait_ge(features_ready, F_L1 + k + 1)
                    for g in (g1_hi, g1_lo):
                        last = nc.tensor.matmul(psum_bank[2 + n % 2], adj_src_dst[:, k, n * P:(n + 1) * P], g[:, k, :],
                                                start=k == 0 and g is g1_hi, stop=k == NT - 1 and g is g1_lo)
                last.then_inc(aggregated, 1)
                if n >= 1:
                    l1_agg_transpose(n - 1)
            l1_agg_transpose(NT - 1)

            def split_product(out, xh, xl, w, start, stop):
                wh, wl = w
                for k in range(KT):
                    c = slice(k * P, (k + 1) * P)
                    nc.tensor.matmul(out, xh[:, c], wh[:, k, :], start=start and k == 0, stop=False)
                    nc.tensor.matmul(out, xh[:, c], wl[:, k, :], start=False, stop=False)
                    last = nc.tensor.matmul(out, xl[:, c], wh[:, k, :], start=False, stop=stop and k == KT - 1)
                return last

            def first_layer(m, new=None):
                need(pe, rows_split, m + 1, R_EX)
                if new is not None:
                    pe.wait_ge(expert_w_first_ready, 2 * new + 1)
                split_product(psum_bank[0], x_agg_split[:, 0, 0], x_agg_split[:, 0, 1], (w_first[:, 0, 0], w_first[:, 0, 1]), True, False)
                if new is not None:
                    pe.wait_ge(expert_w_first_ready, 2 * new + 2)
                split_product(psum_bank[0], x_agg_split[:, 1, 0], x_agg_split[:, 1, 1], (w_first[:, 1, 0], w_first[:, 1, 1]), False, True).then_inc(first_linear_done, 1)

            def transpose_h(m):
                need(pe, ex_h_ready, m + 1)
                for k in range(KT):
                    last = nc.tensor.transpose(psum_bank[2][:, P * k:P * (k + 1)], h_nodes[:, k * P:(k + 1) * P], ident[:])
                last.then_inc(hidden_rows_transposed, 1)

            def second_layer(m, new=None):
                need(pe, hidden_split, m + 1)
                need(pe, ex_r_ready, m)
                if m is not None:
                    need(pe, expert_g_copied, m)
                if new is not None:
                    pe.wait_ge(expert_w_second_ready, 2 * new + 1)
                split_product(psum_bank[4], h_transposed[:, 0], h_transposed[:, 1], (w_second[:, 0, 0], w_second[:, 0, 1]), True, True)
                if new is not None:
                    pe.wait_ge(expert_w_second_ready, 2 * new + 2)
                split_product(psum_bank[5], h_transposed[:, 0], h_transposed[:, 1], (w_second[:, 1, 0], w_second[:, 1, 1]), True, True).then_inc(second_linear_done, 1)

            def expert(e, final):
                m = e * NT + 1
                transpose_h(m - 1)
                first_layer(m)
                second_layer(m - 1, e)
                with pe.Fori(2, NT) as n:
                    transpose_h(e * NT + n - 1)
                    first_layer(e * NT + n)
                    second_layer(e * NT + n - 1)
                if not final:
                    m = e * NT + NT
                    transpose_h(m - 1)
                    first_layer(m, e + 1)
                    second_layer(m - 1)

            first_layer(0, 0)
            with pe.Fori(0, NE - 1) as e:
                expert(e, False)
            expert(NE - 1, True)
            transpose_h(NE * NT - 1)
            second_layer(NE * NT - 1)

            for e in range(NE):
                G = (g2, g1_again)[e % 2]
                for n in range(NT):
                    m = e * NT + n
                    need(pe, gather_scaled, m - 1)
                    for k in range(NT):
                        if n == 0:
                            pe.wait_ge(features_ready, F_GA + e * NT + k + 1)
                        for half in (0, 1):
                            last = nc.tensor.matmul(psum_bank[m % 2], adj_src_dst[:, k, n * P:(n + 1) * P], G[:, half, k],
                                                    start=k == 0 and half == 0, stop=k == NT - 1 and half == 1)
                    last.then_inc(aggregated, 1)

            def l2_transpose(n):
                pe.wait_ge(aggregate_scaled, SC_L2 + n + 1)
                if n >= 1:
                    pe.wait_ge(rows_split, R_L2 + n)
                for k in range(KT):
                    nc.tensor.transpose(psum_bank[0][:, P * k:P * (k + 1)], x_nodes[:, n, k * P:(k + 1) * P], ident[:])
                for k in range(KT):
                    last = nc.tensor.transpose(psum_bank[1][:, P * k:P * (k + 1)], agg2_nodes[:, n % 2, k * P:(k + 1) * P], ident[:])
                last.then_inc(node_rows_transposed, 1)

            def l2_linear(n):
                pe.wait_ge(rows_split, R_L2 + n + 1)
                if n >= 2:
                    pe.wait_ge(linear_biased, n - 1)
                split_product(psum_bank[4 + n % 2], x_agg_split2[:, 0, 0], x_agg_split2[:, 0, 1], (w_first[:, 0, 0], w_first[:, 0, 1]), True, False)
                split_product(psum_bank[4 + n % 2], x_agg_split2[:, 1, 0], x_agg_split2[:, 1, 1], (w_first[:, 1, 0], w_first[:, 1, 1]), False, True).then_inc(first_linear_done, 1)

            pe.wait_ge(gather_scaled, NE * NT)
            pe.wait_ge(weights_split, W_L2 + 1)
            for n in range(NT):
                if n >= 1:
                    l2_transpose(n - 1)
                if n >= 2:
                    pe.wait_ge(aggregate_scaled, SC_L2 + n - 1)
                for k in range(NT):
                    if n == 0:
                        pe.wait_ge(features_ready, F_L2 + k + 1)
                    for half in (0, 1):
                        last = nc.tensor.matmul(psum_bank[2 + n % 2], adj_src_dst[:, k, n * P:(n + 1) * P], g2[:, half, k],
                                                start=k == 0 and half == 0, stop=k == NT - 1 and half == 1)
                last.then_inc(aggregated, 1)
                if n >= 1:
                    l2_linear(n - 1)
            l2_transpose(NT - 1)
            l2_linear(NT - 1)

            def scatter(j):
                for r in range(2 * EPW):
                    t = 2 * EPW * j + r
                    if not (isinstance(j, int) and t + AHEAD >= ET):
                        embed_at(j, r + AHEAD)
                    if whole(r):
                        need(pe, message_hi, t + 1)
                    else:
                        need(pe, message_ready, splits(j, r))
                    for i, w in enumerate(shifts(j, r)):
                        first, final = opens(j, r, w), closes(j, r, w)
                        if first:
                            need(pe, edge_window_copied, 2 * j + w - 1)
                        if whole(r):
                            last = nc.tensor.matmul(psum_bank[4 + w % 2], onehot_dst_r[:, r % 4, i].bitcast(F32),
                                                    message_whole[:], start=first, stop=final)
                        else:
                            nc.tensor.matmul(psum_bank[4 + w % 2], onehot_dst_r[:, r % 4, i], messages[:, r % 2, 0], start=first, stop=False)
                            last = nc.tensor.matmul(psum_bank[4 + w % 2], onehot_dst_r[:, r % 4, i], messages[:, r % 2, 1], start=False,
                                                    stop=final)
                        if final:
                            last.then_inc(edge_window_done, 1)
                    if not final:
                        last.then_inc(message_summed, 1)

            def embed_at(j, r):
                t = 2 * EPW * j + r
                if r % 4 == 0:
                    need(pe, edge_attr_ready, 8 * j + r // 4 + 1)
                need(pe, edge_z_ready, t - 3)
                b, c = (r // 4) % 2, slice((r % 4) * P, (r % 4 + 1) * P)
                nc.tensor.matmul(psum_bank[r % 4], edge_attr_split[:, b, 0, c], w_edge_split[:, 0], start=True, stop=False)
                nc.tensor.matmul(psum_bank[r % 4], edge_attr_split[:, b, 0, c], w_edge_split[:, 1], start=False, stop=False)
                nc.tensor.matmul(psum_bank[r % 4], edge_attr_split[:, b, 1, c], w_edge_split[:, 0], start=False, stop=True).then_inc(edge_embedded, 1)

            pe.wait_ge(weights_split, W_EDGE + 1)
            pe.wait_ge(linear_biased, NT)
            for r in range(AHEAD):
                embed_at(0, r)
            window_loop(pe, scatter)

            pe.wait_ge(edge_window_copied, NT)
            general = pe.value_load(flag[0:1, 0:1], min_val=0, max_val=ET * P)
            with pe.If(general > ET * P - N_EDGES):
                with pe.Fori(0, NT) as d:
                    pe.wait_ge(edge_window_copied, GEN_W + d)
                    nc.tensor.matmul(psum_bank[4], zeros[:], iota_nodes[:, 0:512], start=True, stop=False)
                    with pe.Fori(0, ET) as t:
                        pe.wait_ge(edge_attr_ready, GEN_G + d * ET + t + 1)
                        nc.tensor.matmul(psum_bank[0], edge_attr_split[:, 0, 0, 0:P], w_edge_split[:, 0], start=True, stop=False)
                        nc.tensor.matmul(psum_bank[0], edge_attr_split[:, 0, 0, 0:P], w_edge_split[:, 1], start=False, stop=False)
                        nc.tensor.matmul(psum_bank[0], edge_attr_split[:, 0, 1, 0:P], w_edge_split[:, 0], start=False, stop=True).then_inc(edge_embedded, 1)
                        pe.wait_ge(message_ready, GEN_M + d * ET + t + 1)
                        nc.tensor.matmul(psum_bank[4], onehot_dst_r[:, 0, 0], messages[:, 0, 0], start=False, stop=False)
                        nc.tensor.matmul(psum_bank[4], onehot_dst_r[:, 0, 0], messages[:, 0, 1], start=False, stop=False).then_inc(message_summed, 1)
                    nc.tensor.matmul(psum_bank[4], zeros[:], iota_nodes[:, 0:512], start=False, stop=True).then_inc(edge_window_done, 1)
                pe.wait_ge(edge_window_copied, GEN_W + NT)
                pe.nop()
            with pe.Else():
                pe.nop()
            pe.nop()

            def matrix(q):
                return w3_upper[:, q * KT:(q + 1) * KT], w3_lower[:, q * KT:(q + 1) * KT]

            def up_product(first_matrix):
                split_product(psum_bank[3], split4[:, 0], split4[:, 1], matrix(first_matrix), True, True)
                return split_product(psum_bank[4], split4[:, 0], split4[:, 1], matrix(first_matrix + 1), True, True)

            def down_product(half, first_matrix):
                x = slice(half * D, (half + 1) * D)
                return split_product(psum_bank[5], split8[:, 0, x], split8[:, 1, x], matrix(first_matrix + half), half == 0, half == 1)

            def transpose_row(n, done):
                for k in range(KT):
                    last = nc.tensor.transpose(psum_bank[0][:, P * k:P * (k + 1)], edge_sums[:, n, k * P:(k + 1) * P], ident[:])
                last.then_inc(done, 1)

            def transpose_wide(done):
                for k in range(2 * KT):
                    last = nc.tensor.transpose(psum_bank[1 + k // KT][:, P * (k % KT):P * (k % KT + 1)],
                                               y1_or_m[:, k * P:(k + 1) * P], ident[:])
                last.then_inc(done, 1)

            pe.wait_ge(weights_split, W_MLP + 6 * KT)
            pe.wait_ge(h0_ready, 1)
            transpose_row(0, node_rows_transposed)
            for q in range(2 * NT + 2):
                if q < 2 * NT:
                    pe.wait_ge(rows_split, R_MLP1 + q + 1)
                    if 1 <= q <= NT:
                        pe.wait_ge(y1_biased, q)
                    if q > NT:
                        pe.wait_ge(y1_gelu, q)
                    up_product(0 if q < NT else 4).then_inc(first_linear_done, 1)
                if q + 1 < NT:
                    pe.wait_ge(h0_ready, q + 2)
                    transpose_row(q + 1, node_rows_transposed)
                elif q + 1 < 2 * NT:
                    pe.wait_ge(layer_output_ready, N_MLP1 + q + 2 - NT)
                    transpose_row(q + 1 - NT, node_rows_transposed)
                if q >= 2:
                    pe.wait_ge(hidden_split, HT_MLP1 + q - 1)
                    if q == NT + 2:
                        pe.wait_ge(w3_last_ready, 2 * KT)
                    if q >= 3:
                        pe.wait_ge(linear_biased, B_MLP1 + q - 2)
                    down_product(0, 2 if q < NT + 2 else 6)
                if 1 <= q <= 2 * NT:
                    pe.wait_ge(y1_gelu, q)
                    transpose_wide(hidden_rows_transposed)
                if q >= 2:
                    down_product(1, 2 if q < NT + 2 else 6).then_inc(second_linear_done, 1)


_INS = ["x", "src", "dst", "w0", "b0", "gate_w", "gate_b", "w1", "b1", "w2", "l2_bias", "l2_gamma", "l2_beta",
        "edge_attr", "w_edge", "b_edge", "eps", "w3", "v1", "v2"]


def kernel(**inputs):
    import numpy as _np
    import concourse.bacc as _bacc
    from concourse import mybir as _mybir
    from concourse.bass_utils import run_bass_kernel_spmd as _run

    def edges(a, fill):
        padded = _np.full(ET * P, fill, _np.int32)
        padded[:N_EDGES] = a
        return _np.ascontiguousarray(padded.reshape(ET, P).T)

    def matrix(w):
        return _np.ascontiguousarray(w.reshape(KT, P, D).transpose(1, 0, 2))

    wl, wr = _np.asarray(inputs["L1_gnn_Wl"]), _np.asarray(inputs["L1_gnn_Wr"])
    w1 = _np.stack([_np.stack([_np.stack([matrix(wr[e, 0]), matrix(wl[e, 0])], axis=1),
                               _np.stack([matrix(wl[e, 1]), matrix(wr[e, 1])], axis=1)]) for e in range(NE)])
    w3 = []
    for up, down in (("L3_gnn_W1", "L3_gnn_W2"), ("L3_gnn_M1", "L3_gnn_M2")):
        u, d = _np.asarray(inputs[up]), _np.asarray(inputs[down])
        w3 += [matrix(u[:, :D]), matrix(u[:, D:]), matrix(d[:D]), matrix(d[D:])]
    w3 = _np.stack(w3, axis=1)
    attr = _np.zeros((ET * P, P), _np.float32)
    attr[:N_EDGES] = inputs["edge_attr_128"]
    xp = _np.zeros((NP, D), _np.float32)
    xp[:N_NODES] = inputs["x"]
    data = {
        "x": _np.ascontiguousarray(xp.reshape(NT, P, D).transpose(1, 0, 2)),
        "src": edges(_np.asarray(inputs["src"]), 0), "dst": edges(_np.asarray(inputs["dst"]), NO_NODE),
        "w0": matrix(_np.asarray(inputs["L0_gnn_W"]).T), "b0": _np.asarray(inputs["L0_gnn_b"]),
        "gate_w": _np.asarray(inputs["L1_gnn_gate_W"]).reshape(KT, P, NE).transpose(1, 0, 2),
        "gate_b": _np.asarray(inputs["L1_gnn_gate_b"]),
        "w1": w1, "b1": _np.asarray(inputs["L1_gnn_bl"]),
        "w2": _np.stack([matrix(_np.asarray(inputs["L2_gnn_W_self"]).T),
                         matrix(_np.asarray(inputs["L2_gnn_W_neigh"]).T)], axis=1),
        "l2_bias": _np.asarray(inputs["L2_gnn_bias"]), "l2_gamma": _np.asarray(inputs["L2_gnn_gamma"]),
        "l2_beta": _np.asarray(inputs["L2_gnn_beta"]),
        "edge_attr": _np.ascontiguousarray(attr.reshape(ET // 4, 4 * P, P).transpose(0, 2, 1)),
        "w_edge": _np.asarray(inputs["L3_gnn_W_edge"]), "b_edge": _np.asarray(inputs["L3_gnn_b_edge"]),
        "eps": _np.asarray(inputs["L3_gnn_eps"]).reshape(1), "w3": w3.reshape(P, 8 * KT, D),
        "v1": _np.stack([_np.asarray(inputs["L3_gnn_" + n]) for n in ("b1", "g1", "be1")]),
        "v2": _np.stack([_np.asarray(inputs["L3_gnn_" + n]) for n in ("b2", "g2", "be2", "gA", "bA", "gB", "bB")]),
    }
    nc = _bacc.Bacc("TRN2", target_bir_lowering=False, num_devices=1)
    arrays, args = {}, []
    for name in _INS:
        a = _np.ascontiguousarray(data[name])
        arrays[f"in_{name}_dram"] = a
        args.append(nc.dram_tensor(f"in_{name}_dram", a.shape, _mybir.dt.from_np(a.dtype), kind="ExternalInput").ap())
    out = nc.dram_tensor("out_dram", (P, NT, D), _mybir.dt.float32, kind="ExternalOutput").ap()
    build(nc, *args, out)
    r = _run(nc, [arrays], core_ids=[0])
    y = r.results[0]["out_dram"]
    return _np.ascontiguousarray(y.transpose(1, 0, 2).reshape(NP, D)[:N_NODES])
```
